# Optimizing a Trainium2 kernel written in Bass

```python
import numpy as np
import jax
import jax.numpy as jnp

def _softmax(x, axis=-1):
    return jax.nn.softmax(x, axis=axis)

def _gelu(x):
    return jax.nn.gelu(x, approximate=True)

def _silu(x):
    return jax.nn.silu(x)

def _sigmoid(x):
    return jax.nn.sigmoid(x)

def _layernorm(x, axis=-1, eps=1e-05):
    m = jnp.mean(x, axis=axis, keepdims=True)
    v = jnp.var(x, axis=axis, keepdims=True)
    return (x - m) / jnp.sqrt(v + eps)

def _scatter_add(tgt, idx, src, axis=0):
    return tgt.at[idx].add(src)

def _segment_sum(src, seg, n):
    return jax.ops.segment_sum(src, seg, n)
kernel_name = 'mk_gnn_resnorm_d4_gnn_r32_f7b516'

def setup_inputs(seed: int=0):
    np.random.seed(seed)
    _w = jnp.asarray

    def _rec_inputs():
        import jax
        import jax.numpy as jnp
        _gk = jax.random.key(seed)
        x = 0.0003989 + 1 * jax.random.normal(jax.random.fold_in(_gk, 1), (50000, 128), jnp.float32)
        src = jax.random.randint(jax.random.fold_in(_gk, 2), (50000,), 0, 50000, jnp.int32)
        dst = jnp.minimum((50000 * jax.random.uniform(jax.random.fold_in(_gk, 3), (50000,)) ** 2.0).astype(jnp.int32), 49999)
        _o = jnp.argsort(dst, stable=True)
        src = src[_o]
        dst = dst[_o]
        edge_attr_3 = -0.000451519 + 1.00018 * jax.random.normal(jax.random.fold_in(_gk, 12), (50000, 3), jnp.float32)
        edge_attr_64 = -7.08334e-05 + 0.999895 * jax.random.normal(jax.random.fold_in(_gk, 13), (50000, 64), jnp.float32)
        edge_weight = jax.random.uniform(jax.random.fold_in(_gk, 15), (50000,), jnp.float32, 0.0, 0.999999)
        return (x, src, dst, edge_attr_3, edge_attr_64, edge_weight)
    x, src, dst, edge_attr_3, edge_attr_64, edge_weight = _rec_inputs()

    def _L0_gnn_setup():
        import jax, jax.numpy as jnp
        import numpy as np
        N_NODES = 50000
        N_EDGES = 18750
        D_IN = 128
        D_OUT = 128
        key = jax.random.key(seed)
        ks = jax.random.split(key, 6)
        gain = float(np.sqrt(2.0))
        lim = gain * np.sqrt(6.0 / (D_IN + D_IN))
        pool_w = jax.random.uniform(ks[0], (D_IN, D_IN), jnp.float32, -lim, lim)
        lim2 = gain * np.sqrt(6.0 / (D_IN + D_OUT))
        lin_w = jax.random.uniform(ks[1], (D_OUT, D_IN), jnp.float32, -lim2, lim2)
        return {'node_feats': jax.random.normal(ks[2], (N_NODES, D_IN), jnp.float32), 'src': jax.random.randint(ks[3], (N_EDGES,), 0, N_NODES, jnp.int32), 'dst': jax.random.randint(ks[4], (N_EDGES,), 0, N_NODES, jnp.int32), 'e_weight': jax.random.uniform(ks[5], (N_EDGES,), jnp.float32), 'pool_w': pool_w, 'pool_b': jnp.zeros((D_IN,), jnp.float32), 'lin_w': lin_w, 'lin_b': jnp.zeros((D_OUT,), jnp.float32), 'bias': jnp.zeros((D_OUT,), jnp.float32)}
    _L0_gnn_all = _L0_gnn_setup()
    _L0_gnn_in = {k: v for k, v in _L0_gnn_all.items() if k in ('pool_w', 'pool_b', 'lin_w', 'lin_b', 'bias')}
    del _L0_gnn_all

    def _L1_gnn_setup():
        import jax, jax.numpy as jnp
        import numpy as np
        N_NODES = 50000
        N_EDGES = 25000
        D = 128
        N_LAYERS = 4
        BN_EPS = 1e-05
        key = jax.random.key(seed)
        ks = jax.random.split(key, 6)
        x = jax.random.normal(ks[0], (N_NODES, D), dtype=jnp.float32)
        src = jax.random.randint(ks[1], (N_EDGES,), 0, N_NODES, dtype=jnp.int32)
        dst = jax.random.randint(ks[2], (N_EDGES,), 0, N_NODES, dtype=jnp.int32)
        Ws = jax.random.normal(ks[3], (N_LAYERS, D, D), dtype=jnp.float32) * 0.05
        bs = jnp.zeros((N_LAYERS, D), dtype=jnp.float32)
        gammas = jnp.ones((N_LAYERS, D), dtype=jnp.float32)
        betas = jnp.zeros((N_LAYERS, D), dtype=jnp.float32)
        lin1_w = jax.random.normal(ks[4], (D, D), dtype=jnp.float32) * 0.05
        lin1_b = jnp.zeros((D,), dtype=jnp.float32)
        return {'x': x, 'src': src, 'dst': dst, 'Ws': Ws, 'bs': bs, 'gammas': gammas, 'betas': betas, 'lin1_w': lin1_w, 'lin1_b': lin1_b}
    _L1_gnn_all = _L1_gnn_setup()
    _L1_gnn_in = {k: v for k, v in _L1_gnn_all.items() if k in ('Ws', 'bs', 'gammas', 'betas', 'lin1_w', 'lin1_b')}
    del _L1_gnn_all

    def _L2_gnn_setup():
        import jax, jax.numpy as jnp
        import numpy as np
        N = 50000
        E = 25000
        MUL = 32
        NB = 8
        R_MAX = 1.0
        AVG = 16.0
        SQ3 = 3.0 ** 0.5

        def _radial_embedding(r):
            x = jnp.clip(r / R_MAX, 0.0, 1.0)
            centers = jnp.arange(NB, dtype=jnp.float32) / (NB - 1)
            sigma = 1.0 / (NB - 1)
            emb = jnp.exp(-0.5 * ((x[:, None] - centers[None, :]) / sigma) ** 2)
            emb = emb * NB ** 0.5 * (r <= R_MAX).astype(jnp.float32)[:, None]
            return emb
        key = jax.random.key(seed)
        k = jax.random.split(key, 12)
        inp = {'node_feats': jax.random.normal(k[0], (N, 4 * MUL), dtype=jnp.float32), 'edge_vec': jax.random.normal(k[1], (E, 3), dtype=jnp.float32), 'edge_length': jax.random.uniform(k[2], (E,), dtype=jnp.float32), 'senders': jax.random.randint(k[3], (E,), 0, N, dtype=jnp.int32), 'receivers': jax.random.randint(k[4], (E,), 0, N, dtype=jnp.int32), 'num_nodes': N, 'W_up0': jax.random.normal(k[5], (MUL, MUL), dtype=jnp.float32), 'W_up1': jax.random.normal(k[6], (MUL, MUL), dtype=jnp.float32), 'mlp_w0': jax.random.normal(k[7], (NB, 64), dtype=jnp.float32) / NB ** 0.5, 'mlp_b0': jnp.zeros((64,), dtype=jnp.float32), 'mlp_w1': jax.random.normal(k[8], (64, 64), dtype=jnp.float32) / 8.0, 'mlp_b1': jnp.zeros((64,), dtype=jnp.float32), 'mlp_w2': jax.random.normal(k[9], (64, 4 * MUL), dtype=jnp.float32) / 8.0, 'mlp_b2': jnp.zeros((4 * MUL,), dtype=jnp.float32), 'W_out0': jax.random.normal(k[10], (2 * MUL, MUL), dtype=jnp.float32), 'W_out1': jax.random.normal(k[11], (2 * MUL, MUL), dtype=jnp.float32)}
        return inp
    _L2_gnn_all = _L2_gnn_setup()
    _L2_gnn_in = {k: v for k, v in _L2_gnn_all.items() if k in ('W_up0', 'W_up1', 'mlp_w0', 'mlp_b0', 'mlp_w1', 'mlp_b1', 'mlp_w2', 'mlp_b2', 'W_out0', 'W_out1')}
    del _L2_gnn_all

    def _L3_gnn_setup():
        import jax, jax.numpy as jnp
        import numpy as np
        LOG2 = float(np.log(2.0))

        def ssp(x):
            return jax.nn.softplus(x) - LOG2
        key = jax.random.key(seed)
        k1, k2, k3, k4, k5 = jax.random.split(key, 5)
        N, E, D, F = (3125, 18750, 128, 64)
        nodes = jax.random.normal(k1, (N, D), dtype=jnp.float32)
        edges = jax.random.normal(k2, (E, F), dtype=jnp.float32)
        edges_i = jax.random.randint(k3, (E, 2), 0, N, dtype=jnp.int64)
        W1 = jax.random.normal(k4, (F, D), dtype=jnp.float32) * (1.0 / np.sqrt(F))
        b1 = jnp.zeros((D,), dtype=jnp.float32)
        W2 = jax.random.normal(k5, (D, D), dtype=jnp.float32) * (1.0 / np.sqrt(D))
        b2 = jnp.zeros((D,), dtype=jnp.float32)
        return {'nodes': nodes, 'edges': edges, 'edges_i': edges_i, 'W1': W1, 'b1': b1, 'W2': W2, 'b2': b2}
    _L3_gnn_all = _L3_gnn_setup()
    _L3_gnn_in = {k: v for k, v in _L3_gnn_all.items() if k in ('W1', 'b1', 'W2', 'b2')}
    del _L3_gnn_all
    return {'x': x, 'src': src, 'dst': dst, 'edge_attr_3': edge_attr_3, 'edge_attr_64': edge_attr_64, 'edge_weight': edge_weight, 'L0_gnn_pool_w': _L0_gnn_in['pool_w'], 'L0_gnn_pool_b': _L0_gnn_in['pool_b'], 'L0_gnn_lin_w': _L0_gnn_in['lin_w'], 'L0_gnn_lin_b': _L0_gnn_in['lin_b'], 'L0_gnn_bias': _L0_gnn_in['bias'], 'L1_gnn_Ws': _L1_gnn_in['Ws'], 'L1_gnn_bs': _L1_gnn_in['bs'], 'L1_gnn_gammas': _L1_gnn_in['gammas'], 'L1_gnn_betas': _L1_gnn_in['betas'], 'L1_gnn_lin1_w': _L1_gnn_in['lin1_w'], 'L1_gnn_lin1_b': _L1_gnn_in['lin1_b'], 'L2_gnn_W_up0': _L2_gnn_in['W_up0'], 'L2_gnn_W_up1': _L2_gnn_in['W_up1'], 'L2_gnn_mlp_w0': _L2_gnn_in['mlp_w0'], 'L2_gnn_mlp_b0': _L2_gnn_in['mlp_b0'], 'L2_gnn_mlp_w1': _L2_gnn_in['mlp_w1'], 'L2_gnn_mlp_b1': _L2_gnn_in['mlp_b1'], 'L2_gnn_mlp_w2': _L2_gnn_in['mlp_w2'], 'L2_gnn_mlp_b2': _L2_gnn_in['mlp_b2'], 'L2_gnn_W_out0': _L2_gnn_in['W_out0'], 'L2_gnn_W_out1': _L2_gnn_in['W_out1'], 'L3_gnn_W1': _L3_gnn_in['W1'], 'L3_gnn_b1': _L3_gnn_in['b1'], 'L3_gnn_W2': _L3_gnn_in['W2'], 'L3_gnn_b2': _L3_gnn_in['b2']}

def reference(x, src, dst, edge_attr_3, edge_attr_64, edge_weight, L0_gnn_pool_w, L0_gnn_pool_b, L0_gnn_lin_w, L0_gnn_lin_b, L0_gnn_bias, L1_gnn_Ws, L1_gnn_bs, L1_gnn_gammas, L1_gnn_betas, L1_gnn_lin1_w, L1_gnn_lin1_b, L2_gnn_W_up0, L2_gnn_W_up1, L2_gnn_mlp_w0, L2_gnn_mlp_b0, L2_gnn_mlp_w1, L2_gnn_mlp_b1, L2_gnn_mlp_w2, L2_gnn_mlp_b2, L2_gnn_W_out0, L2_gnn_W_out1, L3_gnn_W1, L3_gnn_b1, L3_gnn_W2, L3_gnn_b2):
    import jax
    import jax.numpy as jnp

    def _L0_gnn_ref(node_feats, src, dst, e_weight, pool_w, pool_b, lin_w, lin_b, bias):
        import jax, jax.numpy as jnp
        import numpy as np
        N_NODES = 50000
        N_EDGES = 18750
        D_IN = 128
        D_OUT = 128
        h_src = jax.nn.relu(node_feats @ pool_w.T + pool_b)
        m = h_src[src] * e_weight[:, None]
        h_new = jax.ops.segment_max(m, dst, num_segments=N_NODES)
        h_new = jnp.where(jnp.isfinite(h_new), h_new, 0.0)
        return h_new @ lin_w.T + lin_b + bias

    def _L1_gnn_ref(x, src, dst, Ws, bs, gammas, betas, lin1_w, lin1_b):
        import jax, jax.numpy as jnp
        import numpy as np
        N_NODES = 50000
        N_EDGES = 25000
        D = 128
        N_LAYERS = 4
        BN_EPS = 1e-05
        n = x.shape[0]
        ones = jnp.ones(src.shape[0], dtype=x.dtype)
        deg_out = jax.ops.segment_sum(ones, src, num_segments=n)
        deg_in = jax.ops.segment_sum(ones, dst, num_segments=n)
        norm_src = jax.lax.rsqrt(jnp.maximum(deg_out, 1.0))[:, None]
        norm_dst = jax.lax.rsqrt(jnp.maximum(deg_in, 1.0))[:, None]
        h = x
        xs = []
        for i in range(N_LAYERS):
            m = h * norm_src
            agg = jax.ops.segment_sum(m[src], dst, num_segments=n)
            h = agg * norm_dst
            h = jax.nn.relu(h @ Ws[i] + bs[i])
            mu = jnp.mean(h, axis=0)
            var = jnp.var(h, axis=0)
            h = (h - mu) * jax.lax.rsqrt(var + BN_EPS) * gammas[i] + betas[i]
            h = jax.nn.relu(h)
            xs.append(h)
        x_jk = jnp.max(jnp.stack(xs, axis=0), axis=0)
        out = jax.nn.relu(x_jk @ lin1_w + lin1_b)
        return out

    def _L2_gnn_ref(node_feats, edge_vec, edge_length, senders, receivers, num_nodes, W_up0, W_up1, mlp_w0, mlp_b0, mlp_w1, mlp_b1, mlp_w2, mlp_b2, W_out0, W_out1):
        import jax, jax.numpy as jnp
        import numpy as np
        N = 50000
        E = 25000
        MUL = 32
        NB = 8
        R_MAX = 1.0
        AVG = 16.0
        SQ3 = 3.0 ** 0.5

        def _radial_embedding(r):
            x = jnp.clip(r / R_MAX, 0.0, 1.0)
            centers = jnp.arange(NB, dtype=jnp.float32) / (NB - 1)
            sigma = 1.0 / (NB - 1)
            emb = jnp.exp(-0.5 * ((x[:, None] - centers[None, :]) / sigma) ** 2)
            emb = emb * NB ** 0.5 * (r <= R_MAX).astype(jnp.float32)[:, None]
            return emb
        f32 = jnp.float32
        rhat = edge_vec / (jnp.linalg.norm(edge_vec, axis=-1, keepdims=True) + 1e-12)
        Y1 = SQ3 * rhat
        emb = _radial_embedding(edge_length)
        h = jax.nn.silu(emb @ mlp_w0 + mlp_b0)
        h = jax.nn.silu(h @ mlp_w1 + mlp_b1)
        w = (h @ mlp_w2 + mlp_b2).reshape(-1, 4, MUL)
        s = node_feats[:, :MUL]
        v = node_feats[:, MUL:].reshape(-1, MUL, 3)
        xs = s @ W_up0 / f32(MUL) ** 0.5
        xv = jnp.einsum('nmc,mk->nkc', v, W_up1) / f32(MUL) ** 0.5
        ss = xs[senders]
        vv = xv[senders]
        m0 = w[:, 0] * ss
        m1 = w[:, 1][:, :, None] * ss[:, :, None] * Y1[:, None, :]
        m2 = w[:, 2][:, :, None] * vv
        m3 = w[:, 3] * (jnp.einsum('emc,ec->em', vv, Y1) / SQ3)
        mid_s = jnp.concatenate([m0, m3], axis=1)
        mid_v = jnp.concatenate([m1, m2], axis=1)
        msg_s = jax.ops.segment_sum(mid_s, receivers, num_segments=num_nodes)
        msg_v = jax.ops.segment_sum(mid_v, receivers, num_segments=num_nodes)
        out_s = msg_s @ W_out0 / f32(2 * MUL) ** 0.5
        out_v = jnp.einsum('nmc,mk->nkc', msg_v, W_out1) / f32(2 * MUL) ** 0.5
        out = jnp.concatenate([out_s, out_v.reshape(-1, 3 * MUL)], axis=1)
        return out / max(AVG, 1e-08)

    def _L3_gnn_ref(nodes, edges, edges_i, W1, b1, W2, b2):
        import jax, jax.numpy as jnp
        import numpy as np
        LOG2 = float(np.log(2.0))

        def ssp(x):
            return jax.nn.softplus(x) - LOG2
        starts = edges_i[:, 0]
        ends = edges_i[:, 1]
        filt = ssp(edges @ W1 + b1)
        filt = ssp(filt @ W2 + b2)
        msgs = nodes[ends] * filt
        return nodes.at[starts].add(msgs)
    edge_index_t = jnp.stack([src, dst], axis=1)
    x = _layernorm(x + _L0_gnn_ref(x, src, dst, edge_weight, L0_gnn_pool_w, L0_gnn_pool_b, L0_gnn_lin_w, L0_gnn_lin_b, L0_gnn_bias), axis=-1)
    x = _layernorm(x + _L1_gnn_ref(x, src, dst, L1_gnn_Ws, L1_gnn_bs, L1_gnn_gammas, L1_gnn_betas, L1_gnn_lin1_w, L1_gnn_lin1_b), axis=-1)
    x = _layernorm(x + _L2_gnn_ref(x, edge_attr_3, edge_weight, src, dst, 50000, L2_gnn_W_up0, L2_gnn_W_up1, L2_gnn_mlp_w0, L2_gnn_mlp_b0, L2_gnn_mlp_w1, L2_gnn_mlp_b1, L2_gnn_mlp_w2, L2_gnn_mlp_b2, L2_gnn_W_out0, L2_gnn_W_out1), axis=-1)
    x = _layernorm(x + _L3_gnn_ref(x, edge_attr_64, edge_index_t, L3_gnn_W1, L3_gnn_b1, L3_gnn_W2, L3_gnn_b2), axis=-1)
    return x

_drawn_inputs = setup_inputs


def setup_inputs(seed=0):
    import zlib

    import numpy as np

    out = dict(_drawn_inputs(seed))
    spreads = {'L0_gnn_pool_b': (0.0, 0.1),
     'L0_gnn_lin_b': (0.0, 0.1),
     'L0_gnn_bias': (0.0, 0.1),
     'L1_gnn_bs': (0.0, 0.1),
     'L1_gnn_gammas': (1.0, 0.2),
     'L1_gnn_betas': (0.0, 0.1),
     'L1_gnn_lin1_b': (0.0, 0.1),
     'L2_gnn_mlp_b0': (0.0, 0.8),
     'L2_gnn_mlp_b1': (0.0, 0.8),
     'L2_gnn_mlp_b2': (0.0, 0.8),
     'L3_gnn_b1': (0.0, 0.573),
     'L3_gnn_b2': (0.0, 0.302)}
    factors = {'edge_attr_3': 2.876, 'L2_gnn_W_up1': 2.729, 'L2_gnn_W_out0': 3.686}
    for name, (base, spread) in spreads.items():
        noise = np.random.default_rng([zlib.crc32(name.encode()), seed]).standard_normal(out[name].shape)
        drawn = base * np.exp(spread * noise) if base else spread * noise
        out[name] = jnp.asarray(drawn.astype(out[name].dtype))
    for name, factor in factors.items():
        out[name] = (out[name] * factor).astype(out[name].dtype)
    return out
```

```python
from contextlib import ExitStack

import concourse.bass as bass
from concourse import mybir

P = 128
D = 128
N = 50000
TILES = 392
NP = TILES * P
TPC = 4
CW = TPC * P
C = TILES // TPC
ROWS = NP + 2 * P
EXT = D + 2
LANES = 4
HUGE = 3.0e38
EPS = 1e-5
LOG2 = 0.6931471805599453
L1 = 4

F32 = mybir.dt.float32
BF16 = mybir.dt.bfloat16
I32 = mybir.dt.int32
U8 = mybir.dt.uint8
ALU = mybir.AluOpType
ACT = mybir.ActivationFunctionType
AX = mybir.AxisListType.X


class Signal:

    def __init__(self, ctx, nc, name):
        self.sem = ctx.enter_context(nc.semaphore(name))
        self.base = 0

    def at(self, count):
        return count + self.base


def paced(eng, step):
    for k in range(2):
        step(k, k, 0)
    with eng.Fori(1, C // 2) as i:
        step(2 * i, 0, i)
        step(2 * i + 1, 1, i)


def skewed(eng, early, late):
    early(0, 0, 0)
    for k in range(3):
        early(k + 1, (k + 1) % 2, (k + 1) // 2)
        late(k, k % 2, k // 2)
    with eng.Fori(2, C // 2) as i:
        early(2 * i, 0, i)
        late(2 * i - 1, 1, i - 1)
        early(2 * i + 1, 1, i)
        late(2 * i, 0, i)
    late(C - 1, 1, C // 2 - 1)


def early_chunk(k):
    return isinstance(k, int) and k < 2


def rows_of(table, k, width=D):
    return table[bass.ds(k * CW, CW), 0:width].rearrange("(t p) d -> p t d", p=P)


def build(nc, a, out):
    with ExitStack() as ctx:
        def sb(name, shape, dt=F32):
            return ctx.enter_context(nc.sbuf_tensor(name, shape, dt))

        def dram(name, shape, dt=F32):
            return nc.dram_tensor(name, shape, dt).ap()

        def signal(name):
            return Signal(ctx, nc, name)

        t_agg = dram("t_agg", [ROWS, D])
        t_h = [dram(f"t_h{i}", [ROWS, D]) for i in range(L1)]
        t_x1e = dram("t_x1e", [ROWS, EXT])
        t_x2 = dram("t_x2", [ROWS, D])
        t_x3 = dram("t_x3", [ROWS, D])
        t_acc = [dram(f"t_acc{i}", [ROWS, D]) for i in range(LANES)]
        r_ns = dram("r_ns", [TILES, P])
        r_sq = dram("r_sq", [1, NP])
        r_y = dram("r_y", [4, NP])
        r_emb = dram("r_emb", [8, NP])

        mask = sb("mask", [P, NP], U8)
        src_i = sb("src_i", [P, TILES], I32)
        dst_i = sb("dst_i", [P, TILES], I32)
        nxt_i = sb("nxt_i", [P, TILES], I32)
        pos_i = sb("pos_i", [P, TILES], I32)
        endp_i = sb("endp_i", [P, TILES], I32)
        endp_f = sb("endp_f", [P, TILES])
        nsrc = sb("nsrc", [P, TILES])
        ndst = sb("ndst", [P, TILES])
        ends = sb("ends", [P, TILES])
        ident = sb("ident", [P, P])
        below = sb("below", [P, P])
        above = sb("above", [P, P])
        ones = sb("ones", [P, P])
        epsc = sb("epsc", [P, 1])
        lane = sb("lane", [P, 1])
        half = sb("half", [P, 1])
        zer = sb("zer", [P, CW])
        one = sb("one", [1, CW])
        w = {}
        for name, shape in (("pool_wT", [D, D]), ("lin_wT", [D, D]), ("lin1_w", [D, D]), ("w_ss", [D, D]),
                            ("w_vv", [D, D]), ("w_outA", [D, D]), ("w_outB", [D, D]), ("w_dot", [D, D]),
                            ("mlp_w0", [8, 64]), ("mlp_w1", [64, 64]), ("mlp_w2A", [64, D]),
                            ("mlp_w2B", [64, D]), ("W1", [64, D]), ("W2", [D, D]),
                            ("pool_b", [D, 1]), ("bsT", [D, L1]), ("gamT", [D, L1]), ("betT", [D, L1]),
                            ("mlp_b0", [64, 1]), ("mlp_b1", [64, 1]), ("mlp_b2A", [D, 1]), ("mlp_b2B", [D, 1]),
                            ("b1", [D, 1]), ("centre", [P, 1])):
            w[name] = sb("w_" + name, shape)
        gcn_w = sb("gcn_w", [D, L1, D])
        rows = sb("rows", [1, L1 + 2, D])
        bcast = sb("bcast", [P, 2 + L1, D])
        czero = sb("czero", [P, L1, D])
        aff = sb("aff", [P, L1, 2])
        gat = sb("gat", [P, 2, TPC, EXT])
        idx = sb("idx", [P, 2, TPC], I32)
        xin = sb("xin", [P, 2, CW])
        brd = sb("brd", [P, 2, CW])
        sca = sb("sca", [P, 2, CW])
        tmp = sb("tmp", [P, 2, CW])
        res = sb("res", [P, 2, TPC, EXT])
        dev = sb("dev", [P, 2, TPC, 2, D])
        sml = sb("sml", [P, 2, 64])
        scn = sb("scn", [P, 2, CW])
        row1 = sb("row1", [1, 2, CW])
        nst = sb("nst", [TPC, 2, P])
        embs = sb("embs", [8, 2, CW])
        att = sb("att", [64, 2, CW])
        sidx = sb("sidx", [P, 2, TPC], I32)
        lrg = sb("lrg", [P, 5 * 2048])

        ps = [ctx.enter_context(nc.psum_tensor(f"ps{i}", [P, CW], F32)) for i in range(8)]

        loaded = signal("loaded")
        got = [signal(f"got{i}") for i in range(2)]
        idx_ready = signal("idx_ready")
        ld = [signal(f"ld{i}") for i in range(2)]
        stored = [signal(f"stored{i}") for i in range(2)]
        pool_link = signal("pool_link")
        dve_link = signal("dve_link")
        act_link = signal("act_link")
        pe_t = signal("pe_t")
        pe_o = signal("pe_o")
        pe_s = signal("pe_s")
        act_x = signal("act_x")
        act_r = signal("act_r")
        dve_s = signal("dve_s")
        dve_d = signal("dve_d")
        act_q = signal("act_q")
        x_a = signal("x_a")
        x_b = signal("x_b")
        x_c = signal("x_c")
        x_d = signal("x_d")
        x_e = signal("x_e")
        x_f = signal("x_f")
        zeroed = signal("zeroed")
        act_e = signal("act_e")
        x_g = signal("x_g")
        x_h = signal("x_h")
        x_i = signal("x_i")
        lanes = [signal(f"lane{i}") for i in range(LANES)]
        turn = {e: ctx.enter_context(nc.semaphore(f"turn_{e}")) for e in ("pool", "dve", "act", "pe", "sp")}

        def chunkwise(*signals, per=1):
            for s in signals:
                s.base += per * C

        def link(eng, sig, ins):
            ins.then_inc(sig.sem, 1)
            sig.base += 1
            eng.wait_ge(sig.sem, sig.base)


        def hold(eng, name):
            eng.sem_inc(turn[name], 1)

        def before(k, slot, n):
            return k - 1, 1 - slot, (n if slot == 1 else n - 1)

        def first(k):
            return isinstance(k, int) and k == 0

        def pool_gather(pool, k, slot, n, table, index, width, freed, per=1):
            if not early_chunk(k):
                pool.wait_ge(freed.sem, freed.at(per * (k - 1)))
                hold(pool, "pool")
            pool.tensor_copy(idx[:, slot, :], index[:, bass.ds(k * TPC, TPC)]).then_inc(idx_ready.sem, 1)
            pool.wait_ge(idx_ready.sem, idx_ready.at(k + 1))
            hold(pool, "pool")
            for t in range(TPC):
                pool.indirect_dma_start(gat[:, slot, t, 0:width], None, table[0:NP + (index is src_i), :],
                                        bass.IndirectOffsetOnAxis(ap=idx[:, slot, t:t + 1], axis=0))\
                    .then_inc(got[slot].sem, 16)

        def gathered():
            idx_ready.base += C
            for s in range(2):
                got[s].base += 16 * TPC * C // 2

        def wait_got(eng, slot, n):
            eng.wait_ge(got[slot].sem, got[slot].at(16 * TPC * n + 16 * TPC))

        def wait_loads(eng, slot, n, each):
            eng.wait_ge(ld[slot].sem, ld[slot].at(16 * each * n + 16 * each))

        def tiles(ap):
            return ap.rearrange("p (t d) -> p t d", t=TPC)

        with nc.Block() as block:
            @block.gpsimd
            def _(pool):
                for m, v in ((ones, 1.0), (ident, 0.0), (below, 0.0), (above, 0.0), (epsc, EPS), (zer, 0.0), (one, 1.0), (half, 0.5)):
                    pool.memset(m[:], v).then_inc(pool_link.sem, 1)
                pool.iota(idx[:, 0, 0:1], [[0, 1]], base=NP + 1, channel_multiplier=1).then_inc(pool_link.sem, 1)
                pool.wait_ge(pool_link.sem, 9)
                for m, op, step, mult in ((ident, ALU.not_equal, -1, 1), (below, ALU.is_ge, 1, -1),
                                          (above, ALU.is_ge, -1, 1)):
                    pool.affine_select(out=m[:], in_=m[:], compare_op=op, fill=1.0, base=0,
                                       pattern=[[step, P]], channel_multiplier=mult).then_inc(pool_link.sem, 1)
                pool.tensor_copy(lane[:], idx[:, 0, 0:1]).then_inc(pool_link.sem, 1)
                pool.wait_ge(pool_link.sem, 13)

            @block.sync
            def _(sp):
                n = 0
                for name, t in w.items():
                    sp.dma_start(t[:], a[name]).then_inc(loaded.sem, 16)
                    n += 1
                for t, s in ((gcn_w[:], a["gcn_w"].rearrange("l i o -> i l o")),
                             (rows[:], a["rows"].rearrange("(a r) d -> a r d", a=1)),
                             (bcast[:], a["bias_rows"].partition_broadcast(P)),
                             (src_i[:], a["src"]), (dst_i[:], a["dst"]), (nxt_i[:], a["dst_next"])):
                    sp.dma_start(t, s).then_inc(loaded.sem, 16)
                    n += 1
                sp.wait_ge(loaded.sem, 16 * n)
                sp.wait_ge(pool_link.sem, 8)
                for table, width in ((t_x1e, EXT), (t_x2, D)):
                    sp.dma_start(table[NP:NP + 1, :], zer[0:1, 0:width]).then_inc(loaded.sem, 16)
                    n += 1
                sp.wait_ge(loaded.sem, 16 * n)
        pool_link.base = 13
        loaded.base = 16 * (len(w) + 8)

        seg = [lrg[:, s * 1024:s * 1024 + CW + 1].bitcast(I32) for s in range(2)]
        cnt = row1
        with nc.Block() as block:
            @block.sync
            def _(sp):
                def load(k, slot, n):
                    if not early_chunk(k):
                        sp.wait_ge(x_a.sem, x_a.at(k - 1))
                        hold(sp, "sp")
                    sp.dma_start(seg[slot], a["dst_row"][bass.ds(k * CW, CW + 1)]
                                 .partition_broadcast(P)).then_inc(ld[slot].sem, 16)

                def store(k, slot, n):
                    sp.wait_ge(act_x.sem, act_x.at(k + 1))
                    hold(sp, "sp")
                    sp.dma_start(r_sq[0:1, bass.ds(k * CW, CW)], tmp[0:1, slot, :]).then_inc(stored[slot].sem, 16)
                skewed(sp, load, store)
                for s in range(2):
                    sp.wait_ge(stored[s].sem, stored[s].at(8 * C))

            @block.vector
            def _(dve):
                def step(k, slot, n):
                    wait_loads(dve, slot, n, 1)
                    hold(dve, "dve")
                    dve.tensor_tensor(mask[:, bass.ds(k * CW, CW)], seg[slot][:, 1:CW + 1], seg[slot][:, 0:CW],
                                      ALU.is_equal).then_inc(x_a.sem, 1)
                    dve.wait_ge(x_a.sem, x_a.at(k + 1))
                    if not early_chunk(k):
                        dve.wait_ge(act_x.sem, act_x.at(k - 1))
                        dve.wait_ge(pe_t.sem, pe_t.at(k - 1))
                    if not first(k):
                        dve.wait_ge(x_b.sem, x_b.at(k))
                    hold(dve, "dve")
                    dve.tensor_tensor_scan(cnt[0:1, slot, :], mask[0:1, bass.ds(k * CW, CW)], one[0:1, :],
                                           0.0 if first(k) else cnt[0:1, 1 - slot, CW - 1:CW],
                                           ALU.mult, ALU.add).then_inc(x_b.sem, 1)
                    dve.wait_ge(pe_t.sem, pe_t.at(k + 1))
                    hold(dve, "dve")
                    dve.tensor_copy(ndst[:, bass.ds(k * TPC, TPC)], ps[0][:, slot * 8:slot * 8 + TPC])\
                       .then_inc(x_c.sem, 1)
                paced(dve, step)
                dve.wait_ge(x_c.sem, x_c.at(C))
                dve.tensor_tensor(ends[:], dst_i[:], nxt_i[:], ALU.not_equal).then_inc(dve_link.sem, 1)
                dve.tensor_scalar(endp_f[:], dst_i[:], float(N), None, ALU.is_lt).then_inc(dve_link.sem, 1)
                dve.wait_ge(dve_link.sem, 2)
                dve.tensor_tensor(ends[:], ends[:], endp_f[:], ALU.mult).then_inc(dve_link.sem, 1)
                dve.wait_ge(dve_link.sem, 3)

            @block.scalar
            def _(act):
                def step(k, slot, n):
                    act.wait_ge(x_b.sem, x_b.at(k + 1))
                    if not early_chunk(k):
                        act.wait_ge(stored[slot].sem, stored[slot].at(16 * n))
                    hold(act, "act")
                    act.activation(tmp[0:1, slot, :], cnt[0:1, slot, :], ACT.Sqrt).then_inc(act_x.sem, 1)
                paced(act, step)
                act.wait_ge(x_c.sem, x_c.at(C))
                act.activation(ndst[:], ndst[:], ACT.Sqrt).then_inc(act_link.sem, 1)
                act.wait_ge(act_link.sem, 1)

            @block.tensor
            def _(pe):
                def step(k, slot, n):
                    pe.wait_ge(x_b.sem, x_b.at(k + 1))
                    if not early_chunk(k):
                        pe.wait_ge(x_c.sem, x_c.at(k - 1))
                    hold(pe, "pe")
                    for t in range(TPC):
                        mm = pe.matmul(ps[0][:, slot * 8 + t:slot * 8 + t + 1], cnt[0:1, slot, t * P:(t + 1) * P],
                                       ones[0:1, 0:1], start=True, stop=True)
                    mm.then_inc(pe_t.sem, 1)
                paced(pe, step)
        chunkwise(x_a, x_b, x_c, act_x, pe_t)
        chunkwise(*ld, *stored, per=8)
        act_link.base = 1
        dve_link.base = 3

        hot = lrg[:, 0:4096].bitcast(BF16).rearrange("p (s t q v) -> p s t q v", s=2, t=TPC, q=4)
        iota_i = lrg[:, 4096:4352].bitcast(I32)
        iota_b = lrg[:, 4352:4480].bitcast(BF16)
        key_i = lrg[:, 4480:4480 + 4 * TILES].bitcast(I32).rearrange("p (q t) -> p q t", q=4)
        key_f = lrg[:, 6048:6048 + 4 * TILES].rearrange("p (q t) -> p q t", q=4)
        work = lrg[:, 7616:7616 + 5 * 512].rearrange("p (q v) -> p q v", q=5)
        x_base = x_b.base
        with nc.Block() as block:
            @block.gpsimd
            def _(pool):
                pool.iota(iota_i, [[1, 256]], base=0, channel_multiplier=0).then_inc(pool_link.sem, 1)
                pool.wait_ge(pool_link.sem, pool_link.at(1))

            @block.vector
            def _(dve):
                link(dve, dve_link, dve.reciprocal(ndst[:], ndst[:]))
                for q, s in ((0, src_i), (2, dst_i)):
                    link(dve, dve_link, dve.tensor_scalar(key_i[:, q, :], s[:], 8, None, ALU.arith_shift_right))
                    link(dve, dve_link, dve.tensor_scalar(key_i[:, q + 1, :], s[:], 255, None, ALU.bitwise_and))
                link(dve, dve_link, dve.tensor_copy(key_f[:], key_i[:]))
                dve.wait_ge(pool_link.sem, pool_link.at(1))
                link(dve, dve_link, dve.tensor_copy(iota_b, iota_i))

                def step(k, slot, n):
                    if not early_chunk(k):
                        dve.wait_ge(pe_t.sem, pe_t.at(k - 1))
                        hold(dve, "dve")
                    for t in range(TPC):
                        for q in range(4):
                            op = dve.tensor_scalar(hot[:, slot, t, q, :], iota_b,
                                                   key_f[:, q, bass.ds(k * TPC + t, 1)], None, ALU.is_equal)
                            op.then_inc(x_a.sem, 1)
                paced(dve, step)
                dve.wait_ge(pe_t.sem, pe_t.at(C))
                cs, cd, ep, z, t5 = (work[:, i, :] for i in range(5))
                link(dve, dve_link, dve.tensor_scalar(cs, ps[1][:], 1.0, None, ALU.max))
                link(dve, dve_link, dve.tensor_copy(cd, ps[2][:]))
                link(dve, dve_link, dve.memset(t5, 1.0))
                for h in range(2):
                    link(dve, dve_link, dve.tensor_tensor_scan(
                        ep[:, h * 256:(h + 1) * 256], t5[:, 0:256], cd[:, h * 256:(h + 1) * 256], 0.0,
                        ALU.mult, ALU.add))
                link(dve, x_b, dve.tensor_copy(sml[:, 0, 0:2], ep[:, 255:512:256]))
                dve.wait_ge(pe_o.sem, 1)
                link(dve, dve_link, dve.tensor_copy(sml[:, 0, 2:4], ps[3][:, 0:2]))
                for h in range(2):
                    link(dve, dve_link, dve.tensor_scalar(ep[:, h * 256:(h + 1) * 256], ep[:, h * 256:(h + 1) * 256],
                                                          sml[:, 0, 2 + h:3 + h], -float(NP), ALU.add, ALU.add))
                link(dve, dve_link, dve.tensor_scalar(z, cd, 0.0, None, ALU.is_gt))
                link(dve, dve_link, dve.tensor_tensor(ep, ep, z, ALU.mult))
                link(dve, dve_link, dve.tensor_scalar(ep, ep, float(NP - 1), None, ALU.add))
                dve.wait_ge(act_link.sem, act_link.at(1))
                link(dve, x_b, dve.reciprocal(cs, cs))
                dve.wait_ge(pe_o.sem, 2)
                for q, dest in ((0, nsrc), (1, endp_f)):
                    for h in range(2):
                        for o in range(2):
                            m = 128 if h == 0 else TILES // 2 - 128
                            link(dve, dve_link, dve.tensor_copy(
                                dest[:, h * 256 + o:h * 256 + o + 2 * m - 1:2],
                                ps[4 + q][:, (2 * h + o) * P:(2 * h + o) * P + m]))
                link(dve, dve_link, dve.tensor_copy(endp_i[:], endp_f[:]))
                link(dve, dve_link, dve.tensor_scalar(czero[:], bcast[:, 2:2 + L1, :], 0.0, None, ALU.max))
                link(dve, dve_link, dve.tensor_tensor(bcast[:, 0, :], bcast[:, 0, :], bcast[:, 1, :], ALU.add))

            @block.scalar
            def _(act):
                act.wait_ge(x_b.sem, x_base + 1)
                act.activation(work[:, 0, :], work[:, 0, :], ACT.Sqrt).then_inc(act_link.sem, 1)

            @block.tensor
            def _(pe):
                for b in (1, 2):
                    pe.matmul(ps[b][:], zer[0:1, 0:P], zer[0:1, :], start=True, stop=False, skip_group_check=True)

                def step(k, slot, n):
                    pe.wait_ge(x_a.sem, x_a.at(16 * k + 16))
                    hold(pe, "pe")
                    for t in range(TPC):
                        for q in range(2):
                            for h in range(2):
                                mm = pe.matmul(ps[1 + q][:, h * 256:(h + 1) * 256],
                                               hot[:, slot, t, 2 * q, h * P:(h + 1) * P],
                                               hot[:, slot, t, 2 * q + 1, :], start=False, stop=False,
                                               skip_group_check=True)
                    mm.then_inc(pe_t.sem, 1)
                paced(pe, step)
                pe.wait_ge(x_b.sem, x_base + 1)
                pe.matmul(ps[3][:, 0:2], above[:], sml[:, 0, 0:2], start=True, stop=False, skip_group_check=True)
                pe.matmul(ps[3][:, 1:2], ones[:], sml[:, 0, 0:1], start=False, stop=True,
                          skip_group_check=True).then_inc(pe_o.sem, 1)
                pe.wait_ge(x_b.sem, x_base + 2)
                for q, r in ((0, 0), (1, 2)):
                    for b in range(4):
                        mm = pe.transpose(ps[4 + q][:, b * P:(b + 1) * P], work[:, r, b * P:(b + 1) * P], ident[:])
                mm.then_inc(pe_o.sem, 1)
        pool_link.base += 1
        act_link.base += 1
        chunkwise(pe_t)
        chunkwise(x_a, per=16)
        pe_o.base = 2

        ea = lrg[:, 0:3 * TILES].rearrange("p (c t) -> p c t", c=3)
        sq = lrg[:, 3 * TILES:6 * TILES].rearrange("p (c t) -> p c t", c=3)
        yy = lrg[:, 6 * TILES:10 * TILES].rearrange("p (c t) -> p c t", c=4)
        nrm = lrg[:, 10 * TILES:11 * TILES]
        RB = NP // 16
        rad = lrg[:, 0:RB]
        wid = lrg[:, RB:2 * RB]
        inr = lrg[:, 2 * RB:3 * RB]
        y_base, l_base, q_base, s_base = x_b.base, loaded.base, act_link.base, stored[0].base
        with nc.Block() as block:
            @block.sync
            def _(sp):
                sp.dma_start(ea, a["edge_vec"]).then_inc(loaded.sem, 16)
                sp.wait_ge(x_b.sem, y_base + 2)
                sp.dma_start(r_y.rearrange("c (p t) -> p c t", p=P), yy).then_inc(stored[0].sem, 16)
                sp.wait_ge(stored[0].sem, s_base + 16)
                for c in range(8):
                    sp.dma_start(rad[16 * c:16 * c + 16, :], a["radius"]).then_inc(loaded.sem, 16)
                sp.wait_ge(x_b.sem, y_base + 4)
                sp.dma_start(r_emb.rearrange("c (s j) -> (c s) j", s=16), wid).then_inc(stored[0].sem, 16)
                sp.wait_ge(stored[0].sem, s_base + 32)

            @block.vector
            def _(dve):
                dve.wait_ge(loaded.sem, l_base + 16)
                link(dve, dve_link, dve.tensor_tensor(sq, ea, ea, ALU.mult))
                link(dve, dve_link, dve.tensor_tensor(nrm, sq[:, 0, :], sq[:, 1, :], ALU.add))
                link(dve, x_b, dve.tensor_tensor(nrm, nrm, sq[:, 2, :], ALU.add))
                dve.wait_ge(act_link.sem, q_base + 1)
                link(dve, dve_link, dve.tensor_scalar(nrm, nrm, 1e-12, None, ALU.add))
                link(dve, dve_link, dve.reciprocal(nrm, nrm))
                link(dve, dve_link, dve.memset(yy[:, 0, :], 1.0))
                for c in range(3):
                    link(dve, dve_link, dve.tensor_tensor(sq[:, c, :], ea[:, c, :], nrm, ALU.mult))
                link(dve, x_b, dve.tensor_scalar(yy[:, 1:4, :], sq, 3.0 ** 0.5, None, ALU.mult))
                dve.wait_ge(loaded.sem, l_base + 9 * 16)
                link(dve, dve_link, dve.tensor_scalar(inr, rad, 1.0, 8.0 ** 0.5, ALU.is_le, ALU.mult))
                link(dve, dve_link, dve.tensor_scalar(wid, rad, 0.0, 1.0, ALU.max, ALU.min))
                link(dve, x_b, dve.tensor_scalar(wid, wid, w["centre"][:, 0:1], 7.0, ALU.subtract, ALU.mult))
                dve.wait_ge(act_link.sem, q_base + 3)
                link(dve, x_b, dve.tensor_tensor(wid, wid, inr, ALU.mult))

            @block.scalar
            def _(act):
                act.wait_ge(x_b.sem, y_base + 1)
                act.activation(nrm, nrm, ACT.Sqrt).then_inc(act_link.sem, 1)
                act.wait_ge(x_b.sem, y_base + 3)
                act.activation(wid, wid, ACT.Square).then_inc(act_link.sem, 1)
                act.wait_ge(act_link.sem, q_base + 2)
                act.activation(wid, wid, ACT.Exp, scale=-0.5).then_inc(act_link.sem, 1)
        act_link.base += 3
        stored[0].base += 32
        loaded.base += 9 * 16

        with nc.Block() as block:
            @block.gpsimd
            def _(pool):
                paced(pool, lambda k, slot, n: pool_gather(pool, k, slot, n, a["x"], src_i, D, pe_t))

            @block.sync
            def _(sp):
                def load(k, slot, n):
                    if not early_chunk(k):
                        sp.wait_ge(x_b.sem, x_b.at(k - 1))
                        hold(sp, "sp")
                    sp.dma_start(brd[:, slot, :], a["weight"][bass.ds(k * CW, CW)].partition_broadcast(P))\
                      .then_inc(ld[slot].sem, 16)

                def store(k, slot, n):
                    sp.wait_ge(act_r.sem, act_r.at(k + 1))
                    hold(sp, "sp")
                    sp.dma_start(rows_of(t_agg, k), res[:, slot, :, 0:D]).then_inc(stored[slot].sem, 16)
                skewed(sp, load, store)
                for s in range(2):
                    sp.wait_ge(stored[s].sem, stored[s].at(8 * C))

            @block.tensor
            def _(pe):
                def turn_rows(k, slot, n):
                    wait_got(pe, slot, n)
                    if not early_chunk(k):
                        pe.wait_ge(act_x.sem, act_x.at(k - 1))
                    hold(pe, "pe")
                    for t in range(TPC):
                        mm = pe.transpose(ps[slot][:, t * P:(t + 1) * P], gat[:, slot, t, 0:D], ident[:])
                    mm.then_inc(pe_t.sem, 1)

                def out_rows(k, slot, n):
                    pe.wait_ge(dve_s.sem, dve_s.at(k + 1))
                    if not early_chunk(k):
                        pe.wait_ge(act_r.sem, act_r.at(k - 1))
                    hold(pe, "pe")
                    for t in range(TPC):
                        mm = pe.matmul(ps[4 + slot][:, t * P:(t + 1) * P], scn[:, slot, t * P:(t + 1) * P],
                                       w["lin_wT"][:], start=True, stop=True)
                    mm.then_inc(pe_o.sem, 1)

                def late(k, slot, n):
                    pe.wait_ge(act_x.sem, act_x.at(k + 1))
                    if not early_chunk(k):
                        pe.wait_ge(act_q.sem, act_q.at(k - 1))
                    hold(pe, "pe")
                    pe.matmul(ps[2 + slot][:], w["pool_wT"][:], xin[:, slot, :], start=True, stop=True)\
                      .then_inc(x_a.sem, 1)
                    if not first(k):
                        out_rows(*before(k, slot, n))
                skewed(pe, turn_rows, late)
                out_rows(C - 1, 1, C // 2 - 1)

            @block.scalar
            def _(act):
                def evacuate(k, slot, n):
                    act.wait_ge(pe_t.sem, pe_t.at(k + 1))
                    if not early_chunk(k):
                        act.wait_ge(x_a.sem, x_a.at(k - 1))
                    hold(act, "act")
                    act.activation(xin[:, slot, :], ps[slot][:], ACT.Copy).then_inc(act_x.sem, 1)

                def pooled(k, slot, n):
                    act.wait_ge(x_a.sem, x_a.at(k + 1))
                    if not early_chunk(k):
                        act.wait_ge(x_b.sem, x_b.at(k - 1))
                    hold(act, "act")
                    act.activation(sca[:, slot, :], ps[2 + slot][:], ACT.Relu, bias=w["pool_b"][:, 0:1])\
                       .then_inc(act_q.sem, 1)
                skewed(act, evacuate, pooled)

            @block.vector
            def _(dve):
                def scan(k, slot, n):
                    wait_loads(dve, slot, n, 1)
                    dve.wait_ge(act_q.sem, act_q.at(k + 1))
                    if not first(k):
                        dve.wait_ge(dve_s.sem, dve_s.at(k))
                    hold(dve, "dve")
                    dve.tensor_tensor(tmp[:, 0, :], sca[:, slot, :], brd[:, slot, :], ALU.mult).then_inc(x_b.sem, 1)
                    dve.tensor_scalar(tmp[:, 1, :], mask[:, bass.ds(k * CW, CW)], -1.0, HUGE, ALU.add, ALU.mult)\
                       .then_inc(x_c.sem, 1)
                    dve.wait_ge(x_b.sem, x_b.at(k + 1))
                    dve.wait_ge(x_c.sem, x_c.at(k + 1))
                    if not early_chunk(k):
                        dve.wait_ge(pe_o.sem, pe_o.at(k - 1))
                    hold(dve, "dve")
                    dve.tensor_tensor_scan(scn[:, slot, :], tmp[:, 1, :], tmp[:, 0, :],
                                           0.0 if first(k) else scn[:, 1 - slot, CW - 1:CW],
                                           ALU.add, ALU.max).then_inc(dve_s.sem, 1)

                def finish(k, slot, n):
                    dve.wait_ge(pe_o.sem, pe_o.at(k + 1))
                    if not early_chunk(k):
                        dve.wait_ge(stored[slot].sem, stored[slot].at(16 * n))
                    hold(dve, "dve")
                    dve.tensor_tensor(res[:, slot, :, 0:D], tiles(ps[4 + slot][:]),
                                      bcast[:, 0:1, :].to_broadcast([P, TPC, D]), ALU.add).then_inc(act_r.sem, 1)
                skewed(dve, scan, finish)
        gathered()
        chunkwise(pe_t, pe_o, x_a, x_b, x_c, act_x, act_q, act_r, dve_s)
        chunkwise(*ld, *stored, per=8)

        def node_pass(base_rows, agg, stores, extend=False, lanes_in=None):
            width = EXT if extend else D
            loads = LANES if lanes_in else 1
            wide = lrg[:, 0:4 * LANES * CW // 2 * 1].rearrange("p (s l v) -> p s l v", s=2, l=LANES) \
                if lanes_in else None
            with nc.Block() as block:
                if not lanes_in:
                    @block.gpsimd
                    def _(pool):
                        paced(pool, lambda k, slot, n: pool_gather(pool, k, slot, n, agg, endp_i, D, x_a))

                @block.sync
                def _(sp):
                    def load(k, slot, n):
                        if not early_chunk(k):
                            sp.wait_ge(x_a.sem, x_a.at(k - 1))
                            hold(sp, "sp")
                        if lanes_in:
                            for l, table in enumerate(lanes_in):
                                sp.dma_start(tiles(wide[:, slot, l, :]), rows_of(table, k)).then_inc(ld[slot].sem, 16)
                        else:
                            sp.dma_start(tiles(brd[:, slot, :]), rows_of(base_rows, k)).then_inc(ld[slot].sem, 16)

                    def store(k, slot, n):
                        sp.wait_ge(act_r.sem, act_r.at(k + 1))
                        hold(sp, "sp")
                        for table in stores:
                            sp.dma_start(rows_of(table, k, width), res[:, slot, :, 0:width])\
                              .then_inc(stored[slot].sem, 16)
                    skewed(sp, load, store)
                    for s in range(2):
                        sp.wait_ge(stored[s].sem, stored[s].at(8 * C * len(stores)))

                @block.vector
                def _(dve):
                    def stats(k, slot, n):
                        wait_loads(dve, slot, n, loads)
                        if not lanes_in:
                            wait_got(dve, slot, n)
                        if not early_chunk(k):
                            dve.wait_ge(act_r.sem, act_r.at(k - 1))
                        hold(dve, "dve")
                        if lanes_in:
                            dve.tensor_tensor(tmp[:, slot, :], wide[:, slot, 0, :], wide[:, slot, 1, :], ALU.add)\
                               .then_inc(x_d.sem, 1)
                            dve.tensor_tensor(xin[:, slot, :], wide[:, slot, 2, :], wide[:, slot, 3, :], ALU.add)\
                               .then_inc(x_d.sem, 1)
                            dve.wait_ge(x_d.sem, x_d.at(2 * k + 2))
                            hold(dve, "dve")
                            dve.tensor_tensor(sca[:, slot, :], tmp[:, slot, :], xin[:, slot, :], ALU.add)\
                               .then_inc(x_a.sem, 1)
                        else:
                            dve.tensor_tensor(tiles(sca[:, slot, :]), gat[:, slot, :, 0:D], tiles(brd[:, slot, :]),
                                              ALU.add).then_inc(x_a.sem, 1)
                        dve.wait_ge(x_a.sem, x_a.at(k + 1))
                        hold(dve, "dve")
                        for t in range(TPC):
                            dve.bn_stats(sml[:, slot, 6 * t:6 * t + 6], sca[:, slot, t * P:(t + 1) * P])\
                               .then_inc(x_e.sem, 1)
                        dve.wait_ge(x_e.sem, x_e.at(4 * k + 4))
                        hold(dve, "dve")
                        for t in range(TPC):
                            dve.bn_aggr(sml[:, slot, 24 + 2 * t:26 + 2 * t], sml[:, slot, 6 * t:6 * t + 6])\
                               .then_inc(x_b.sem, 1)

                    def scales(k, slot, n):
                        dve.wait_ge(act_q.sem, act_q.at(k + 1))
                        hold(dve, "dve")
                        dve.reciprocal(sml[:, slot, 36:40], sml[:, slot, 32:36]).then_inc(x_f.sem, 1)
                        dve.wait_ge(x_f.sem, x_f.at(k + 1))
                        hold(dve, "dve")
                        dve.scalar_tensor_tensor(out=sml[:, slot, 40:44], in0=sml[:, slot, 24:32:2], scalar=-1.0,
                                                 in1=sml[:, slot, 36:40], op0=ALU.mult, op1=ALU.mult)\
                           .then_inc(x_c.sem, 1)
                    skewed(dve, stats, scales)

                @block.scalar
                def _(act):
                    def root(k, slot, n):
                        act.wait_ge(x_b.sem, x_b.at(4 * k + 4))
                        hold(act, "act")
                        act.activation(sml[:, slot, 32:36], sml[:, slot, 25:32:2], ACT.Sqrt, bias=epsc[:, 0:1])\
                           .then_inc(act_q.sem, 1)

                    def normalise(k, slot, n):
                        act.wait_ge(x_c.sem, x_c.at(k + 1))
                        if not early_chunk(k):
                            act.wait_ge(stored[slot].sem, stored[slot].at(16 * len(stores) * n))
                        hold(act, "act")
                        if extend:
                            act.activation(res[:, slot, :, D], nsrc[:, bass.ds(k * TPC, TPC)], ACT.Copy)
                            act.activation(res[:, slot, :, D + 1], endp_f[:, bass.ds(k * TPC, TPC)], ACT.Copy)
                        for t in range(TPC):
                            op = act.activation(res[:, slot, t, 0:D], sca[:, slot, t * P:(t + 1) * P], ACT.Identity,
                                                bias=sml[:, slot, 40 + t:41 + t], scale=sml[:, slot, 36 + t:37 + t])
                        op.then_inc(act_r.sem, 1)
                    skewed(act, root, normalise)
            if not lanes_in:
                gathered()
            else:
                chunkwise(x_d, per=2)
            chunkwise(x_a, x_c, x_f, act_q, act_r)
            chunkwise(x_b, x_e, per=4)
            chunkwise(*ld, per=8 * loads)
            chunkwise(*stored, per=8 * len(stores))

        node_pass(a["x"], t_agg, [t_x1e], extend=True)

        def gcn_pass(l):
            table = t_x1e if l == 0 else t_h[l - 1]
            loads = 1 if l == 0 else 2
            saves = 2 if l == 0 else 1
            freed = x_a if l == 0 else pe_t
            p_base = pe_o.base
            with nc.Block() as block:
                @block.gpsimd
                def _(pool):
                    if l == 0:
                        paced(pool, lambda k, slot, n: pool_gather(pool, k, slot, n, table, src_i, EXT, x_a, per=3))
                    else:
                        paced(pool, lambda k, slot, n: pool_gather(pool, k, slot, n, table, pos_i, D, pe_t))

                @block.sync
                def _(sp):
                    def load(k, slot, n):
                        if not early_chunk(k):
                            sp.wait_ge(pe_o.sem, pe_o.at(k - 1))
                            hold(sp, "sp")
                            if l:
                                sp.wait_ge(x_b.sem, x_b.at(k - 1))
                                hold(sp, "sp")
                        sp.dma_start(row1[0:1, slot, :], r_sq[0:1, bass.ds(k * CW, CW)]).then_inc(ld[slot].sem, 16)
                        if l:
                            sp.dma_start(brd[:, slot, :], r_ns.rearrange("t p -> (t p)")[bass.ds(k * CW, CW)]
                                         .partition_broadcast(P)).then_inc(ld[slot].sem, 16)

                    def store(k, slot, n):
                        if l == 0:
                            sp.wait_ge(x_d.sem, x_d.at(k + 1))
                            hold(sp, "sp")
                            sp.dma_start(r_ns[bass.ds(k * TPC, TPC), :], nst[:, slot, :]).then_inc(stored[slot].sem, 16)
                        sp.wait_ge(act_r.sem, act_r.at(k + 1))
                        hold(sp, "sp")
                        sp.dma_start(rows_of(t_h[l], k), res[:, slot, :, 0:D]).then_inc(stored[slot].sem, 16)
                    skewed(sp, load, store)
                    for s in range(2):
                        sp.wait_ge(stored[s].sem, stored[s].at(8 * saves * C))

                @block.tensor
                def _(pe):
                    def turn_rows(k, slot, n):
                        if l == 0:
                            pe.wait_ge(x_a.sem, x_a.at(3 * k + 3))
                        else:
                            wait_got(pe, slot, n)
                        if not early_chunk(k):
                            pe.wait_ge(act_x.sem, act_x.at(k - 1))
                            if l == 0:
                                pe.wait_ge(x_d.sem, x_d.at(k - 1))
                        hold(pe, "pe")
                        if l == 0:
                            pe.matmul(ps[7][0:TPC, slot * P:(slot + 1) * P], sml[:, slot, 0:TPC], ident[:],
                                      start=True, stop=True)
                        for t in range(TPC):
                            rows_in = sca[:, slot, t * P:(t + 1) * P] if l == 0 else gat[:, slot, t, 0:D]
                            mm = pe.transpose(ps[slot][:, t * P:(t + 1) * P], rows_in, ident[:])
                        mm.then_inc(pe_t.sem, 1)

                    def sums(k, slot, n):
                        pe.wait_ge(act_q.sem, act_q.at(k + 1))
                        hold(pe, "pe")
                        for q in range(2):
                            for t in range(TPC):
                                mm = pe.matmul(ps[6][:, q:q + 1], dev[:, slot, t, q, :], ends[:, bass.ds(k * TPC + t, 1)],
                                               start=False, stop=False, skip_group_check=True)
                        mm.then_inc(pe_s.sem, 1)

                    def late(k, slot, n):
                        pe.wait_ge(dve_s.sem, dve_s.at(k + 1))
                        wait_loads(pe, slot, n, loads)
                        if not early_chunk(k):
                            pe.wait_ge(act_r.sem, act_r.at(k - 1))
                        hold(pe, "pe")
                        for t in range(TPC):
                            pe.matmul(ps[4 + slot][:, t * P:(t + 1) * P], scn[:, slot, t * P:(t + 1) * P],
                                      gcn_w[:, l, :], start=True, stop=False)
                            mm = pe.matmul(ps[4 + slot][:, t * P:(t + 1) * P], row1[0:1, slot, t * P:(t + 1) * P],
                                           rows[0:1, l, :], start=False, stop=True)
                        mm.then_inc(pe_o.sem, 1)
                        if not first(k):
                            sums(*before(k, slot, n))
                    pe.matmul(ps[6][:, 0:2], zer[0:1, 0:P], zer[0:1, 0:2], start=True, stop=False,
                              skip_group_check=True)
                    skewed(pe, turn_rows, late)
                    sums(C - 1, 1, C // 2 - 1)

                @block.scalar
                def _(act):
                    def evacuate(k, slot, n):
                        act.wait_ge(pe_t.sem, pe_t.at(k + 1))
                        if not early_chunk(k):
                            act.wait_ge((dve_s if l == 0 else x_b).sem, (dve_s if l == 0 else x_b).at(k - 1))
                            if l == 0:
                                act.wait_ge(stored[slot].sem, stored[slot].at(16 * saves * n))
                        hold(act, "act")
                        if l == 0:
                            act.activation(nst[:, slot, :], ps[7][0:TPC, slot * P:(slot + 1) * P], ACT.Copy)\
                               .then_inc(x_d.sem, 1)
                            act.activation(xin[:, slot, :], ps[slot][:], ACT.Copy).then_inc(act_x.sem, 1)
                        else:
                            act.activation(xin[:, slot, :], ps[slot][:], ACT.Relu, bias=aff[:, l - 1, 1:2],
                                           scale=aff[:, l - 1, 0:1]).then_inc(act_x.sem, 1)

                    def square(k, slot, n):
                        act.wait_ge(dve_d.sem, dve_d.at(k + 1))
                        hold(act, "act")
                        act.activation(dev[:, slot, :, 1, :], dev[:, slot, :, 0, :], ACT.Square).then_inc(act_q.sem, 1)

                    def late(k, slot, n):
                        if not first(k):
                            square(*before(k, slot, n))
                        act.wait_ge(pe_o.sem, pe_o.at(k + 1))
                        if not early_chunk(k):
                            act.wait_ge(stored[slot].sem, stored[slot].at(16 * saves * n))
                            act.wait_ge(dve_d.sem, dve_d.at(k - 1))
                        hold(act, "act")
                        for t in range(TPC):
                            op = act.activation(res[:, slot, t, 0:D], ps[4 + slot][:, t * P:(t + 1) * P], ACT.Relu,
                                                scale=ndst[:, bass.ds(k * TPC + t, 1)])
                        op.then_inc(act_r.sem, 1)
                    if l < 2:
                        act.dma_start(t_acc[l][NP:ROWS, :].rearrange("(p r) d -> p (r d)", p=P), zer[:, 0:2 * D])\
                           .then_inc(loaded.sem, 16)
                    else:
                        act.dma_start(t_acc[l].rearrange("(p a r) d -> p a (r d)", p=P, a=ROWS // P // 2),
                                      zer[:, 0:2 * D].unsqueeze(1).to_broadcast([P, ROWS // P // 2, 2 * D]))\
                           .then_inc(loaded.sem, 16)
                    skewed(act, evacuate, late)
                    square(C - 1, 1, C // 2 - 1)
                    act.wait_ge(loaded.sem, loaded.at(16))
                    act.wait_ge(x_e.sem, x_e.at(1))
                    act.activation(sml[:, 1, 4:5], sml[:, 1, 3:4], ACT.Sqrt, bias=epsc[:, 0:1])\
                       .then_inc(act_link.sem, 1)

                @block.vector
                def _(dve):
                    def scan(k, slot, n):
                        if l == 0:
                            wait_got(dve, slot, n)
                            if not early_chunk(k):
                                dve.wait_ge(pe_t.sem, pe_t.at(k - 1))
                            hold(dve, "dve")
                            dve.tensor_copy(sml[:, slot, 0:TPC], gat[:, slot, :, D]).then_inc(x_a.sem, 1)
                            dve.tensor_tensor(tiles(sca[:, slot, :]), gat[:, slot, :, 0:D],
                                              gat[:, slot, :, D:D + 1].to_broadcast([P, TPC, D]), ALU.mult)\
                               .then_inc(x_a.sem, 1)
                            dve.tensor_copy(pos_i[:, bass.ds(k * TPC, TPC)], gat[:, slot, :, D + 1])\
                               .then_inc(x_a.sem, 1)
                        dve.wait_ge(act_x.sem, act_x.at(k + 1))
                        if l:
                            wait_loads(dve, slot, n, loads)
                        if not early_chunk(k):
                            dve.wait_ge(pe_o.sem, pe_o.at(k - 1))
                        if not first(k):
                            dve.wait_ge(dve_s.sem, dve_s.at(k))
                        hold(dve, "dve")
                        if l:
                            dve.tensor_tensor(tmp[:, slot, :], xin[:, slot, :], brd[:, slot, :], ALU.mult)\
                               .then_inc(x_b.sem, 1)
                            dve.wait_ge(x_b.sem, x_b.at(k + 1))
                            hold(dve, "dve")
                        dve.tensor_tensor_scan(scn[:, slot, :], mask[:, bass.ds(k * CW, CW)],
                                               (tmp if l else xin)[:, slot, :],
                                               0.0 if first(k) else scn[:, 1 - slot, CW - 1:CW],
                                               ALU.mult, ALU.add).then_inc(dve_s.sem, 1)

                    def deviate(k, slot, n):
                        dve.wait_ge(act_r.sem, act_r.at(k + 1))
                        if not early_chunk(k):
                            dve.wait_ge(pe_s.sem, pe_s.at(k - 1))
                        hold(dve, "dve")
                        dve.tensor_tensor(dev[:, slot, :, 0, :], res[:, slot, :, 0:D],
                                          czero[:, l:l + 1, :].to_broadcast([P, TPC, D]), ALU.subtract)\
                           .then_inc(dve_d.sem, 1)
                    skewed(dve, scan, deviate)
                    dve.wait_ge(pe_s.sem, pe_s.at(C))
                    m = sml[:, 1, :]
                    link(dve, dve_link, dve.tensor_scalar(m[:, 0:2], ps[6][:, 0:2], 1.0 / N, None, ALU.mult))
                    link(dve, dve_link, dve.tensor_tensor(m[:, 2:3], m[:, 0:1], m[:, 0:1], ALU.mult))
                    link(dve, x_e, dve.tensor_tensor(m[:, 3:4], m[:, 1:2], m[:, 2:3], ALU.subtract))
                    dve.wait_ge(act_link.sem, act_link.at(1))
                    link(dve, dve_link, dve.reciprocal(m[:, 5:6], m[:, 4:5]))
                    link(dve, dve_link, dve.tensor_tensor(aff[:, l, 0:1], m[:, 5:6], w["gamT"][:, l:l + 1], ALU.mult))
                    link(dve, dve_link, dve.tensor_scalar(m[:, 6:7], w["bsT"][:, l:l + 1], 0.0, m[:, 0:1],
                                                          ALU.max, ALU.add))
                    link(dve, dve_link, dve.tensor_tensor(m[:, 7:8], m[:, 6:7], aff[:, l, 0:1], ALU.mult))
                    link(dve, dve_link, dve.tensor_tensor(aff[:, l, 1:2], w["betT"][:, l:l + 1], m[:, 7:8],
                                                          ALU.subtract))
            act_link.base += 1
            gathered()
            loaded.base += 16
            chunkwise(pe_t, pe_o, pe_s, act_x, act_q, act_r, dve_s, dve_d)
            if l == 0:
                chunkwise(x_a, per=3)
                chunkwise(x_d)
            else:
                chunkwise(x_b)
            chunkwise(*ld, per=8 * loads)
            chunkwise(*stored, per=8 * saves)

        for l in range(L1):
            gcn_pass(l)

        hin = lrg[:, 0:4096].rearrange("p (s l t d) -> p s l t d", s=2, l=L1, t=TPC)
        hfm = lrg[:, 4096:8192].rearrange("p (s l v) -> p s l v", s=2, l=L1)
        with nc.Block() as block:
            @block.sync
            def _(sp):
                def load(k, slot, n):
                    if not early_chunk(k):
                        sp.wait_ge(pe_t.sem, pe_t.at(L1 * (k - 1)))
                        hold(sp, "sp")
                    for l in range(L1):
                        sp.dma_start(hin[:, slot, l, :, :], rows_of(t_h[l], k)).then_inc(ld[slot].sem, 16)

                def store(k, slot, n):
                    sp.wait_ge(act_r.sem, act_r.at(k + 1))
                    hold(sp, "sp")
                    sp.dma_start(rows_of(t_agg, k), res[:, slot, :, 0:D]).then_inc(stored[slot].sem, 16)
                skewed(sp, load, store)
                for s in range(2):
                    sp.wait_ge(stored[s].sem, stored[s].at(8 * C))

            @block.tensor
            def _(pe):
                def turn_rows(k, slot, n):
                    wait_loads(pe, slot, n, L1)
                    for l in range(L1):
                        if not first(k):
                            pe.wait_ge(act_x.sem, act_x.at(L1 * (k - 1) + l + 1))
                        hold(pe, "pe")
                        for t in range(TPC):
                            mm = pe.transpose(ps[l][:, t * P:(t + 1) * P], hin[:, slot, l, t, :], ident[:])
                        mm.then_inc(pe_t.sem, 1)

                def late(k, slot, n):
                    pe.wait_ge(dve_s.sem, dve_s.at(k + 1))
                    if not early_chunk(k):
                        pe.wait_ge(act_r.sem, act_r.at(k - 1))
                    hold(pe, "pe")
                    for t in range(TPC):
                        pe.matmul(ps[4 + slot][:, t * P:(t + 1) * P], scn[:, slot, t * P:(t + 1) * P],
                                  w["lin1_w"][:], start=True, stop=False)
                        mm = pe.matmul(ps[4 + slot][:, t * P:(t + 1) * P], ones[0:1, :], rows[0:1, L1, :],
                                       start=False, stop=True)
                    mm.then_inc(pe_o.sem, 1)
                skewed(pe, turn_rows, late)

            @block.scalar
            def _(act):
                def normed(k, slot, n):
                    for l in range(L1):
                        act.wait_ge(pe_t.sem, pe_t.at(L1 * k + l + 1))
                        if l == 0 and not early_chunk(k):
                            act.wait_ge(x_a.sem, x_a.at(2 * (k - 1)))
                        hold(act, "act")
                        act.activation(hfm[:, slot, l, :], ps[l][:], ACT.Relu, bias=aff[:, l, 1:2],
                                       scale=aff[:, l, 0:1]).then_inc(act_x.sem, 1)

                def finish(k, slot, n):
                    act.wait_ge(pe_o.sem, pe_o.at(k + 1))
                    if not early_chunk(k):
                        act.wait_ge(stored[slot].sem, stored[slot].at(16 * n))
                    hold(act, "act")
                    act.activation(res[:, slot, :, 0:D], tiles(ps[4 + slot][:]), ACT.Relu).then_inc(act_r.sem, 1)
                skewed(act, normed, finish)

            @block.vector
            def _(dve):
                def step(k, slot, n):
                    dve.wait_ge(act_x.sem, act_x.at(L1 * k + L1))
                    if not first(k):
                        dve.wait_ge(dve_s.sem, dve_s.at(k))
                    hold(dve, "dve")
                    dve.tensor_tensor(tmp[:, slot, :], hfm[:, slot, 0, :], hfm[:, slot, 1, :], ALU.max)\
                       .then_inc(x_a.sem, 1)
                    dve.tensor_tensor(sca[:, slot, :], hfm[:, slot, 2, :], hfm[:, slot, 3, :], ALU.max)\
                       .then_inc(x_a.sem, 1)
                    dve.wait_ge(x_a.sem, x_a.at(2 * k + 2))
                    if not early_chunk(k):
                        dve.wait_ge(pe_o.sem, pe_o.at(k - 1))
                    hold(dve, "dve")
                    dve.tensor_tensor(scn[:, slot, :], tmp[:, slot, :], sca[:, slot, :], ALU.max)\
                       .then_inc(dve_s.sem, 1)
                paced(dve, step)
        chunkwise(pe_o, act_r, dve_s)
        chunkwise(pe_t, act_x, *ld[0:0], per=L1)
        chunkwise(x_a, per=2)
        chunkwise(*ld, per=8 * L1)
        chunkwise(*stored, per=8)

        node_pass(t_x1e, t_agg, [t_x2])

        def big(i):
            return lrg[:, i * CW:(i + 1) * CW]
        wA, wB, vy, mA, mB = (big(i) for i in range(5))
        sA = [big(5), big(6)]
        sB = [big(7), big(8)]
        h1, h2 = tmp, sca
        with nc.Block() as block:
            @block.gpsimd
            def _(pool):
                paced(pool, lambda k, slot, n: pool_gather(pool, k, slot, n, t_x2, src_i, D, pe_t))

            @block.sync
            def _(sp):
                def load(k, slot, n):
                    if not early_chunk(k):
                        sp.wait_ge(x_c.sem, x_c.at(k - 1))
                        hold(sp, "sp")
                        sp.wait_ge(x_e.sem, x_e.at(k - 1))
                        hold(sp, "sp")
                    sp.dma_start(embs[:, slot, :], r_emb[:, bass.ds(k * CW, CW)]).then_inc(ld[slot].sem, 16)
                    for c in range(4):
                        sp.dma_start(brd[32 * c:32 * c + 32, slot, :],
                                     r_y[c, bass.ds(k * CW, CW)].partition_broadcast(32)).then_inc(ld[slot].sem, 16)

                def store(k, slot, n):
                    sp.wait_ge(act_r.sem, act_r.at(k + 1))
                    hold(sp, "sp")
                    sp.dma_start(rows_of(t_agg, k), res[:, slot, :, 0:D]).then_inc(stored[slot].sem, 16)
                skewed(sp, load, lambda k, slot, n: None if first(k) else store(*before(k, slot, n)))
                store(C - 1, 1, C // 2 - 1)
                for s in range(2):
                    sp.wait_ge(stored[s].sem, stored[s].at(8 * C))

            @block.tensor
            def _(pe):
                def early(k, slot, n):
                    wait_loads(pe, slot, n, 5)
                    if not first(k):
                        pe.wait_ge(act_q.sem, act_q.at(2 * k))
                    hold(pe, "pe")
                    pe.matmul(ps[2][0:64, :], w["mlp_w0"][:], embs[:, slot, :], start=True, stop=True)\
                      .then_inc(x_e.sem, 1)
                    wait_got(pe, slot, n)
                    if not early_chunk(k):
                        pe.wait_ge(act_x.sem, act_x.at(k - 1))
                    hold(pe, "pe")
                    for t in range(TPC):
                        mm = pe.transpose(ps[slot][:, t * P:(t + 1) * P], gat[:, slot, t, 0:D], ident[:])
                    mm.then_inc(pe_t.sem, 1)
                    pe.wait_ge(act_q.sem, act_q.at(2 * k + 1))
                    hold(pe, "pe")
                    pe.matmul(ps[2][0:64, :], w["mlp_w1"][:], h1[0:64, slot, :], start=True, stop=True)\
                      .then_inc(x_f.sem, 1)

                def out_rows(k, slot, n):
                    pe.wait_ge(dve_s.sem, dve_s.at(2 * k + 2))
                    if not first(k):
                        pe.wait_ge(act_r.sem, act_r.at(k))
                    hold(pe, "pe")
                    for t in range(TPC):
                        pe.matmul(ps[3][:, t * P:(t + 1) * P], sA[slot][:, t * P:(t + 1) * P], w["w_outA"][:],
                                  start=True, stop=False)
                        mm = pe.matmul(ps[3][:, t * P:(t + 1) * P], sB[slot][:, t * P:(t + 1) * P], w["w_outB"][:],
                                       start=False, stop=True)
                    mm.then_inc(pe_o.sem, 1)

                def late(k, slot, n):
                    pe.wait_ge(act_x.sem, act_x.at(k + 1))
                    if not first(k):
                        pe.wait_ge(x_d.sem, x_d.at(k))
                    hold(pe, "pe")
                    pe.matmul(ps[7][:], w["w_vv"][:], xin[:, slot, :], start=True, stop=True,
                              skip_group_check=True).then_inc(x_a.sem, 1)
                    pe.wait_ge(act_q.sem, act_q.at(2 * k + 2))
                    if not first(k):
                        pe.wait_ge(dve_d.sem, dve_d.at(2 * k))
                        pe.wait_ge(x_c.sem, x_c.at(k))
                    hold(pe, "pe")
                    pe.matmul(ps[4][:], w["mlp_w2A"][:], h2[0:64, slot, :], start=True, stop=True).then_inc(pe_s.sem, 1)
                    pe.matmul(ps[6][:], w["w_ss"][:], xin[:, slot, :], start=True, stop=True).then_inc(x_a.sem, 1)
                    pe.matmul(ps[5][:], w["mlp_w2B"][:], h2[0:64, slot, :], start=True, stop=True).then_inc(pe_s.sem, 1)
                    pe.wait_ge(x_b.sem, x_b.at(k + 1))
                    hold(pe, "pe")
                    pe.matmul(ps[7][:], w["w_dot"][:], vy, start=False, stop=True,
                              skip_group_check=True).then_inc(zeroed.sem, 1)
                    if not first(k):
                        out_rows(*before(k, slot, n))
                skewed(pe, early, late)
                out_rows(C - 1, 1, C // 2 - 1)

            @block.scalar
            def _(act):
                def early(k, slot, n):
                    act.wait_ge(x_e.sem, x_e.at(k + 1))
                    if not early_chunk(k):
                        act.wait_ge(x_f.sem, x_f.at(k - 1))
                    hold(act, "act")
                    act.activation(h1[0:64, slot, :], ps[2][0:64, :], ACT.Silu, bias=w["mlp_b0"][:, 0:1])\
                       .then_inc(act_q.sem, 1)
                    act.wait_ge(pe_t.sem, pe_t.at(k + 1))
                    if not early_chunk(k):
                        act.wait_ge(x_a.sem, x_a.at(2 * (k - 1)))
                    hold(act, "act")
                    act.activation(xin[:, slot, :], ps[slot][:], ACT.Copy).then_inc(act_x.sem, 1)
                    act.wait_ge(x_f.sem, x_f.at(k + 1))
                    if not early_chunk(k):
                        act.wait_ge(pe_s.sem, pe_s.at(2 * (k - 1)))
                    hold(act, "act")
                    act.activation(h2[0:64, slot, :], ps[2][0:64, :], ACT.Silu, bias=w["mlp_b1"][:, 0:1])\
                       .then_inc(act_q.sem, 1)

                def finish(k, slot, n):
                    act.wait_ge(pe_o.sem, pe_o.at(k + 1))
                    if not early_chunk(k):
                        act.wait_ge(stored[slot].sem, stored[slot].at(16 * n))
                    hold(act, "act")
                    act.activation(res[:, slot, :, 0:D], tiles(ps[3][:]), ACT.Copy,
                                   scale=1.0 / (32.0 ** 0.5 * 8.0 * 16.0)).then_inc(act_r.sem, 1)

                def late(k, slot, n):
                    act.wait_ge(pe_s.sem, pe_s.at(2 * k + 1))
                    if not first(k):
                        act.wait_ge(x_c.sem, x_c.at(k))
                    hold(act, "act")
                    act.activation(wA, ps[4][:], ACT.Identity, bias=w["mlp_b2A"][:, 0:1]).then_inc(dve_d.sem, 1)
                    act.wait_ge(pe_s.sem, pe_s.at(2 * k + 2))
                    if not first(k):
                        act.wait_ge(x_d.sem, x_d.at(k))
                    hold(act, "act")
                    act.activation(wB, ps[5][:], ACT.Identity, bias=w["mlp_b2B"][:, 0:1]).then_inc(dve_d.sem, 1)
                    if not first(k):
                        finish(*before(k, slot, n))
                skewed(act, early, late)
                finish(C - 1, 1, C // 2 - 1)

            @block.vector
            def _(dve):
                def step(k, slot, n):
                    wait_loads(dve, slot, n, 5)
                    dve.wait_ge(x_a.sem, x_a.at(2 * k + 1))
                    if not first(k):
                        dve.wait_ge(zeroed.sem, zeroed.at(k))
                    hold(dve, "dve")
                    dve.tensor_tensor(vy, ps[7][:], brd[:, slot, :], ALU.mult).then_inc(x_b.sem, 1)
                    dve.wait_ge(x_a.sem, x_a.at(2 * k + 2))
                    dve.wait_ge(dve_d.sem, dve_d.at(2 * k + 1))
                    if not first(k):
                        dve.wait_ge(dve_s.sem, dve_s.at(2 * k))
                    hold(dve, "dve")
                    dve.tensor_tensor(mA, ps[6][:], wA, ALU.mult).then_inc(act_e.sem, 1)
                    dve.wait_ge(act_e.sem, act_e.at(k + 1))
                    hold(dve, "dve")
                    dve.tensor_tensor(mA, mA, brd[:, slot, :], ALU.mult).then_inc(x_c.sem, 1)
                    dve.wait_ge(x_c.sem, x_c.at(k + 1))
                    if not early_chunk(k):
                        dve.wait_ge(pe_o.sem, pe_o.at(k - 1))
                    hold(dve, "dve")
                    here = mask[:, bass.ds(k * CW, CW)]
                    dve.tensor_tensor_scan(sA[slot], here, mA, 0.0 if first(k) else sA[1 - slot][:, CW - 1:CW],
                                           ALU.mult, ALU.add).then_inc(dve_s.sem, 1)
                    dve.wait_ge(zeroed.sem, zeroed.at(k + 1))
                    dve.wait_ge(dve_d.sem, dve_d.at(2 * k + 2))
                    hold(dve, "dve")
                    dve.tensor_tensor(mB, ps[7][:], wB, ALU.mult).then_inc(x_d.sem, 1)
                    dve.wait_ge(x_d.sem, x_d.at(k + 1))
                    hold(dve, "dve")
                    dve.tensor_tensor_scan(sB[slot], here, mB, 0.0 if first(k) else sB[1 - slot][:, CW - 1:CW],
                                           ALU.mult, ALU.add).then_inc(dve_s.sem, 1)
                paced(dve, step)
        gathered()
        chunkwise(pe_t, pe_o, x_b, x_c, x_d, x_e, x_f, act_x, act_r, act_e, zeroed)
        chunkwise(x_a, pe_s, act_q, dve_d, dve_s, per=2)
        chunkwise(*ld, per=8 * 5)
        chunkwise(*stored, per=8)

        node_pass(t_x2, t_agg, [t_x3, t_acc[0], t_acc[1]])

        eq = lrg[:, 0:512].rearrange("p (t v) -> p t v", t=TPC)
        eqs = [lrg[:, 1024 * s:1024 * s + CW] for s in range(2)]
        eqb = lrg[:, 512:1024]
        f1 = [lrg[:, 2048 + CW * s:2048 + CW * (s + 1)] for s in range(2)]
        f2 = [lrg[:, 3072 + CW * s:3072 + CW * (s + 1)] for s in range(2)]
        msg = [lrg[:, 4096 + CW * s:4096 + CW * (s + 1)] for s in range(2)]
        srow = [lrg[:, 5120 + CW * s:5120 + CW * (s + 1)].bitcast(I32) for s in range(2)]
        ab = lrg[:, 6144:6144 + CW]
        ex = lrg[:, 6656:6656 + CW]
        src_f = lrg[:, 8192:8192 + TILES]
        away = lrg[:, 8704:8704 + TILES]
        with nc.Block() as block:
            @block.gpsimd
            def _(pool):
                def scatter(k, slot, n):
                    pool.wait_ge(act_r.sem, act_r.at(k + 1))
                    pool.wait_ge(x_d.sem, x_d.at(k + 1))
                    if not first(k):
                        for t in range(TPC):
                            pool.wait_ge(lanes[t].sem, lanes[t].at(16 * k))
                    hold(pool, "pool")
                    for t in range(TPC):
                        pool.indirect_dma_start(t_acc[t], bass.IndirectOffsetOnAxis(ap=sidx[:, slot, t:t + 1], axis=0),
                                                res[:, slot, t, 0:D], None, compute_op=ALU.add)\
                            .then_inc(lanes[t].sem, 16)
                skewed(pool, lambda k, slot, n: pool_gather(pool, k, slot, n, t_x3, dst_i, D, x_b), scatter)
                for t in range(TPC):
                    pool.wait_ge(lanes[t].sem, lanes[t].at(16 * C))

            @block.sync
            def _(sp):
                def load(k, slot, n):
                    if not early_chunk(k):
                        sp.wait_ge(pe_t.sem, pe_t.at(k - 1))
                        hold(sp, "sp")
                        sp.wait_ge(x_a.sem, x_a.at(k - 1))
                        hold(sp, "sp")
                    sp.dma_start(att[:, slot, :], a["edge_attr"][:, bass.ds(k * CW, CW)]).then_inc(ld[slot].sem, 16)
                    sp.dma_start(srow[slot], a["src_row"][bass.ds(k * CW, CW)].partition_broadcast(P))\
                      .then_inc(ld[slot].sem, 16)
                paced(sp, load)

            @block.tensor
            def _(pe):
                def filt1(k, slot, n):
                    wait_loads(pe, slot, n, 2)
                    if not early_chunk(k):
                        pe.wait_ge(x_e.sem, x_e.at(k - 1))
                    hold(pe, "pe")
                    pe.matmul(ps[slot][:], w["W1"][:], att[:, slot, :], start=True, stop=True).then_inc(pe_t.sem, 1)

                def dedupe(k, slot, n):
                    pe.wait_ge(x_b.sem, x_b.at(k + 1))
                    pe.wait_ge(x_a.sem, x_a.at(k + 1))
                    if not early_chunk(k):
                        pe.wait_ge(act_r.sem, act_r.at(k - 1))
                    hold(pe, "pe")
                    for t in range(TPC):
                        mm = pe.matmul(ps[4 + slot][:, t * P:(t + 1) * P], eqs[slot][:, t * P:(t + 1) * P],
                                       msg[slot][:, t * P:(t + 1) * P], start=True, stop=True)
                    mm.then_inc(pe_o.sem, 1)

                def late(k, slot, n):
                    pe.wait_ge(x_e.sem, x_e.at(k + 1))
                    if not early_chunk(k):
                        pe.wait_ge(x_i.sem, x_i.at(k - 1))
                    hold(pe, "pe")
                    for t in range(TPC):
                        pe.matmul(ps[2 + slot][:, t * P:(t + 1) * P], f1[slot][:, t * P:(t + 1) * P], w["W2"][:],
                                  start=True, stop=False)
                        mm = pe.matmul(ps[2 + slot][:, t * P:(t + 1) * P], ones[0:1, :], rows[0:1, L1 + 1, :],
                                       start=False, stop=True)
                    mm.then_inc(pe_s.sem, 1)
                    if not first(k):
                        dedupe(*before(k, slot, n))
                skewed(pe, filt1, late)
                dedupe(C - 1, 1, C // 2 - 1)

            @block.scalar
            def _(act):
                def soft1(k, slot, n):
                    act.wait_ge(x_g.sem, x_g.at(k + 1))
                    hold(act, "act")
                    act.activation(f1[slot], f1[slot], ACT.Exp).then_inc(act_q.sem, 1)
                    act.wait_ge(act_q.sem, act_q.at(k + 1))
                    hold(act, "act")
                    act.activation(f1[slot], f1[slot], ACT.Ln, bias=half[:, 0:1], scale=0.5).then_inc(act_x.sem, 1)

                def summed(k, slot, n):
                    act.wait_ge(pe_o.sem, pe_o.at(k + 1))
                    if not early_chunk(k):
                        for t in range(TPC):
                            act.wait_ge(lanes[t].sem, lanes[t].at(16 * (k - 1)))
                    hold(act, "act")
                    act.activation(res[:, slot, :, 0:D], tiles(ps[4 + slot][:]), ACT.Copy).then_inc(act_r.sem, 1)

                def late(k, slot, n):
                    if not first(k):
                        summed(*before(k, slot, n))
                    act.wait_ge(x_h.sem, x_h.at(k + 1))
                    hold(act, "act")
                    act.activation(f2[slot], f2[slot], ACT.Exp).then_inc(act_e.sem, 1)
                    act.wait_ge(act_e.sem, act_e.at(k + 1))
                    hold(act, "act")
                    act.activation(f2[slot], f2[slot], ACT.Ln, bias=half[:, 0:1], scale=0.5).then_inc(x_f.sem, 1)
                skewed(act, soft1, late)
                summed(C - 1, 1, C // 2 - 1)

            @block.vector
            def _(dve):
                link(dve, dve_link, dve.tensor_copy(src_f, src_i[:]))
                link(dve, dve_link, dve.tensor_scalar(away, src_f, -1.0, lane[:, 0:1], ALU.mult, ALU.add))

                link(dve, dve_link, dve.tensor_scalar(sml[:, 0, 63:64], w["b1"][:], -LOG2, None, ALU.add))

                def early(k, slot, n):
                    dve.wait_ge(pe_t.sem, pe_t.at(k + 1))
                    if not early_chunk(k):
                        dve.wait_ge(pe_s.sem, pe_s.at(k - 1))
                    hold(dve, "dve")
                    dve.tensor_scalar(f1[slot], ps[slot][:], w["b1"][:, 0:1], 40.0, ALU.add, ALU.min)\
                       .then_inc(x_g.sem, 1)
                    wait_loads(dve, slot, n, 2)
                    if not early_chunk(k):
                        dve.wait_ge(pe_o.sem, pe_o.at(k - 1))
                    if not first(k):
                        dve.wait_ge(x_d.sem, x_d.at(k))
                    hold(dve, "dve")
                    dve.tensor_tensor(tiles(eqs[slot]), tiles(srow[slot]),
                                      src_i[:, bass.ds(k * TPC, TPC)].unsqueeze(2).to_broadcast([P, TPC, P]),
                                      ALU.is_equal).then_inc(x_a.sem, 1)
                    dve.wait_ge(x_a.sem, x_a.at(k + 1))
                    hold(dve, "dve")
                    dve.tensor_tensor(tiles(eqb), tiles(eqs[slot]), below[:].unsqueeze(1).to_broadcast([P, TPC, P]),
                                      ALU.mult).then_inc(x_c.sem, 1)
                    dve.wait_ge(x_c.sem, x_c.at(4 * k + 1))
                    hold(dve, "dve")
                    dve.tensor_reduce(sml[:, slot, 0:TPC], tiles(eqb), AX, ALU.max).then_inc(x_c.sem, 1)
                    dve.wait_ge(x_c.sem, x_c.at(4 * k + 2))
                    hold(dve, "dve")
                    dve.tensor_tensor(sml[:, slot, 8:8 + TPC], sml[:, slot, 0:TPC], away[:, bass.ds(k * TPC, TPC)],
                                      ALU.mult).then_inc(x_c.sem, 1)
                    dve.wait_ge(x_c.sem, x_c.at(4 * k + 3))
                    hold(dve, "dve")
                    dve.tensor_tensor(sml[:, slot, 16:16 + TPC], sml[:, slot, 8:8 + TPC],
                                      src_f[:, bass.ds(k * TPC, TPC)], ALU.add).then_inc(x_c.sem, 1)
                    dve.wait_ge(x_c.sem, x_c.at(4 * k + 4))
                    if not early_chunk(k):
                        for t in range(TPC):
                            dve.wait_ge(lanes[t].sem, lanes[t].at(16 * (k - 1)))
                    hold(dve, "dve")
                    dve.tensor_copy(sidx[:, slot, :], sml[:, slot, 16:16 + TPC]).then_inc(x_d.sem, 1)
                    dve.wait_ge(act_x.sem, act_x.at(k + 1))
                    hold(dve, "dve")
                    dve.scalar_tensor_tensor(out=f1[slot], in0=ps[slot][:], scalar=sml[:, 0, 63:64], in1=f1[slot],
                                             op0=ALU.add, op1=ALU.max).then_inc(x_e.sem, 1)

                def late(k, slot, n):
                    dve.wait_ge(pe_s.sem, pe_s.at(k + 1))
                    hold(dve, "dve")
                    dve.tensor_scalar(f2[slot], ps[2 + slot][:], 40.0, None, ALU.min).then_inc(x_h.sem, 1)
                    message(k, slot, n)

                def message(k, slot, n):
                    dve.wait_ge(x_f.sem, x_f.at(k + 1))
                    if not early_chunk(k):
                        dve.wait_ge(pe_o.sem, pe_o.at(k - 1))
                    hold(dve, "dve")
                    dve.scalar_tensor_tensor(out=msg[slot], in0=ps[2 + slot][:], scalar=-LOG2, in1=f2[slot],
                                             op0=ALU.add, op1=ALU.max).then_inc(x_i.sem, 1)
                    dve.wait_ge(x_i.sem, x_i.at(k + 1))
                    wait_got(dve, slot, n)
                    hold(dve, "dve")
                    dve.tensor_tensor(tiles(msg[slot]), tiles(msg[slot]), gat[:, slot, :, 0:D], ALU.mult)\
                       .then_inc(x_b.sem, 1)
                skewed(dve, early, late)
        gathered()
        chunkwise(pe_t, pe_s, pe_o, x_a, x_b, x_d, x_e, x_f, x_g, x_h, x_i, act_x, act_q, act_e, act_r)
        chunkwise(x_c, per=4)
        chunkwise(*ld, per=16)
        chunkwise(*lanes, per=16)

        node_pass(None, None, [out], lanes_in=t_acc)


def kernel(**inputs):
    import numpy as np
    import concourse.bacc as bacc
    from concourse.bass_utils import run_bass_kernel_spmd

    f32 = np.float32
    g = {k: np.asarray(v) for k, v in inputs.items()}
    pad = NP - N

    def edges(v, fill):
        return np.concatenate([v, np.full((pad,) + v.shape[1:], fill, v.dtype)])

    def by_tile(v):
        return np.ascontiguousarray(v.reshape(TILES, P).T)

    src = edges(g["src"], NP)
    dst = edges(g["dst"], NP - 1)
    x = np.zeros((ROWS, D), f32)
    x[:N] = g["x"]
    up0, up1 = g["L2_gnn_W_up0"], g["L2_gnn_W_up1"]
    o0, o1 = g["L2_gnn_W_out0"], g["L2_gnn_W_out1"]
    w_ss, w_vv, w_dot = (np.zeros((D, D), f32) for _ in range(3))
    w_outA, w_outB = np.zeros((D, D), f32), np.zeros((D, D), f32)
    w_outA[0:32, 0:32], w_outB[0:32, 0:32] = o0[0:32], o0[32:64]
    for c in range(4):
        w_ss[0:32, 32 * c:32 * c + 32] = up0
    for c in range(3):
        b = 32 * (c + 1)
        w_vv[32 + c:D:3, b:b + 32] = up1
        w_outA[b:b + 32, 32 + c:D:3] = o1[0:32]
        w_outB[b:b + 32, 32 + c:D:3] = o1[32:64]
        w_dot[np.arange(b, b + 32), np.arange(32)] = 3.0 ** -0.5
    w2, b2 = g["L2_gnn_mlp_w2"], g["L2_gnn_mlp_b2"]
    colA = np.concatenate([np.arange(0, 32)] + 3 * [np.arange(32, 64)])
    colB = np.concatenate([np.arange(96, 128)] + 3 * [np.arange(64, 96)])
    arrays = {
        "x": x, "src": by_tile(src), "dst": by_tile(dst),
        "dst_next": by_tile(np.concatenate([dst[1:], np.full(1, -1, dst.dtype)])),
        "dst_row": np.concatenate([np.full(1, -1, dst.dtype), dst]), "src_row": src,
        "weight": edges(g["edge_weight"], 0), "radius": edges(g["edge_weight"], 0).reshape(16, NP // 16),
        "edge_vec": np.ascontiguousarray(edges(g["edge_attr_3"], 0).reshape(P, TILES, 3).transpose(0, 2, 1)),
        "edge_attr": np.ascontiguousarray(edges(g["edge_attr_64"], 0).T),
        "pool_wT": np.ascontiguousarray(g["L0_gnn_pool_w"].T), "lin_wT": np.ascontiguousarray(g["L0_gnn_lin_w"].T),
        "pool_b": g["L0_gnn_pool_b"][:, None], "lin1_w": g["L1_gnn_lin1_w"],
        "bias_rows": np.concatenate([g["L0_gnn_lin_b"][None], g["L0_gnn_bias"][None], g["L1_gnn_bs"]]),
        "rows": np.concatenate([g["L1_gnn_bs"], g["L1_gnn_lin1_b"][None], g["L3_gnn_b2"][None]]),
        "gcn_w": g["L1_gnn_Ws"], "bsT": np.ascontiguousarray(g["L1_gnn_bs"].T),
        "gamT": np.ascontiguousarray(g["L1_gnn_gammas"].T), "betT": np.ascontiguousarray(g["L1_gnn_betas"].T),
        "w_ss": w_ss, "w_vv": w_vv, "w_dot": w_dot, "w_outA": w_outA, "w_outB": w_outB,
        "mlp_w0": g["L2_gnn_mlp_w0"], "mlp_w1": g["L2_gnn_mlp_w1"],
        "mlp_w2A": np.ascontiguousarray(w2[:, colA]), "mlp_w2B": np.ascontiguousarray(w2[:, colB]),
        "mlp_b0": g["L2_gnn_mlp_b0"][:, None], "mlp_b1": g["L2_gnn_mlp_b1"][:, None],
        "mlp_b2A": b2[colA][:, None], "mlp_b2B": b2[colB][:, None],
        "W1": g["L3_gnn_W1"], "W2": g["L3_gnn_W2"], "b1": g["L3_gnn_b1"][:, None],
        "centre": np.repeat(np.arange(8, dtype=f32) / f32(7), 16)[:, None],
    }
    nc = bacc.Bacc("TRN2", target_bir_lowering=False, num_devices=1)
    feed, a = {}, {}
    for name, v in arrays.items():
        feed["in_" + name] = np.ascontiguousarray(v)
        a[name] = nc.dram_tensor("in_" + name, v.shape, mybir.dt.from_np(v.dtype), kind="ExternalInput").ap()
    out = nc.dram_tensor("out_x", (NP, D), F32, kind="ExternalOutput").ap()
    build(nc, a, out)
    r = run_bass_kernel_spmd(nc, [feed], core_ids=[0])
    return r.results[0]["out_x"][:N]
```

```python
from contextlib import ExitStack

import concourse.bass as bass
from concourse import mybir

P = 128
D = 128
N = 50000
TILES = 392
NP = TILES * P
TPC = 4
CW = TPC * P
C = TILES // TPC
ROWS = NP + 2 * P
EXT = D + 2
LANES = 2
HUGE = 3.0e38
EPS = 1e-5
LOG2 = 0.6931471805599453
L1 = 4

F32 = mybir.dt.float32
BF16 = mybir.dt.bfloat16
I32 = mybir.dt.int32
U8 = mybir.dt.uint8
ALU = mybir.AluOpType
ACT = mybir.ActivationFunctionType
AX = mybir.AxisListType.X


class Signal:

    def __init__(self, ctx, nc, name):
        self.sem = ctx.enter_context(nc.semaphore(name))
        self.base = 0

    def at(self, count):
        return count + self.base


RING = 4


class Chunk:

    def __init__(self, turn, lap):
        self.turn, self.lap = turn, lap
        self.k = RING * turn + lap
        self.slot = lap % 2
        self.round = RING // 2 * turn + lap // 2

    @property
    def before(self):
        return Chunk(self.turn, self.lap - 1) if self.lap else Chunk(self.turn - 1, RING - 1)


TURNS = C // RING
TAIL = [Chunk(TURNS, lap) for lap in range(C % RING)]
LAST = TAIL[-1]


def paced(eng, step):
    for lap in range(RING):
        step(Chunk(0, lap))
    with eng.Fori(1, TURNS) as i:
        for lap in range(RING):
            step(Chunk(i, lap))
    for c in TAIL:
        step(c)


def skewed(eng, early, late):
    early(Chunk(0, 0))
    for lap in range(1, RING):
        early(Chunk(0, lap))
        late(Chunk(0, lap - 1))
    with eng.Fori(1, TURNS) as i:
        for lap in range(RING):
            early(Chunk(i, lap))
            late(Chunk(i, lap).before)
    for c in TAIL:
        early(c)
        late(c.before)
    late(LAST)


def early_chunk(k, ring=2):
    return isinstance(k, int) and k < ring


def rows_of(table, k, width=D):
    return table[bass.ds(k * CW, CW), 0:width].rearrange("(t p) d -> p t d", p=P)


def build(nc, a, out):
    with ExitStack() as ctx:
        def sb(name, shape, dt=F32):
            return ctx.enter_context(nc.sbuf_tensor(name, shape, dt))

        def dram(name, shape, dt=F32):
            return nc.dram_tensor(name, shape, dt).ap()

        def signal(name):
            return Signal(ctx, nc, name)

        t_agg = dram("t_agg", [ROWS, D])
        t_h = [dram(f"t_h{i}", [ROWS, D]) for i in range(L1)]
        t_x1e = dram("t_x1e", [ROWS, EXT])
        t_x2 = dram("t_x2", [ROWS, D])
        t_x3 = dram("t_x3", [ROWS, D])
        t_acc = [dram(f"t_acc{i}", [ROWS, D]) for i in range(LANES)]
        r_ns = dram("r_ns", [TILES, P])
        r_sq = dram("r_sq", [9, NP], BF16)
        r_mask = dram("r_mask", [NP], U8)
        r_lin = dram("r_lin", [2, NP])
        r_h2 = dram("r_h2", [64, NP])
        r_y = dram("r_y", [4, NP])
        r_emb = dram("r_emb", [8, NP])

        mask = sb("mask", [P, NP], U8)
        src_i = sb("src_i", [P, TILES], I32)
        dst_i = sb("dst_i", [P, TILES], I32)
        pos_i = sb("pos_i", [P, TILES], I32)
        endp_i = sb("endp_i", [P, TILES], I32)
        endp_f = sb("endp_f", [P, TILES])
        nsrc = sb("nsrc", [P, TILES])
        ndst = sb("ndst", [P, TILES])
        ends = sb("ends", [P, TILES])
        ident = sb("ident", [P, P])
        below = sb("below", [P, P])
        above = sb("above", [P, P])
        ones = sb("ones", [P, P])
        epsc = sb("epsc", [P, 1])
        lane = sb("lane", [P, 1])
        half = sb("half", [P, 1])
        zer = sb("zer", [P, CW])
        one = sb("one", [1, CW])
        w = {}
        for name, shape in (("pool_wT", [D, D]), ("lin_wT", [D, D]), ("lin1_w", [D, D]), ("w_ss", [D, D]),
                            ("w_vv", [D, D]), ("w_outA", [D, D]), ("w_outB", [D, D]), ("w_dot", [D, D]),
                            ("mlp_w0", [8, 64]), ("mlp_w1", [64, 64]), ("mlp_w2A", [64, D]),
                            ("mlp_w2B", [64, D]), ("W1", [64, D]), ("W2", [D, D]),
                            ("pool_b", [D, 1]), ("bsT", [D, L1]), ("gamT", [D, L1]), ("betT", [D, L1]),
                            ("mlp_b0", [64, 1]), ("mlp_b1", [64, 1]), ("mlp_b2A", [D, 1]), ("mlp_b2B", [D, 1]),
                            ("b1", [D, 1]), ("centre", [P, 1]), ("third", [9, 3]), ("leads", [9, P])):
            w[name] = sb("w_" + name, shape)
        gcn_w = sb("gcn_w", [D, L1, D])
        bias9 = sb("bias9", [9, L1 + 3, D], BF16)
        ones9 = sb("ones9", [9, P], BF16)
        sq9 = sb("sq9", [9, 2, CW], BF16)
        esrc_i = sb("esrc_i", [P, TILES], I32)
        h2s = sb("h2s", [64, 2, CW])
        bcast = sb("bcast", [P, 2 + L1, D])
        czero = sb("czero", [P, L1, D])
        aff = sb("aff", [P, L1, 2])
        gat = sb("gat", [P, RING, TPC, EXT])
        idx = sb("idx", [P, RING, TPC], I32)
        xin = sb("xin", [P, 2, CW])
        brd = sb("brd", [P, 2, CW])
        sca = sb("sca", [P, 2, CW])
        tmp = sb("tmp", [P, 2, CW])
        res = sb("res", [P, 2, TPC, EXT])
        dev = sb("dev", [P, 2, 2, CW])
        sml = sb("sml", [P, 2, 64])
        scn = sb("scn", [P, 2, CW])
        row1 = sb("row1", [1, 2, CW])
        nst = sb("nst", [TPC, 2, P])
        embs = sb("embs", [8, 2, CW])
        att = sb("att", [64, 2, CW])
        sidx = sb("sidx", [P, 2, TPC], I32)
        lrg = sb("lrg", [P, 5 * 2048])

        ps = [ctx.enter_context(nc.psum_tensor(f"ps{i}", [P, CW], F32)) for i in range(8)]

        loaded = signal("loaded")
        got = [signal(f"got{i}") for i in range(RING)]
        idx_ready = signal("idx_ready")
        ld = [signal(f"ld{i}") for i in range(2)]
        stored = [signal(f"stored{i}") for i in range(2)]
        pool_link = signal("pool_link")
        dve_link = signal("dve_link")
        act_link = signal("act_link")
        pe_t = signal("pe_t")
        pe_o = signal("pe_o")
        pe_s = signal("pe_s")
        act_x = signal("act_x")
        act_r = signal("act_r")
        dve_s = signal("dve_s")
        dve_d = signal("dve_d")
        act_q = signal("act_q")
        x_a = signal("x_a")
        x_b = signal("x_b")
        x_c = signal("x_c")
        x_d = signal("x_d")
        x_e = signal("x_e")
        x_f = signal("x_f")
        zeroed = signal("zeroed")
        act_e = signal("act_e")
        x_g = signal("x_g")
        x_h = signal("x_h")
        x_i = signal("x_i")
        x_j = signal("x_j")
        lanes = [signal(f"lane{i}") for i in range(LANES)]
        turn = {e: ctx.enter_context(nc.semaphore(f"turn_{e}")) for e in ("pool", "dve", "act", "pe", "sp")}

        def chunkwise(*signals, per=1):
            for s in signals:
                s.base += per * C

        def link(eng, sig, ins):
            ins.then_inc(sig.sem, 1)
            sig.base += 1
            eng.wait_ge(sig.sem, sig.base)


        def hold(eng, name):
            eng.sem_inc(turn[name], 1)

        def first(k):
            return isinstance(k, int) and k == 0

        def pool_ready(pool, c, index, freed, per=1):
            if not early_chunk(c.k, RING):
                pool.wait_ge(freed.sem, freed.at(per * (c.k - RING + 1)))
                hold(pool, "pool")
            pool.tensor_copy(idx[:, c.lap, :], index[:, bass.ds(c.k * TPC, TPC)]).then_inc(idx_ready.sem, 1)
            pool.wait_ge(idx_ready.sem, idx_ready.at(c.k + 1))
            hold(pool, "pool")

        def gather_tile(pool, c, t, table, width):
            pool.indirect_dma_start(gat[:, c.lap, t, 0:width], None, table,
                                    bass.IndirectOffsetOnAxis(ap=idx[:, c.lap, t:t + 1], axis=0))\
                .then_inc(got[c.lap].sem, 16)

        def pool_gather(pool, c, table, index, width, freed, per=1):
            pool_ready(pool, c, index, freed, per)
            for t in range(TPC):
                gather_tile(pool, c, t, table[0:NP + (index is src_i), :], width)

        def gathered():
            idx_ready.base += C
            for lap in range(RING):
                got[lap].base += 16 * TPC * (TURNS + (lap < C % RING))

        def wait_got(eng, c):
            eng.wait_ge(got[c.lap].sem, got[c.lap].at(16 * TPC * c.turn + 16 * TPC))

        def wait_loads(eng, slot, n, each):
            eng.wait_ge(ld[slot].sem, ld[slot].at(16 * each * n + 16 * each))

        def tiles(ap):
            return ap.rearrange("p (t d) -> p t d", t=TPC)

        with nc.Block() as block:
            @block.gpsimd
            def _(pool):
                for m, v in ((ones, 1.0), (ident, 0.0), (below, 0.0), (above, 0.0), (epsc, EPS), (zer, 0.0), (one, 1.0), (half, 0.5)):
                    pool.memset(m[:], v).then_inc(pool_link.sem, 1)
                pool.iota(idx[:, 0, 0:1], [[0, 1]], base=NP + 1, channel_multiplier=1).then_inc(pool_link.sem, 1)
                pool.wait_ge(pool_link.sem, 9)
                for m, op, step, mult in ((ident, ALU.not_equal, -1, 1), (below, ALU.is_ge, 1, -1),
                                          (above, ALU.is_ge, -1, 1)):
                    pool.affine_select(out=m[:], in_=m[:], compare_op=op, fill=1.0, base=0,
                                       pattern=[[step, P]], channel_multiplier=mult).then_inc(pool_link.sem, 1)
                pool.tensor_copy(lane[:], idx[:, 0, 0:1]).then_inc(pool_link.sem, 1)
                pool.wait_ge(pool_link.sem, 13)

            @block.sync
            def _(sp):
                n = 0
                for name, t in w.items():
                    sp.dma_start(t[:], a[name]).then_inc(loaded.sem, 16)
                    n += 1
                for t, s in ((gcn_w[:], a["gcn_w"].rearrange("l i o -> i l o")),
                             (bcast[:], a["bias_rows"].partition_broadcast(P)),
                             (dst_i[:], a["dst"]), (esrc_i[:], a["src"])):
                    sp.dma_start(t, s).then_inc(loaded.sem, 16)
                    n += 1
                sp.wait_ge(loaded.sem, 16 * n)
                sp.wait_ge(pool_link.sem, 8)
                for table, width in ((t_x1e, EXT), (t_x2, D)):
                    sp.dma_start(table[NP:NP + 1, :], zer[0:1, 0:width]).then_inc(loaded.sem, 16)
                    n += 1
                sp.wait_ge(loaded.sem, 16 * n)
        pool_link.base = 13
        loaded.base = 16 * (len(w) + 6)

        cur, prv, nxt = (lrg[:, i * TILES:(i + 1) * TILES].bitcast(I32) for i in range(3))
        m_f, c_f, q_f, s_f, e_f, o_f, z_f = (lrg[:, i * TILES:(i + 1) * TILES] for i in range(3, 10))
        m_u = lrg[:, 10 * TILES:10 * TILES + TILES // 4].bitcast(U8)
        part = [lrg[:, 11 * TILES + i * TILES // 2:11 * TILES + (i + 1) * TILES // 2].bitcast(BF16) for i in range(3)]
        crow = row1[0:1, 0, :]
        blocks = lrg[:, 13 * TILES:13 * TILES + 12 * P].rearrange("p (q b v) -> p q b v", q=3, b=4)
        b9, b9r = (lrg[0:9, 17 * TILES + i * 1024:17 * TILES + i * 1024 + 7 * D] for i in range(2))
        b9p = lrg[0:9, 17 * TILES + 2048:17 * TILES + 2048 + 7 * D // 2].bitcast(BF16)

        def linear(row):
            return row.rearrange("(p t) -> p t", p=P)
        l_base, s_base = loaded.base, stored[0].base
        with nc.Block() as block:
            @block.sync
            def _(sp):
                sp.dma_start(cur, linear(a["dst_row"][1:NP + 1])).then_inc(loaded.sem, 16)
                sp.dma_start(prv, linear(a["dst_row"][0:NP])).then_inc(loaded.sem, 16)
                sp.dma_start(nxt, linear(a["dst_row"][2:NP + 2])).then_inc(loaded.sem, 16)
                sp.dma_start(b9, a["rows"].rearrange("r d -> (r d)").partition_broadcast(9)).then_inc(loaded.sem, 16)
                sp.wait_ge(x_a.sem, 1)
                sp.dma_start(linear(r_mask), m_u).then_inc(stored[0].sem, 16)
                sp.wait_ge(stored[0].sem, s_base + 16)
                sp.dma_start(mask[:], r_mask.partition_broadcast(P)).then_inc(loaded.sem, 16)
                sp.wait_ge(x_a.sem, 3)
                sp.dma_start(linear(r_lin[0]), s_f).then_inc(stored[0].sem, 16)
                sp.dma_start(linear(r_lin[1]), e_f).then_inc(stored[0].sem, 16)
                sp.wait_ge(x_a.sem, 4)
                for r in range(9):
                    sp.dma_start(linear(r_sq[r]), part[r // 3]).then_inc(stored[0].sem, 16)
                sp.wait_ge(stored[0].sem, s_base + 16 * 12)
                sources = (r_lin[0], r_lin[1], a["src_row"])
                for q in range(3):
                    by_rows = sources[q].rearrange("(t p) -> t p", p=P)
                    target = blocks[:, q, :, :] if q < 2 else blocks[:, q, :, :].bitcast(I32)
                    sp.dma_start(target[:, 0:3, :], by_rows[0:384, :].rearrange("(b t) p -> t b p", b=3))\
                      .then_inc(loaded.sem, 16)
                    sp.dma_start(target[0:8, 3, :], by_rows[384:392, :]).then_inc(loaded.sem, 16)
                sp.wait_ge(loaded.sem, l_base + 16 * 11)

            @block.vector
            def _(dve):
                dve.wait_ge(loaded.sem, l_base + 64)
                link(dve, dve_link, dve.tensor_tensor(m_f, cur, prv, ALU.is_equal))
                link(dve, x_a, dve.tensor_copy(m_u, m_f))
                link(dve, dve_link, dve.memset(o_f, 1.0))
                link(dve, dve_link, dve.memset(z_f, 0.0))
                link(dve, dve_link, dve.tensor_tensor_scan(c_f, m_f, o_f, 0.0, ALU.mult, ALU.add))
                link(dve, dve_link, dve.tensor_tensor_scan(q_f, m_f, z_f, 1.0, ALU.mult, ALU.add))
                link(dve, dve_link, dve.tensor_copy(sml[:, 0, 0:1], c_f[:, TILES - 1:TILES]))
                link(dve, x_b, dve.tensor_copy(sml[:, 0, 1:2], q_f[:, TILES - 1:TILES]))
                dve.wait_ge(pe_t.sem, 1)
                link(dve, dve_link, dve.tensor_copy(crow[:, 0:256], ps[0][0:1, 0:256]))
                link(dve, dve_link, dve.memset(crow[:, 256:257], 0.0))
                link(dve, x_b, dve.tensor_tensor_scan(crow[:, 257:385], crow[:, 128:256], crow[:, 0:128], 0.0,
                                                      ALU.mult, ALU.add))
                dve.wait_ge(pe_t.sem, 2)
                link(dve, dve_link, dve.tensor_copy(sml[:, 0, 2:3], ps[1][:, 0:1]))
                link(dve, x_b, dve.scalar_tensor_tensor(out=c_f, in0=q_f, scalar=sml[:, 0, 2:3], in1=c_f,
                                                        op0=ALU.mult, op1=ALU.add))
                link(dve, dve_link, dve.tensor_tensor(e_f, cur, nxt, ALU.not_equal))
                link(dve, dve_link, dve.tensor_scalar(z_f, cur, float(N), None, ALU.is_lt))
                link(dve, x_a, dve.tensor_tensor(e_f, e_f, z_f, ALU.mult))
                dve.wait_ge(act_link.sem, 1)
                link(dve, x_a, dve.reciprocal(s_f, c_f))
                link(dve, dve_link, dve.tensor_copy(part[0], c_f))
                link(dve, dve_link, dve.tensor_tensor(c_f, c_f, part[0], ALU.subtract))
                link(dve, dve_link, dve.tensor_copy(part[1], c_f))
                link(dve, dve_link, dve.tensor_tensor(c_f, c_f, part[1], ALU.subtract))
                link(dve, x_a, dve.tensor_copy(part[2], c_f))
                link(dve, dve_link, dve.tensor_tensor(b9[:, 6 * D:7 * D], b9[:, 6 * D:7 * D], bcast[0:9, 1, :], ALU.add))
                for j in range(3):
                    link(dve, dve_link, dve.tensor_copy(b9p, b9))
                    link(dve, dve_link, dve.tensor_tensor(b9, b9, b9p, ALU.subtract))
                    sel = w["third"][:, j:j + 1]
                    if j == 0:
                        link(dve, dve_link, dve.tensor_scalar(b9r, b9p, sel, None, ALU.mult))
                    else:
                        link(dve, dve_link, dve.scalar_tensor_tensor(out=b9r, in0=b9p, scalar=sel, in1=b9r,
                                                                     op0=ALU.mult, op1=ALU.add))
                link(dve, dve_link, dve.tensor_copy(bias9[:], b9r.rearrange("p (r d) -> p r d", d=D)))
                link(dve, dve_link, dve.tensor_copy(ones9[:], w["leads"][:]))
                link(dve, dve_link, dve.tensor_scalar(czero[:], bcast[:, 2:2 + L1, :], 0.0, None, ALU.max))
                dve.wait_ge(loaded.sem, l_base + 16 * 11)
                link(dve, dve_link, dve.tensor_copy(blocks[:, 2, 0:3, :], blocks[:, 2, 0:3, :].bitcast(I32)))
                link(dve, x_b, dve.tensor_copy(blocks[0:8, 2, 3, :], blocks[0:8, 2, 3, :].bitcast(I32)))
                dve.wait_ge(pe_t.sem, 3)
                for q, t in enumerate((ndst, ends, src_i)):
                    link(dve, dve_link, dve.tensor_copy(t[:], ps[2 + q][:, 0:TILES]))

            @block.scalar
            def _(act):
                act.wait_ge(x_b.sem, 3)
                act.activation(c_f, c_f, ACT.Sqrt).then_inc(act_link.sem, 1)

            @block.tensor
            def _(pe):
                pe.wait_ge(x_b.sem, 1)
                for q in range(2):
                    mm = pe.matmul(ps[0][0:1, q * P:(q + 1) * P], sml[:, 0, q:q + 1], ident[:], start=True, stop=True)
                mm.then_inc(pe_t.sem, 1)
                pe.wait_ge(x_b.sem, 2)
                pe.matmul(ps[1][:, 0:1], crow[:, 256:384], one[0:1, 0:1], start=True, stop=True).then_inc(pe_t.sem, 1)
                pe.wait_ge(x_b.sem, 4)
                for q in range(3):
                    for b in range(4):
                        n = P if b < 3 else 8
                        mm = pe.transpose(ps[2 + q][:, b * P:b * P + n], blocks[0:n, q, b, :], ident[0:n, 0:n])
                mm.then_inc(pe_t.sem, 1)
        loaded.base += 16 * 11
        stored[0].base += 16 * 12
        act_link.base = 1
        pe_t.base = 3

        ea = lrg[:, 0:3 * TILES].rearrange("p (c t) -> p c t", c=3)
        sq = lrg[:, 3 * TILES:6 * TILES].rearrange("p (c t) -> p c t", c=3)
        yy = lrg[:, 6 * TILES:10 * TILES].rearrange("p (c t) -> p c t", c=4)
        nrm = lrg[:, 10 * TILES:11 * TILES]
        RB = NP // 16
        rad = lrg[:, 0:RB]
        wid = lrg[:, RB:2 * RB]
        inr = lrg[:, 2 * RB:3 * RB]
        y_base, l_base, q_base, s_base = x_b.base, loaded.base, act_link.base, stored[0].base
        with nc.Block() as block:
            @block.sync
            def _(sp):
                sp.dma_start(ea, a["edge_vec"]).then_inc(loaded.sem, 16)
                sp.wait_ge(x_b.sem, y_base + 2)
                sp.dma_start(r_y.rearrange("c (p t) -> p c t", p=P), yy).then_inc(stored[0].sem, 16)
                sp.wait_ge(stored[0].sem, s_base + 16)
                for c in range(8):
                    sp.dma_start(rad[16 * c:16 * c + 16, :], a["radius"]).then_inc(loaded.sem, 16)
                sp.wait_ge(x_b.sem, y_base + 4)
                sp.dma_start(r_emb.rearrange("c (s j) -> (c s) j", s=16), wid).then_inc(stored[0].sem, 16)
                sp.wait_ge(stored[0].sem, s_base + 32)

            @block.vector
            def _(dve):
                dve.wait_ge(loaded.sem, l_base + 16)
                link(dve, dve_link, dve.tensor_tensor(sq, ea, ea, ALU.mult))
                link(dve, dve_link, dve.tensor_tensor(nrm, sq[:, 0, :], sq[:, 1, :], ALU.add))
                link(dve, x_b, dve.tensor_tensor(nrm, nrm, sq[:, 2, :], ALU.add))
                dve.wait_ge(act_link.sem, q_base + 1)
                link(dve, dve_link, dve.tensor_scalar(nrm, nrm, 1e-12, None, ALU.add))
                link(dve, dve_link, dve.reciprocal(nrm, nrm))
                link(dve, dve_link, dve.memset(yy[:, 0, :], 1.0))
                for c in range(3):
                    link(dve, dve_link, dve.tensor_tensor(sq[:, c, :], ea[:, c, :], nrm, ALU.mult))
                link(dve, x_b, dve.tensor_scalar(yy[:, 1:4, :], sq, 3.0 ** 0.5, None, ALU.mult))
                dve.wait_ge(loaded.sem, l_base + 9 * 16)
                link(dve, dve_link, dve.tensor_scalar(inr, rad, 1.0, 8.0 ** 0.5, ALU.is_le, ALU.mult))
                link(dve, dve_link, dve.tensor_scalar(wid, rad, 0.0, 1.0, ALU.max, ALU.min))
                link(dve, x_b, dve.tensor_scalar(wid, wid, w["centre"][:, 0:1], 7.0, ALU.subtract, ALU.mult))
                dve.wait_ge(act_link.sem, q_base + 3)
                link(dve, x_b, dve.tensor_tensor(wid, wid, inr, ALU.mult))

            @block.scalar
            def _(act):
                act.wait_ge(x_b.sem, y_base + 1)
                act.activation(nrm, nrm, ACT.Sqrt).then_inc(act_link.sem, 1)
                act.wait_ge(x_b.sem, y_base + 3)
                act.activation(wid, wid, ACT.Square).then_inc(act_link.sem, 1)
                act.wait_ge(act_link.sem, q_base + 2)
                act.activation(wid, wid, ACT.Exp, scale=-0.5).then_inc(act_link.sem, 1)
        act_link.base += 3
        stored[0].base += 32
        loaded.base += 9 * 16

        hot = lrg[:, 0:4096].bitcast(BF16).rearrange("p (s t q v) -> p s t q v", s=2, t=TPC, q=4)
        iota_i = lrg[:, 4096:4352].bitcast(I32)
        iota_b = lrg[:, 4352:4480].bitcast(BF16)
        key_i = lrg[:, 4480:4480 + 4 * TILES].bitcast(I32).rearrange("p (q t) -> p q t", q=4)
        key_f = lrg[:, 6048:6048 + 4 * TILES].rearrange("p (q t) -> p q t", q=4)
        work = lrg[:, 0:5 * 512].rearrange("p (q v) -> p q v", q=5)
        x_base, l_base, h_base, i_base, k_base = x_h.base, act_link.base, pe_s.base, pool_link.base, loaded.base
        neg = [lrg[:, 9216 + CW * s:9216 + CW * (s + 1)] for s in range(2)]
        with nc.Block() as block:
            @block.gpsimd
            def _(pool):
                pool.iota(iota_i, [[1, 256]], base=0, channel_multiplier=0).then_inc(pool_link.sem, 1)
                paced(pool, lambda c: pool_gather(pool, c, a["x"], src_i, D, pe_t))

            @block.sync
            def _(sp):
                def load(c):
                    k, slot, n = c.k, c.slot, c.round
                    if not early_chunk(k):
                        sp.wait_ge(x_b.sem, x_b.at(k - 1))
                        hold(sp, "sp")
                    sp.dma_start(brd[:, slot, :], a["weight"][bass.ds(k * CW, CW)].partition_broadcast(P))\
                      .then_inc(ld[slot].sem, 16)

                sp.dma_start(key_i[:, 0, :], linear(a["src_row"])).then_inc(loaded.sem, 16)
                sp.dma_start(key_i[:, 2, :], linear(a["dst_row"][1:NP + 1])).then_inc(loaded.sem, 16)
                paced(sp, load)

            @block.tensor
            def _(pe):
                for b in (6, 7):
                    pe.matmul(ps[b][:], zer[0:1, 0:P], zer[0:1, :], start=True, stop=False, skip_group_check=True)

                def turn_rows(c):
                    k, slot, n = c.k, c.slot, c.round
                    wait_got(pe, c)
                    if not early_chunk(k):
                        pe.wait_ge(act_x.sem, act_x.at(k - 1))
                    hold(pe, "pe")
                    for t in range(TPC):
                        mm = pe.transpose(ps[slot][:, t * P:(t + 1) * P], gat[:, c.lap, t, 0:D], ident[:])
                    mm.then_inc(pe_t.sem, 1)

                def out_rows(c):
                    k, slot, n = c.k, c.slot, c.round
                    pe.wait_ge(dve_s.sem, dve_s.at(k + 1))
                    if not early_chunk(k):
                        pe.wait_ge(act_r.sem, act_r.at(k - 1))
                    hold(pe, "pe")
                    for t in range(TPC):
                        pe.matmul(ps[4 + slot][:, t * P:(t + 1) * P], scn[:, slot, t * P:(t + 1) * P],
                                  w["lin_wT"][:], start=True, stop=False)
                        mm = pe.matmul(ps[4 + slot][:, t * P:(t + 1) * P], ones9[:], bias9[:, L1 + 2, :],
                                       start=False, stop=True)
                    mm.then_inc(pe_o.sem, 1)

                def late(c):
                    k, slot, n = c.k, c.slot, c.round
                    pe.wait_ge(act_x.sem, act_x.at(k + 1))
                    if not early_chunk(k):
                        pe.wait_ge(act_q.sem, act_q.at(k - 1))
                    hold(pe, "pe")
                    pe.matmul(ps[2 + slot][:], w["pool_wT"][:], xin[:, slot, :], start=True, stop=True)\
                      .then_inc(x_a.sem, 1)
                    pe.wait_ge(x_i.sem, x_i.at(16 * k + 16))
                    hold(pe, "pe")
                    for t in range(TPC):
                        for q in range(2):
                            for h in range(2):
                                mm = pe.matmul(ps[6 + q][:, h * 256:(h + 1) * 256],
                                               hot[:, slot, t, 2 * q, h * P:(h + 1) * P],
                                               hot[:, slot, t, 2 * q + 1, :], start=False, stop=False,
                                               skip_group_check=True)
                    mm.then_inc(x_g.sem, 1)
                    if not first(k):
                        out_rows(c.before)
                skewed(pe, turn_rows, late)
                out_rows(LAST)
                pe.wait_ge(x_h.sem, x_base + 1)
                pe.matmul(ps[3][:, 0:2], above[:], sml[:, 0, 0:2], start=True, stop=False, skip_group_check=True)
                pe.matmul(ps[3][:, 1:2], ones[:], sml[:, 0, 0:1], start=False, stop=True,
                          skip_group_check=True).then_inc(pe_s.sem, 1)
                pe.wait_ge(x_h.sem, x_base + 2)
                pe.wait_ge(act_r.sem, act_r.at(C))
                for q, r in ((0, 0), (1, 2)):
                    for b in range(4):
                        mm = pe.transpose(ps[4 + q][:, b * P:(b + 1) * P], work[:, r, b * P:(b + 1) * P], ident[:])
                mm.then_inc(pe_s.sem, 1)

            @block.scalar
            def _(act):
                def evacuate(c):
                    k, slot, n = c.k, c.slot, c.round
                    act.wait_ge(pe_t.sem, pe_t.at(k + 1))
                    if not early_chunk(k):
                        act.wait_ge(x_a.sem, x_a.at(k - 1))
                    hold(act, "act")
                    act.activation(xin[:, slot, :], ps[slot][:], ACT.Copy).then_inc(act_x.sem, 1)

                def pooled(c):
                    k, slot, n = c.k, c.slot, c.round
                    act.wait_ge(x_a.sem, x_a.at(k + 1))
                    if not early_chunk(k):
                        act.wait_ge(x_b.sem, x_b.at(k - 1))
                    hold(act, "act")
                    act.activation(sca[:, slot, :], ps[2 + slot][:], ACT.Relu, bias=w["pool_b"][:, 0:1])\
                       .then_inc(act_q.sem, 1)

                def finish(c):
                    k, slot, n = c.k, c.slot, c.round
                    act.wait_ge(pe_o.sem, pe_o.at(k + 1))
                    if not early_chunk(k):
                        act.wait_ge(stored[slot].sem, stored[slot].at(16 * n))
                    hold(act, "act")
                    act.activation(res[:, slot, :, 0:D], tiles(ps[4 + slot][:]), ACT.Copy).then_inc(act_r.sem, 1)
                    act.wait_ge(act_r.sem, act_r.at(k + 1))
                    hold(act, "act")
                    act.dma_start(rows_of(t_agg, k), res[:, slot, :, 0:D]).then_inc(stored[slot].sem, 16)

                def late(c):
                    k, slot, n = c.k, c.slot, c.round
                    if not early_chunk(k):
                        act.wait_ge(dve_s.sem, dve_s.at(k - 1))
                        hold(act, "act")
                    act.activation(neg[slot], mask[:, bass.ds(k * CW, CW)], ACT.Copy, bias=-HUGE, scale=HUGE)\
                       .then_inc(x_c.sem, 1)
                    pooled(c)
                    if not first(k):
                        finish(c.before)
                skewed(act, evacuate, late)
                finish(LAST)
                act.wait_ge(x_h.sem, x_base + 1)
                act.activation(work[:, 0, :], work[:, 0, :], ACT.Sqrt).then_inc(act_link.sem, 1)
                for s in range(2):
                    act.wait_ge(stored[s].sem, stored[s].at(8 * C))

            @block.vector
            def _(dve):
                dve.wait_ge(loaded.sem, k_base + 32)
                for q in (0, 2):
                    link(dve, dve_link, dve.tensor_scalar(key_i[:, q + 1, :], key_i[:, q, :], 255, None,
                                                          ALU.bitwise_and))
                    link(dve, dve_link, dve.tensor_scalar(key_i[:, q, :], key_i[:, q, :], 8, None,
                                                          ALU.arith_shift_right))
                link(dve, dve_link, dve.tensor_copy(key_f[:], key_i[:]))
                dve.wait_ge(pool_link.sem, i_base + 1)
                link(dve, dve_link, dve.tensor_copy(iota_b, iota_i))

                def scan(c):
                    k, slot, n = c.k, c.slot, c.round
                    wait_loads(dve, slot, n, 1)
                    dve.wait_ge(act_q.sem, act_q.at(k + 1))
                    if not first(k):
                        dve.wait_ge(dve_s.sem, dve_s.at(k))
                    hold(dve, "dve")
                    dve.tensor_tensor(tmp[:, 0, :], sca[:, slot, :], brd[:, slot, :], ALU.mult).then_inc(x_b.sem, 1)
                    dve.wait_ge(x_b.sem, x_b.at(k + 1))
                    dve.wait_ge(x_c.sem, x_c.at(k + 1))
                    if not early_chunk(k):
                        dve.wait_ge(pe_o.sem, pe_o.at(k - 1))
                    hold(dve, "dve")
                    dve.tensor_tensor_scan(scn[:, slot, :], neg[slot], tmp[:, 0, :],
                                           0.0 if first(k) else scn[:, 1 - slot, CW - 1:CW],
                                           ALU.add, ALU.max).then_inc(dve_s.sem, 1)
                    if not early_chunk(k):
                        dve.wait_ge(x_g.sem, x_g.at(k - 1))
                        hold(dve, "dve")
                    for t in range(TPC):
                        for q in range(4):
                            dve.tensor_scalar(hot[:, slot, t, q, :], iota_b, key_f[:, q, bass.ds(k * TPC + t, 1)],
                                              None, ALU.is_equal).then_inc(x_i.sem, 1)
                paced(dve, scan)
                dve.wait_ge(x_g.sem, x_g.at(C))
                cs, cd, ep, z, t5 = (work[:, i, :] for i in range(5))
                link(dve, dve_link, dve.tensor_scalar(cs, ps[6][:], 1.0, None, ALU.max))
                link(dve, dve_link, dve.tensor_copy(cd, ps[7][:]))
                link(dve, dve_link, dve.memset(t5, 1.0))
                for h in range(2):
                    link(dve, dve_link, dve.tensor_tensor_scan(
                        ep[:, h * 256:(h + 1) * 256], t5[:, 0:256], cd[:, h * 256:(h + 1) * 256], 0.0,
                        ALU.mult, ALU.add))
                link(dve, x_h, dve.tensor_copy(sml[:, 0, 0:2], ep[:, 255:512:256]))
                dve.wait_ge(pe_s.sem, h_base + 1)
                link(dve, dve_link, dve.tensor_copy(sml[:, 0, 2:4], ps[3][:, 0:2]))
                for h in range(2):
                    link(dve, dve_link, dve.tensor_scalar(ep[:, h * 256:(h + 1) * 256], ep[:, h * 256:(h + 1) * 256],
                                                          sml[:, 0, 2 + h:3 + h], -float(NP), ALU.add, ALU.add))
                link(dve, dve_link, dve.tensor_scalar(z, cd, 0.0, None, ALU.is_gt))
                link(dve, dve_link, dve.tensor_tensor(ep, ep, z, ALU.mult))
                link(dve, dve_link, dve.tensor_scalar(ep, ep, float(NP - 1), None, ALU.add))
                dve.wait_ge(act_link.sem, l_base + 1)
                link(dve, x_h, dve.reciprocal(cs, cs))
                dve.wait_ge(pe_s.sem, h_base + 2)
                for q, dest in ((0, nsrc), (1, endp_f)):
                    for h in range(2):
                        for o in range(2):
                            m = 128 if h == 0 else TILES // 2 - 128
                            link(dve, dve_link, dve.tensor_copy(
                                dest[:, h * 256 + o:h * 256 + o + 2 * m - 1:2],
                                ps[4 + q][:, (2 * h + o) * P:(2 * h + o) * P + m]))
                link(dve, dve_link, dve.tensor_copy(endp_i[:], endp_f[:]))
        gathered()
        loaded.base += 32
        pool_link.base += 1
        act_link.base += 1
        pe_s.base += 2
        chunkwise(x_g)
        chunkwise(x_i, per=16)
        chunkwise(pe_t, pe_o, x_a, x_b, x_c, act_x, act_q, act_r, dve_s)
        chunkwise(*ld, *stored, per=8)

        def node_pass(base_rows, agg, stores, extend=False, lanes_in=None):
            width = EXT if extend else D
            loads = LANES if lanes_in else 1
            wide = lrg[:, 0:2 * LANES * CW].rearrange("p (s l v) -> p s l v", s=2, l=LANES) \
                if lanes_in else None
            with nc.Block() as block:
                if not lanes_in:
                    @block.gpsimd
                    def _(pool):
                        paced(pool, lambda c: pool_gather(pool, c, agg, endp_i, D, x_a))

                @block.sync
                def _(sp):
                    def load(c):
                        k, slot, n = c.k, c.slot, c.round
                        if not early_chunk(k):
                            sp.wait_ge(x_a.sem, x_a.at(k - 1))
                            hold(sp, "sp")
                        if lanes_in:
                            for l, table in enumerate(lanes_in):
                                sp.dma_start(tiles(wide[:, slot, l, :]), rows_of(table, k)).then_inc(ld[slot].sem, 16)
                        else:
                            sp.dma_start(tiles(brd[:, slot, :]), rows_of(base_rows, k)).then_inc(ld[slot].sem, 16)

                    paced(sp, load)

                @block.vector
                def _(dve):
                    def stats(c):
                        k, slot, n = c.k, c.slot, c.round
                        wait_loads(dve, slot, n, loads)
                        if not lanes_in:
                            wait_got(dve, c)
                        if not early_chunk(k):
                            dve.wait_ge(act_r.sem, act_r.at(k - 1))
                        hold(dve, "dve")
                        if lanes_in:
                            dve.tensor_tensor(sca[:, slot, :], wide[:, slot, 0, :], wide[:, slot, 1, :], ALU.add)\
                               .then_inc(x_a.sem, 1)
                        else:
                            dve.tensor_tensor(tiles(sca[:, slot, :]), gat[:, c.lap, :, 0:D], tiles(brd[:, slot, :]),
                                              ALU.add).then_inc(x_a.sem, 1)
                        dve.wait_ge(x_a.sem, x_a.at(k + 1))
                        hold(dve, "dve")
                        for t in range(TPC):
                            dve.bn_stats(sml[:, slot, 6 * t:6 * t + 6], sca[:, slot, t * P:(t + 1) * P])\
                               .then_inc(x_e.sem, 1)
                        dve.wait_ge(x_e.sem, x_e.at(4 * k + 4))
                        hold(dve, "dve")
                        for t in range(TPC):
                            dve.bn_aggr(sml[:, slot, 24 + 2 * t:26 + 2 * t], sml[:, slot, 6 * t:6 * t + 6])\
                               .then_inc(x_b.sem, 1)

                    def scales(c):
                        k, slot, n = c.k, c.slot, c.round
                        dve.wait_ge(act_q.sem, act_q.at(k + 1))
                        hold(dve, "dve")
                        dve.reciprocal(sml[:, slot, 36:40], sml[:, slot, 32:36]).then_inc(x_f.sem, 1)
                        dve.wait_ge(x_f.sem, x_f.at(k + 1))
                        hold(dve, "dve")
                        dve.scalar_tensor_tensor(out=sml[:, slot, 40:44], in0=sml[:, slot, 24:32:2], scalar=-1.0,
                                                 in1=sml[:, slot, 36:40], op0=ALU.mult, op1=ALU.mult)\
                           .then_inc(x_c.sem, 1)
                    skewed(dve, stats, scales)

                @block.scalar
                def _(act):
                    def root(c):
                        k, slot, n = c.k, c.slot, c.round
                        act.wait_ge(x_b.sem, x_b.at(4 * k + 4))
                        hold(act, "act")
                        act.activation(sml[:, slot, 32:36], sml[:, slot, 25:32:2], ACT.Sqrt, bias=epsc[:, 0:1])\
                           .then_inc(act_q.sem, 1)

                    def normalise(c):
                        k, slot, n = c.k, c.slot, c.round
                        act.wait_ge(x_c.sem, x_c.at(k + 1))
                        if not early_chunk(k):
                            act.wait_ge(stored[slot].sem, stored[slot].at(16 * len(stores) * n))
                        hold(act, "act")
                        if extend:
                            act.activation(res[:, slot, :, D], nsrc[:, bass.ds(k * TPC, TPC)], ACT.Copy)
                            act.activation(res[:, slot, :, D + 1], endp_f[:, bass.ds(k * TPC, TPC)], ACT.Copy)
                        for t in range(TPC):
                            op = act.activation(res[:, slot, t, 0:D], sca[:, slot, t * P:(t + 1) * P], ACT.Identity,
                                                bias=sml[:, slot, 40 + t:41 + t], scale=sml[:, slot, 36 + t:37 + t])
                        op.then_inc(act_r.sem, 1)
                        act.wait_ge(act_r.sem, act_r.at(k + 1))
                        hold(act, "act")
                        for table in stores:
                            act.dma_start(rows_of(table, k, width), res[:, slot, :, 0:width])\
                               .then_inc(stored[slot].sem, 16)
                    skewed(act, root, normalise)
                    for s in range(2):
                        act.wait_ge(stored[s].sem, stored[s].at(8 * C * len(stores)))
            if not lanes_in:
                gathered()
            chunkwise(x_a, x_c, x_f, act_q, act_r)
            chunkwise(x_b, x_e, per=4)
            chunkwise(*ld, per=8 * loads)
            chunkwise(*stored, per=8 * len(stores))

        node_pass(a["x"], t_agg, [t_x1e], extend=True)

        def gcn_pass(l):
            table = t_x1e if l == 0 else t_h[l - 1]
            radial = l == 1
            loads = 1 if l == 0 else 3 if radial else 2
            acc = lrg[:, 0:2 * CW]
            saves = 2 if l == 0 or radial else 1
            freed = x_a if l == 0 else pe_t
            p_base = pe_o.base
            with nc.Block() as block:
                @block.gpsimd
                def _(pool):
                    if l == 0:
                        paced(pool, lambda c: pool_gather(pool, c, table, src_i, EXT, x_a, per=3))
                    else:
                        paced(pool, lambda c: pool_gather(pool, c, table, pos_i, D, pe_t))

                @block.sync
                def _(sp):
                    def load(c):
                        k, slot, n = c.k, c.slot, c.round
                        if not early_chunk(k):
                            sp.wait_ge(pe_o.sem, pe_o.at(k - 1))
                            hold(sp, "sp")
                            if l:
                                sp.wait_ge(x_b.sem, x_b.at(k - 1))
                                hold(sp, "sp")
                        sp.dma_start(sq9[:, slot, :], r_sq[:, bass.ds(k * CW, CW)]).then_inc(ld[slot].sem, 16)
                        if radial:
                            sp.dma_start(embs[:, slot, :], r_emb[:, bass.ds(k * CW, CW)]).then_inc(ld[slot].sem, 16)
                        if l:
                            sp.dma_start(brd[:, slot, :], r_ns.rearrange("t p -> (t p)")[bass.ds(k * CW, CW)]
                                         .partition_broadcast(P)).then_inc(ld[slot].sem, 16)

                    paced(sp, load)

                @block.tensor
                def _(pe):
                    def turn_rows(c):
                        k, slot, n = c.k, c.slot, c.round
                        if radial:
                            wait_loads(pe, slot, n, loads)
                            if not first(k):
                                pe.wait_ge(x_i.sem, x_i.at(k))
                            hold(pe, "pe")
                            pe.matmul(ps[2][0:64, :], w["mlp_w0"][:], embs[:, slot, :], start=True, stop=True)\
                              .then_inc(x_d.sem, 1)
                        if l == 0:
                            pe.wait_ge(x_a.sem, x_a.at(3 * k + 3))
                        else:
                            wait_got(pe, c)
                        if not early_chunk(k):
                            pe.wait_ge(act_x.sem, act_x.at(k - 1))
                            if l == 0:
                                pe.wait_ge(x_d.sem, x_d.at(k - 1))
                        hold(pe, "pe")
                        if l == 0:
                            pe.matmul(ps[7][0:TPC, slot * P:(slot + 1) * P], sml[:, slot, 0:TPC], ident[:],
                                      start=True, stop=True)
                        for t in range(TPC):
                            rows_in = sca[:, slot, t * P:(t + 1) * P] if l == 0 else gat[:, c.lap, t, 0:D]
                            mm = pe.transpose(ps[slot][:, t * P:(t + 1) * P], rows_in, ident[:])
                        mm.then_inc(pe_t.sem, 1)

                    def late(c):
                        k, slot, n = c.k, c.slot, c.round
                        if radial:
                            pe.wait_ge(x_i.sem, x_i.at(k + 1))
                            if not first(k):
                                pe.wait_ge(x_j.sem, x_j.at(k))
                            hold(pe, "pe")
                            pe.matmul(ps[3][0:64, :], w["mlp_w1"][:], sca[0:64, slot, :], start=True, stop=True)\
                              .then_inc(zeroed.sem, 1)
                        pe.wait_ge(dve_s.sem, dve_s.at(k + 1))
                        wait_loads(pe, slot, n, loads)
                        if not early_chunk(k):
                            pe.wait_ge(act_r.sem, act_r.at(k - 1))
                        hold(pe, "pe")
                        for t in range(TPC):
                            pe.matmul(ps[4 + slot][:, t * P:(t + 1) * P], scn[:, slot, t * P:(t + 1) * P],
                                      gcn_w[:, l, :], start=True, stop=False)
                            mm = pe.matmul(ps[4 + slot][:, t * P:(t + 1) * P], sq9[:, slot, t * P:(t + 1) * P],
                                           bias9[:, l, :], start=False, stop=True)
                        mm.then_inc(pe_o.sem, 1)
                    skewed(pe, turn_rows, late)
                    pe.wait_ge(pe_s.sem, pe_s.at(C))
                    for q in range(2):
                        for t in range(TPC):
                            mm = pe.matmul(ps[6][:, q:q + 1], acc[:, q * CW + t * P:q * CW + (t + 1) * P],
                                           ones[:, 0:1], start=(t == 0), stop=(t == TPC - 1))
                    mm.then_inc(x_f.sem, 1)

                @block.scalar
                def _(act):
                    def evacuate(c):
                        k, slot, n = c.k, c.slot, c.round
                        if radial:
                            act.wait_ge(x_d.sem, x_d.at(k + 1))
                            if not early_chunk(k):
                                act.wait_ge(zeroed.sem, zeroed.at(k - 1))
                            hold(act, "act")
                            act.activation(sca[0:64, slot, :], ps[2][0:64, :], ACT.Silu, bias=w["mlp_b0"][:, 0:1])\
                               .then_inc(x_i.sem, 1)
                        act.wait_ge(pe_t.sem, pe_t.at(k + 1))
                        if not early_chunk(k):
                            act.wait_ge((dve_s if l == 0 else x_b).sem, (dve_s if l == 0 else x_b).at(k - 1))
                            if l == 0:
                                act.wait_ge(stored[slot].sem, stored[slot].at(16 * saves * n))
                        hold(act, "act")
                        if l == 0:
                            act.activation(nst[:, slot, :], ps[7][0:TPC, slot * P:(slot + 1) * P], ACT.Copy)\
                               .then_inc(x_d.sem, 1)
                            act.wait_ge(x_d.sem, x_d.at(k + 1))
                            hold(act, "act")
                            act.dma_start(r_ns[bass.ds(k * TPC, TPC), :], nst[:, slot, :]).then_inc(stored[slot].sem, 16)
                            act.activation(xin[:, slot, :], ps[slot][:], ACT.Copy).then_inc(act_x.sem, 1)
                        else:
                            act.activation(xin[:, slot, :], ps[slot][:], ACT.Relu, bias=aff[:, l - 1, 1:2],
                                           scale=aff[:, l - 1, 0:1]).then_inc(act_x.sem, 1)

                    def square(c):
                        k, slot, n = c.k, c.slot, c.round
                        act.wait_ge(x_g.sem, x_g.at(k + 1))
                        if not early_chunk(k):
                            act.wait_ge(pe_s.sem, pe_s.at(k - 1))
                        hold(act, "act")
                        act.activation(dev[:, slot, 1, :], dev[:, slot, 0, :], ACT.Square).then_inc(act_q.sem, 1)

                    def late(c):
                        k, slot, n = c.k, c.slot, c.round
                        if not first(k):
                            square(c.before)
                        act.wait_ge(pe_o.sem, pe_o.at(k + 1))
                        if not early_chunk(k):
                            act.wait_ge(stored[slot].sem, stored[slot].at(16 * saves * n))
                            act.wait_ge(dve_d.sem, dve_d.at(k - 1))
                        hold(act, "act")
                        for t in range(TPC):
                            op = act.activation(res[:, slot, t, 0:D], ps[4 + slot][:, t * P:(t + 1) * P], ACT.Relu,
                                                scale=ndst[:, bass.ds(k * TPC + t, 1)])
                        op.then_inc(act_r.sem, 1)
                        act.wait_ge(act_r.sem, act_r.at(k + 1))
                        hold(act, "act")
                        act.dma_start(rows_of(t_h[l], k), res[:, slot, :, 0:D]).then_inc(stored[slot].sem, 16)
                        if radial:
                            act.wait_ge(zeroed.sem, zeroed.at(k + 1))
                            hold(act, "act")
                            act.activation(h2s[:, slot, :], ps[3][0:64, :], ACT.Silu, bias=w["mlp_b1"][:, 0:1])\
                               .then_inc(x_j.sem, 1)
                            act.wait_ge(x_j.sem, x_j.at(k + 1))
                            hold(act, "act")
                            act.dma_start(r_h2[:, bass.ds(k * CW, CW)], h2s[:, slot, :]).then_inc(stored[slot].sem, 16)
                    if l < LANES:
                        act.dma_start(t_acc[l][NP:ROWS, :].rearrange("(p r) d -> p (r d)", p=P), zer[:, 0:2 * D])\
                           .then_inc(loaded.sem, 16)
                    skewed(act, evacuate, late)
                    square(LAST)
                    if l < LANES:
                        act.wait_ge(loaded.sem, loaded.at(16))
                    for s in range(2):
                        act.wait_ge(stored[s].sem, stored[s].at(8 * saves * C))
                    act.wait_ge(x_e.sem, x_e.at(1))
                    act.activation(sml[:, 1, 4:5], sml[:, 1, 3:4], ACT.Sqrt, bias=epsc[:, 0:1])\
                       .then_inc(act_link.sem, 1)

                @block.vector
                def _(dve):
                    def scan(c):
                        k, slot, n = c.k, c.slot, c.round
                        if l == 0:
                            wait_got(dve, c)
                            if not early_chunk(k):
                                dve.wait_ge(pe_t.sem, pe_t.at(k - 1))
                            hold(dve, "dve")
                            dve.tensor_copy(sml[:, slot, 0:TPC], gat[:, c.lap, :, D]).then_inc(x_a.sem, 1)
                            dve.tensor_tensor(tiles(sca[:, slot, :]), gat[:, c.lap, :, 0:D],
                                              gat[:, c.lap, :, D:D + 1].to_broadcast([P, TPC, D]), ALU.mult)\
                               .then_inc(x_a.sem, 1)
                            dve.tensor_copy(pos_i[:, bass.ds(k * TPC, TPC)], gat[:, c.lap, :, D + 1])\
                               .then_inc(x_a.sem, 1)
                        dve.wait_ge(act_x.sem, act_x.at(k + 1))
                        if l:
                            wait_loads(dve, slot, n, loads)
                        if not early_chunk(k):
                            dve.wait_ge(pe_o.sem, pe_o.at(k - 1))
                        if not first(k):
                            dve.wait_ge(dve_s.sem, dve_s.at(k))
                        hold(dve, "dve")
                        if l:
                            dve.tensor_tensor(tmp[:, slot, :], xin[:, slot, :], brd[:, slot, :], ALU.mult)\
                               .then_inc(x_b.sem, 1)
                            dve.wait_ge(x_b.sem, x_b.at(k + 1))
                            hold(dve, "dve")
                        dve.tensor_tensor_scan(scn[:, slot, :], mask[:, bass.ds(k * CW, CW)],
                                               (tmp if l else xin)[:, slot, :],
                                               0.0 if first(k) else scn[:, 1 - slot, CW - 1:CW],
                                               ALU.mult, ALU.add).then_inc(dve_s.sem, 1)

                    def deviate(c):
                        k, slot, n = c.k, c.slot, c.round
                        dve.wait_ge(act_r.sem, act_r.at(k + 1))
                        if not early_chunk(k):
                            dve.wait_ge(pe_s.sem, pe_s.at(k - 1))
                        hold(dve, "dve")
                        dve.tensor_tensor(tiles(dev[:, slot, 0, :]), res[:, slot, :, 0:D],
                                          czero[:, l:l + 1, :].to_broadcast([P, TPC, D]), ALU.subtract)\
                           .then_inc(dve_d.sem, 1)
                        dve.wait_ge(dve_d.sem, dve_d.at(k + 1))
                        hold(dve, "dve")
                        dve.tensor_tensor(tiles(dev[:, slot, 0, :]), tiles(dev[:, slot, 0, :]),
                                          ends[:, bass.ds(k * TPC, TPC)].unsqueeze(2).to_broadcast([P, TPC, D]),
                                          ALU.mult).then_inc(x_g.sem, 1)
                        if not first(k):
                            gather_sums(c.before)

                    def gather_sums(c):
                        k, slot = c.k, c.slot
                        dve.wait_ge(act_q.sem, act_q.at(k + 1))
                        if first(k):
                            dve.wait_ge(x_h.sem, x_h.at(1))
                        else:
                            dve.wait_ge(pe_s.sem, pe_s.at(k))
                        hold(dve, "dve")
                        dve.tensor_tensor(acc, acc, dev[:, slot, :, :].rearrange("p q v -> p (q v)"), ALU.add)\
                           .then_inc(pe_s.sem, 1)
                    dve.memset(acc, 0.0).then_inc(x_h.sem, 1)
                    skewed(dve, scan, deviate)
                    gather_sums(LAST)
                    dve.wait_ge(x_f.sem, x_f.at(1))
                    m = sml[:, 1, :]
                    link(dve, dve_link, dve.tensor_scalar(m[:, 0:2], ps[6][:, 0:2], 1.0 / N, None, ALU.mult))
                    link(dve, dve_link, dve.tensor_tensor(m[:, 2:3], m[:, 0:1], m[:, 0:1], ALU.mult))
                    link(dve, x_e, dve.tensor_tensor(m[:, 3:4], m[:, 1:2], m[:, 2:3], ALU.subtract))
                    dve.wait_ge(act_link.sem, act_link.at(1))
                    link(dve, dve_link, dve.reciprocal(m[:, 5:6], m[:, 4:5]))
                    link(dve, dve_link, dve.tensor_tensor(aff[:, l, 0:1], m[:, 5:6], w["gamT"][:, l:l + 1], ALU.mult))
                    link(dve, dve_link, dve.tensor_scalar(m[:, 6:7], w["bsT"][:, l:l + 1], 0.0, m[:, 0:1],
                                                          ALU.max, ALU.add))
                    link(dve, dve_link, dve.tensor_tensor(m[:, 7:8], m[:, 6:7], aff[:, l, 0:1], ALU.mult))
                    link(dve, dve_link, dve.tensor_tensor(aff[:, l, 1:2], w["betT"][:, l:l + 1], m[:, 7:8],
                                                          ALU.subtract))
            act_link.base += 1
            gathered()
            loaded.base += 16 * (l < LANES)
            chunkwise(pe_t, pe_o, pe_s, act_x, act_q, act_r, dve_s, dve_d)
            chunkwise(x_g)
            x_h.base += 1
            x_f.base += 1
            if l == 0:
                chunkwise(x_a, per=3)
                chunkwise(x_d)
            else:
                chunkwise(x_b)
            if radial:
                chunkwise(x_d, x_i, x_j, zeroed)
            chunkwise(*ld, per=8 * loads)
            chunkwise(*stored, per=8 * saves)

        for l in range(L1):
            gcn_pass(l)

        hin = lrg[:, 0:4096].rearrange("p (s l t d) -> p s l t d", s=2, l=L1, t=TPC)
        hfm = lrg[:, 4096:8192].rearrange("p (s l v) -> p s l v", s=2, l=L1)
        with nc.Block() as block:
            @block.sync
            def _(sp):
                def load(c):
                    k, slot, n = c.k, c.slot, c.round
                    if not early_chunk(k):
                        sp.wait_ge(pe_t.sem, pe_t.at(L1 * (k - 1)))
                        hold(sp, "sp")
                    for l in range(L1):
                        sp.dma_start(hin[:, slot, l, :, :], rows_of(t_h[l], k)).then_inc(ld[slot].sem, 16)

                paced(sp, load)

            @block.tensor
            def _(pe):
                def turn_rows(c):
                    k, slot, n = c.k, c.slot, c.round
                    wait_loads(pe, slot, n, L1)
                    for l in range(L1):
                        if not first(k):
                            pe.wait_ge(act_x.sem, act_x.at(L1 * (k - 1) + l + 1))
                        hold(pe, "pe")
                        for t in range(TPC):
                            mm = pe.transpose(ps[l][:, t * P:(t + 1) * P], hin[:, slot, l, t, :], ident[:])
                        mm.then_inc(pe_t.sem, 1)

                def late(c):
                    k, slot, n = c.k, c.slot, c.round
                    pe.wait_ge(dve_s.sem, dve_s.at(k + 1))
                    if not early_chunk(k):
                        pe.wait_ge(act_r.sem, act_r.at(k - 1))
                    hold(pe, "pe")
                    for t in range(TPC):
                        pe.matmul(ps[4 + slot][:, t * P:(t + 1) * P], scn[:, slot, t * P:(t + 1) * P],
                                  w["lin1_w"][:], start=True, stop=False)
                        mm = pe.matmul(ps[4 + slot][:, t * P:(t + 1) * P], ones9[:], bias9[:, L1, :],
                                       start=False, stop=True)
                    mm.then_inc(pe_o.sem, 1)
                skewed(pe, turn_rows, late)

            @block.scalar
            def _(act):
                def normed(c):
                    k, slot, n = c.k, c.slot, c.round
                    for l in range(L1):
                        act.wait_ge(pe_t.sem, pe_t.at(L1 * k + l + 1))
                        if l == 0 and not early_chunk(k):
                            act.wait_ge(x_a.sem, x_a.at(2 * (k - 1)))
                        hold(act, "act")
                        act.activation(hfm[:, slot, l, :], ps[l][:], ACT.Relu, bias=aff[:, l, 1:2],
                                       scale=aff[:, l, 0:1]).then_inc(act_x.sem, 1)

                def finish(c):
                    k, slot, n = c.k, c.slot, c.round
                    act.wait_ge(pe_o.sem, pe_o.at(k + 1))
                    if not early_chunk(k):
                        act.wait_ge(stored[slot].sem, stored[slot].at(16 * n))
                    hold(act, "act")
                    act.activation(res[:, slot, :, 0:D], tiles(ps[4 + slot][:]), ACT.Relu).then_inc(act_r.sem, 1)
                    act.wait_ge(act_r.sem, act_r.at(k + 1))
                    hold(act, "act")
                    act.dma_start(rows_of(t_agg, k), res[:, slot, :, 0:D]).then_inc(stored[slot].sem, 16)
                skewed(act, normed, finish)
                for s in range(2):
                    act.wait_ge(stored[s].sem, stored[s].at(8 * C))

            @block.vector
            def _(dve):
                def step(c):
                    k, slot, n = c.k, c.slot, c.round
                    dve.wait_ge(act_x.sem, act_x.at(L1 * k + L1))
                    if not first(k):
                        dve.wait_ge(dve_s.sem, dve_s.at(k))
                    hold(dve, "dve")
                    dve.tensor_tensor(tmp[:, slot, :], hfm[:, slot, 0, :], hfm[:, slot, 1, :], ALU.max)\
                       .then_inc(x_a.sem, 1)
                    dve.tensor_tensor(sca[:, slot, :], hfm[:, slot, 2, :], hfm[:, slot, 3, :], ALU.max)\
                       .then_inc(x_a.sem, 1)
                    dve.wait_ge(x_a.sem, x_a.at(2 * k + 2))
                    if not early_chunk(k):
                        dve.wait_ge(pe_o.sem, pe_o.at(k - 1))
                    hold(dve, "dve")
                    dve.tensor_tensor(scn[:, slot, :], tmp[:, slot, :], sca[:, slot, :], ALU.max)\
                       .then_inc(dve_s.sem, 1)
                paced(dve, step)
        chunkwise(pe_o, act_r, dve_s)
        chunkwise(pe_t, act_x, *ld[0:0], per=L1)
        chunkwise(x_a, per=2)
        chunkwise(*ld, per=8 * L1)
        chunkwise(*stored, per=8)

        node_pass(t_x1e, t_agg, [t_x2])

        def big(i):
            return lrg[:, i * CW:(i + 1) * CW]
        wA, wB, vy, mA, mB = (big(i) for i in range(5))
        sA = [big(5), big(6)]
        sB = [big(7), big(8)]
        with nc.Block() as block:
            @block.gpsimd
            def _(pool):
                paced(pool, lambda c: pool_gather(pool, c, t_x2, src_i, D, pe_t))

            @block.sync
            def _(sp):
                def load(c):
                    k, slot, n = c.k, c.slot, c.round
                    if not early_chunk(k):
                        sp.wait_ge(x_c.sem, x_c.at(k - 1))
                        hold(sp, "sp")
                        sp.wait_ge(pe_s.sem, pe_s.at(2 * (k - 1)))
                        hold(sp, "sp")
                    sp.dma_start(h2s[:, slot, :], r_h2[:, bass.ds(k * CW, CW)]).then_inc(ld[slot].sem, 16)
                    for c in range(4):
                        sp.dma_start(brd[32 * c:32 * c + 32, slot, :],
                                     r_y[c, bass.ds(k * CW, CW)].partition_broadcast(32)).then_inc(ld[slot].sem, 16)

                paced(sp, load)

            @block.tensor
            def _(pe):
                def early(c):
                    k, slot, n = c.k, c.slot, c.round
                    wait_got(pe, c)
                    if not early_chunk(k):
                        pe.wait_ge(act_x.sem, act_x.at(k - 1))
                    hold(pe, "pe")
                    for t in range(TPC):
                        mm = pe.transpose(ps[slot][:, t * P:(t + 1) * P], gat[:, c.lap, t, 0:D], ident[:])
                    mm.then_inc(pe_t.sem, 1)

                def out_rows(c):
                    k, slot, n = c.k, c.slot, c.round
                    pe.wait_ge(dve_s.sem, dve_s.at(2 * k + 2))
                    if not first(k):
                        pe.wait_ge(act_r.sem, act_r.at(k))
                    hold(pe, "pe")
                    for t in range(TPC):
                        pe.matmul(ps[3][:, t * P:(t + 1) * P], sA[slot][:, t * P:(t + 1) * P], w["w_outA"][:],
                                  start=True, stop=False)
                        mm = pe.matmul(ps[3][:, t * P:(t + 1) * P], sB[slot][:, t * P:(t + 1) * P], w["w_outB"][:],
                                       start=False, stop=True)
                    mm.then_inc(pe_o.sem, 1)

                def late(c):
                    k, slot, n = c.k, c.slot, c.round
                    pe.wait_ge(act_x.sem, act_x.at(k + 1))
                    if not first(k):
                        pe.wait_ge(x_d.sem, x_d.at(k))
                    hold(pe, "pe")
                    pe.matmul(ps[7][:], w["w_vv"][:], xin[:, slot, :], start=True, stop=True,
                              skip_group_check=True).then_inc(x_a.sem, 1)
                    wait_loads(pe, slot, n, 5)
                    if not first(k):
                        pe.wait_ge(dve_d.sem, dve_d.at(2 * k))
                        pe.wait_ge(x_c.sem, x_c.at(k))
                    hold(pe, "pe")
                    pe.matmul(ps[4][:], w["mlp_w2A"][:], h2s[:, slot, :], start=True, stop=True).then_inc(pe_s.sem, 1)
                    pe.matmul(ps[6][:], w["w_ss"][:], xin[:, slot, :], start=True, stop=True).then_inc(x_a.sem, 1)
                    pe.matmul(ps[5][:], w["mlp_w2B"][:], h2s[:, slot, :], start=True, stop=True).then_inc(pe_s.sem, 1)
                    pe.wait_ge(x_b.sem, x_b.at(k + 1))
                    hold(pe, "pe")
                    pe.matmul(ps[7][:], w["w_dot"][:], vy, start=False, stop=True,
                              skip_group_check=True).then_inc(zeroed.sem, 1)
                    if not first(k):
                        out_rows(c.before)
                skewed(pe, early, late)
                out_rows(LAST)

            @block.scalar
            def _(act):
                def early(c):
                    k, slot, n = c.k, c.slot, c.round
                    act.wait_ge(pe_t.sem, pe_t.at(k + 1))
                    if not early_chunk(k):
                        act.wait_ge(x_a.sem, x_a.at(2 * (k - 1)))
                    hold(act, "act")
                    act.activation(xin[:, slot, :], ps[slot][:], ACT.Copy).then_inc(act_x.sem, 1)

                def finish(c):
                    k, slot, n = c.k, c.slot, c.round
                    act.wait_ge(pe_o.sem, pe_o.at(k + 1))
                    if not early_chunk(k):
                        act.wait_ge(stored[slot].sem, stored[slot].at(16 * n))
                    hold(act, "act")
                    act.activation(res[:, slot, :, 0:D], tiles(ps[3][:]), ACT.Copy,
                                   scale=1.0 / (32.0 ** 0.5 * 8.0 * 16.0)).then_inc(act_r.sem, 1)
                    act.wait_ge(act_r.sem, act_r.at(k + 1))
                    hold(act, "act")
                    act.dma_start(rows_of(t_agg, k), res[:, slot, :, 0:D]).then_inc(stored[slot].sem, 16)

                def late(c):
                    k, slot, n = c.k, c.slot, c.round
                    act.wait_ge(pe_s.sem, pe_s.at(2 * k + 1))
                    if not first(k):
                        act.wait_ge(x_c.sem, x_c.at(k))
                    hold(act, "act")
                    act.activation(wA, ps[4][:], ACT.Identity, bias=w["mlp_b2A"][:, 0:1]).then_inc(dve_d.sem, 1)
                    act.wait_ge(pe_s.sem, pe_s.at(2 * k + 2))
                    if not first(k):
                        act.wait_ge(x_d.sem, x_d.at(k))
                    hold(act, "act")
                    act.activation(wB, ps[5][:], ACT.Identity, bias=w["mlp_b2B"][:, 0:1]).then_inc(dve_d.sem, 1)
                    if not first(k):
                        finish(c.before)
                skewed(act, early, late)
                finish(LAST)
                for s in range(2):
                    act.wait_ge(stored[s].sem, stored[s].at(8 * C))

            @block.vector
            def _(dve):
                def step(c):
                    k, slot, n = c.k, c.slot, c.round
                    wait_loads(dve, slot, n, 5)
                    dve.wait_ge(x_a.sem, x_a.at(2 * k + 1))
                    if not first(k):
                        dve.wait_ge(zeroed.sem, zeroed.at(k))
                    hold(dve, "dve")
                    dve.tensor_tensor(vy, ps[7][:], brd[:, slot, :], ALU.mult).then_inc(x_b.sem, 1)
                    dve.wait_ge(x_a.sem, x_a.at(2 * k + 2))
                    dve.wait_ge(dve_d.sem, dve_d.at(2 * k + 1))
                    if not first(k):
                        dve.wait_ge(dve_s.sem, dve_s.at(2 * k))
                    hold(dve, "dve")
                    dve.tensor_tensor(mA, ps[6][:], wA, ALU.mult).then_inc(act_e.sem, 1)
                    dve.wait_ge(act_e.sem, act_e.at(k + 1))
                    hold(dve, "dve")
                    dve.tensor_tensor(mA, mA, brd[:, slot, :], ALU.mult).then_inc(x_c.sem, 1)
                    dve.wait_ge(x_c.sem, x_c.at(k + 1))
                    if not early_chunk(k):
                        dve.wait_ge(pe_o.sem, pe_o.at(k - 1))
                    hold(dve, "dve")
                    here = mask[:, bass.ds(k * CW, CW)]
                    dve.tensor_tensor_scan(sA[slot], here, mA, 0.0 if first(k) else sA[1 - slot][:, CW - 1:CW],
                                           ALU.mult, ALU.add).then_inc(dve_s.sem, 1)
                    dve.wait_ge(zeroed.sem, zeroed.at(k + 1))
                    dve.wait_ge(dve_d.sem, dve_d.at(2 * k + 2))
                    hold(dve, "dve")
                    dve.tensor_tensor(mB, ps[7][:], wB, ALU.mult).then_inc(x_d.sem, 1)
                    dve.wait_ge(x_d.sem, x_d.at(k + 1))
                    hold(dve, "dve")
                    dve.tensor_tensor_scan(sB[slot], here, mB, 0.0 if first(k) else sB[1 - slot][:, CW - 1:CW],
                                           ALU.mult, ALU.add).then_inc(dve_s.sem, 1)
                paced(dve, step)
        gathered()
        chunkwise(pe_t, pe_o, x_b, x_c, x_d, act_x, act_r, act_e, zeroed)
        chunkwise(x_a, pe_s, dve_d, dve_s, per=2)
        chunkwise(*ld, per=8 * 5)
        chunkwise(*stored, per=8)

        node_pass(t_x2, t_agg, [t_x3, t_acc[0], t_acc[1]])

        eq = lrg[:, 0:512].rearrange("p (t v) -> p t v", t=TPC)
        eqs = [lrg[:, 1024 * s:1024 * s + CW] for s in range(2)]
        eqb = lrg[:, 512:1024]
        f1 = [lrg[:, 2048 + CW * s:2048 + CW * (s + 1)] for s in range(2)]
        f2 = [lrg[:, 3072 + CW * s:3072 + CW * (s + 1)] for s in range(2)]
        msg = [lrg[:, 4096 + CW * s:4096 + CW * (s + 1)] for s in range(2)]
        srow = [lrg[:, 5120 + CW * s:5120 + CW * (s + 1)].bitcast(I32) for s in range(2)]
        ab = lrg[:, 6144:6144 + CW]
        ex = lrg[:, 6656:6656 + CW]
        src_f = lrg[:, 8192:8192 + TILES]
        away = lrg[:, 8704:8704 + TILES]
        with nc.Block() as block:
            @block.gpsimd
            def _(pool):
                def scatter(c):
                    k, slot = c.k, c.slot
                    pool.wait_ge(act_r.sem, act_r.at(k + 1))
                    pool.wait_ge(x_d.sem, x_d.at(k + 1))
                    hold(pool, "pool")
                    for t in range(TPC):
                        scatter_tile(c, t)

                def scatter_tile(c, t):
                    lane, lap = t % LANES, t // LANES
                    if not (first(c.k) and lap == 0):
                        pool.wait_ge(lanes[lane].sem, lanes[lane].at(16 * (TPC // LANES * c.k + lap)))
                        hold(pool, "pool")
                    pool.indirect_dma_start(t_acc[lane],
                                            bass.IndirectOffsetOnAxis(ap=sidx[:, c.slot, t:t + 1], axis=0),
                                            res[:, c.slot, t, 0:D], None, compute_op=ALU.add)\
                        .then_inc(lanes[lane].sem, 16)

                def ahead(c):
                    b = c.before.before
                    pool_ready(pool, c, dst_i, x_b)
                    pool.wait_ge(act_r.sem, act_r.at(b.k + 1))
                    pool.wait_ge(x_d.sem, x_d.at(b.k + 1))
                    hold(pool, "pool")
                    for t in range(TPC):
                        gather_tile(pool, c, t, t_x3[0:NP, :], D)
                        scatter_tile(b, t)
                for lap in range(2):
                    pool_gather(pool, Chunk(0, lap), t_x3, dst_i, D, x_b)
                for lap in range(2, RING):
                    ahead(Chunk(0, lap))
                with pool.Fori(1, TURNS) as i:
                    for lap in range(RING):
                        ahead(Chunk(i, lap))
                for c in TAIL:
                    ahead(c)
                scatter(LAST.before)
                scatter(LAST)
                for lane in range(LANES):
                    pool.wait_ge(lanes[lane].sem, lanes[lane].at(16 * TPC // LANES * C))

            @block.sync
            def _(sp):
                def load(c):
                    k, slot, n = c.k, c.slot, c.round
                    if not early_chunk(k):
                        sp.wait_ge(pe_t.sem, pe_t.at(k - 1))
                        hold(sp, "sp")
                        sp.wait_ge(x_a.sem, x_a.at(k - 1))
                        hold(sp, "sp")
                    sp.dma_start(att[:, slot, :], a["edge_attr"][:, bass.ds(k * CW, CW)]).then_inc(ld[slot].sem, 16)
                    sp.dma_start(srow[slot], a["src_row"][bass.ds(k * CW, CW)].partition_broadcast(P))\
                      .then_inc(ld[slot].sem, 16)
                paced(sp, load)

            @block.tensor
            def _(pe):
                def filt1(c):
                    k, slot, n = c.k, c.slot, c.round
                    wait_loads(pe, slot, n, 2)
                    if not early_chunk(k):
                        pe.wait_ge(x_e.sem, x_e.at(k - 1))
                    hold(pe, "pe")
                    pe.matmul(ps[slot][:], w["W1"][:], att[:, slot, :], start=True, stop=True).then_inc(pe_t.sem, 1)

                def dedupe(c):
                    k, slot, n = c.k, c.slot, c.round
                    pe.wait_ge(x_b.sem, x_b.at(k + 1))
                    pe.wait_ge(x_a.sem, x_a.at(k + 1))
                    if not early_chunk(k):
                        pe.wait_ge(act_r.sem, act_r.at(k - 1))
                    hold(pe, "pe")
                    for t in range(TPC):
                        mm = pe.matmul(ps[4 + slot][:, t * P:(t + 1) * P], eqs[slot][:, t * P:(t + 1) * P],
                                       msg[slot][:, t * P:(t + 1) * P], start=True, stop=True)
                    mm.then_inc(pe_o.sem, 1)

                def late(c):
                    k, slot, n = c.k, c.slot, c.round
                    pe.wait_ge(x_e.sem, x_e.at(k + 1))
                    if not early_chunk(k):
                        pe.wait_ge(x_i.sem, x_i.at(k - 1))
                    hold(pe, "pe")
                    for t in range(TPC):
                        pe.matmul(ps[2 + slot][:, t * P:(t + 1) * P], f1[slot][:, t * P:(t + 1) * P], w["W2"][:],
                                  start=True, stop=False)
                        mm = pe.matmul(ps[2 + slot][:, t * P:(t + 1) * P], ones9[:], bias9[:, L1 + 1, :],
                                       start=False, stop=True)
                    mm.then_inc(pe_s.sem, 1)
                    if not first(k):
                        dedupe(c.before)
                skewed(pe, filt1, late)
                dedupe(LAST)

            @block.scalar
            def _(act):
                def soft1(c):
                    k, slot, n = c.k, c.slot, c.round
                    act.wait_ge(x_g.sem, x_g.at(k + 1))
                    hold(act, "act")
                    act.activation(f1[slot], f1[slot], ACT.Exp).then_inc(act_q.sem, 1)
                    act.wait_ge(act_q.sem, act_q.at(k + 1))
                    hold(act, "act")
                    act.activation(f1[slot], f1[slot], ACT.Ln, bias=half[:, 0:1], scale=0.5).then_inc(act_x.sem, 1)

                def summed(c):
                    k, slot, n = c.k, c.slot, c.round
                    act.wait_ge(pe_o.sem, pe_o.at(k + 1))
                    if not early_chunk(k):
                        for lane in range(LANES):
                            act.wait_ge(lanes[lane].sem, lanes[lane].at(16 * TPC // LANES * (k - 1)))
                    hold(act, "act")
                    act.activation(res[:, slot, :, 0:D], tiles(ps[4 + slot][:]), ACT.Copy).then_inc(act_r.sem, 1)

                def late(c):
                    k, slot, n = c.k, c.slot, c.round
                    if not first(k):
                        summed(c.before)
                    act.wait_ge(x_h.sem, x_h.at(k + 1))
                    hold(act, "act")
                    act.activation(f2[slot], f2[slot], ACT.Exp).then_inc(act_e.sem, 1)
                    act.wait_ge(act_e.sem, act_e.at(k + 1))
                    hold(act, "act")
                    act.activation(f2[slot], f2[slot], ACT.Ln, bias=half[:, 0:1], scale=0.5).then_inc(x_f.sem, 1)
                act.preload_act_table_set("natural_log_exp_and_others")
                skewed(act, soft1, late)
                summed(LAST)

            @block.vector
            def _(dve):
                link(dve, dve_link, dve.tensor_copy(src_f, esrc_i[:]))
                link(dve, dve_link, dve.tensor_scalar(away, src_f, -1.0, lane[:, 0:1], ALU.mult, ALU.add))

                link(dve, dve_link, dve.tensor_scalar(sml[:, 0, 63:64], w["b1"][:], -LOG2, None, ALU.add))

                def early(c):
                    k, slot, n = c.k, c.slot, c.round
                    dve.wait_ge(pe_t.sem, pe_t.at(k + 1))
                    if not early_chunk(k):
                        dve.wait_ge(pe_s.sem, pe_s.at(k - 1))
                    hold(dve, "dve")
                    dve.tensor_scalar(f1[slot], ps[slot][:], w["b1"][:, 0:1], 40.0, ALU.add, ALU.min)\
                       .then_inc(x_g.sem, 1)
                    wait_loads(dve, slot, n, 2)
                    if not early_chunk(k):
                        dve.wait_ge(pe_o.sem, pe_o.at(k - 1))
                    if not first(k):
                        dve.wait_ge(x_d.sem, x_d.at(k))
                    hold(dve, "dve")
                    dve.tensor_tensor(tiles(eqs[slot]), tiles(srow[slot]),
                                      esrc_i[:, bass.ds(k * TPC, TPC)].unsqueeze(2).to_broadcast([P, TPC, P]),
                                      ALU.is_equal).then_inc(x_a.sem, 1)
                    dve.wait_ge(x_a.sem, x_a.at(k + 1))
                    hold(dve, "dve")
                    dve.tensor_tensor(tiles(eqb), tiles(eqs[slot]), below[:].unsqueeze(1).to_broadcast([P, TPC, P]),
                                      ALU.mult).then_inc(x_c.sem, 1)
                    dve.wait_ge(x_c.sem, x_c.at(4 * k + 1))
                    hold(dve, "dve")
                    dve.tensor_reduce(sml[:, slot, 0:TPC], tiles(eqb), AX, ALU.max).then_inc(x_c.sem, 1)
                    dve.wait_ge(x_c.sem, x_c.at(4 * k + 2))
                    hold(dve, "dve")
                    dve.tensor_tensor(sml[:, slot, 8:8 + TPC], sml[:, slot, 0:TPC], away[:, bass.ds(k * TPC, TPC)],
                                      ALU.mult).then_inc(x_c.sem, 1)
                    dve.wait_ge(x_c.sem, x_c.at(4 * k + 3))
                    hold(dve, "dve")
                    dve.tensor_tensor(sml[:, slot, 16:16 + TPC], sml[:, slot, 8:8 + TPC],
                                      src_f[:, bass.ds(k * TPC, TPC)], ALU.add).then_inc(x_c.sem, 1)
                    dve.wait_ge(x_c.sem, x_c.at(4 * k + 4))
                    if not early_chunk(k):
                        for lane in range(LANES):
                            dve.wait_ge(lanes[lane].sem, lanes[lane].at(16 * TPC // LANES * (k - 1)))
                    hold(dve, "dve")
                    dve.tensor_copy(sidx[:, slot, :], sml[:, slot, 16:16 + TPC]).then_inc(x_d.sem, 1)
                    dve.wait_ge(act_x.sem, act_x.at(k + 1))
                    hold(dve, "dve")
                    dve.scalar_tensor_tensor(out=f1[slot], in0=ps[slot][:], scalar=sml[:, 0, 63:64], in1=f1[slot],
                                             op0=ALU.add, op1=ALU.max).then_inc(x_e.sem, 1)

                def late(c):
                    k, slot, n = c.k, c.slot, c.round
                    dve.wait_ge(pe_s.sem, pe_s.at(k + 1))
                    hold(dve, "dve")
                    dve.tensor_scalar(f2[slot], ps[2 + slot][:], 40.0, None, ALU.min).then_inc(x_h.sem, 1)
                    message(c)

                def message(c):
                    k, slot, n = c.k, c.slot, c.round
                    dve.wait_ge(x_f.sem, x_f.at(k + 1))
                    if not early_chunk(k):
                        dve.wait_ge(pe_o.sem, pe_o.at(k - 1))
                    hold(dve, "dve")
                    dve.scalar_tensor_tensor(out=msg[slot], in0=ps[2 + slot][:], scalar=-LOG2, in1=f2[slot],
                                             op0=ALU.add, op1=ALU.max).then_inc(x_i.sem, 1)
                    dve.wait_ge(x_i.sem, x_i.at(k + 1))
                    wait_got(dve, c)
                    hold(dve, "dve")
                    dve.tensor_tensor(tiles(msg[slot]), tiles(msg[slot]), gat[:, c.lap, :, 0:D], ALU.mult)\
                       .then_inc(x_b.sem, 1)
                skewed(dve, early, late)
        gathered()
        chunkwise(pe_t, pe_s, pe_o, x_a, x_b, x_d, x_e, x_f, x_g, x_h, x_i, act_x, act_q, act_e, act_r)
        chunkwise(x_c, per=4)
        chunkwise(*ld, per=16)
        chunkwise(*lanes, per=16 * TPC // LANES)

        node_pass(None, None, [out], lanes_in=t_acc)


def kernel(**inputs):
    import numpy as np
    import concourse.bacc as bacc
    from concourse.bass_utils import run_bass_kernel_spmd

    f32 = np.float32
    g = {k: np.asarray(v) for k, v in inputs.items()}
    pad = NP - N

    def edges(v, fill):
        return np.concatenate([v, np.full((pad,) + v.shape[1:], fill, v.dtype)])

    def by_tile(v):
        return np.ascontiguousarray(v.reshape(TILES, P).T)

    src = edges(g["src"], NP)
    dst = edges(g["dst"], NP - 1)
    x = np.zeros((ROWS, D), f32)
    x[:N] = g["x"]
    up0, up1 = g["L2_gnn_W_up0"], g["L2_gnn_W_up1"]
    o0, o1 = g["L2_gnn_W_out0"], g["L2_gnn_W_out1"]
    w_ss, w_vv, w_dot = (np.zeros((D, D), f32) for _ in range(3))
    w_outA, w_outB = np.zeros((D, D), f32), np.zeros((D, D), f32)
    w_outA[0:32, 0:32], w_outB[0:32, 0:32] = o0[0:32], o0[32:64]
    for c in range(4):
        w_ss[0:32, 32 * c:32 * c + 32] = up0
    for c in range(3):
        b = 32 * (c + 1)
        w_vv[32 + c:D:3, b:b + 32] = up1
        w_outA[b:b + 32, 32 + c:D:3] = o1[0:32]
        w_outB[b:b + 32, 32 + c:D:3] = o1[32:64]
        w_dot[np.arange(b, b + 32), np.arange(32)] = 3.0 ** -0.5
    w2, b2 = g["L2_gnn_mlp_w2"], g["L2_gnn_mlp_b2"]
    colA = np.concatenate([np.arange(0, 32)] + 3 * [np.arange(32, 64)])
    colB = np.concatenate([np.arange(96, 128)] + 3 * [np.arange(64, 96)])
    arrays = {
        "x": x, "src": by_tile(src), "dst": by_tile(dst),
        "dst_row": np.concatenate([np.full(1, -1, dst.dtype), dst, np.full(1, -1, dst.dtype)]), "src_row": src,
        "weight": edges(g["edge_weight"], 0), "radius": edges(g["edge_weight"], 0).reshape(16, NP // 16),
        "edge_vec": np.ascontiguousarray(edges(g["edge_attr_3"], 0).reshape(P, TILES, 3).transpose(0, 2, 1)),
        "edge_attr": np.ascontiguousarray(edges(g["edge_attr_64"], 0).T),
        "pool_wT": np.ascontiguousarray(g["L0_gnn_pool_w"].T), "lin_wT": np.ascontiguousarray(g["L0_gnn_lin_w"].T),
        "pool_b": g["L0_gnn_pool_b"][:, None], "lin1_w": g["L1_gnn_lin1_w"],
        "bias_rows": np.concatenate([g["L0_gnn_lin_b"][None], g["L0_gnn_bias"][None], g["L1_gnn_bs"]]),
        "rows": np.concatenate([g["L1_gnn_bs"], g["L1_gnn_lin1_b"][None], g["L3_gnn_b2"][None],
                                g["L0_gnn_lin_b"][None]]),
        "third": np.tile(np.eye(3, dtype=f32), (3, 1)),
        "leads": np.repeat((np.arange(9) < 3).astype(f32)[:, None], P, axis=1),
        "gcn_w": g["L1_gnn_Ws"], "bsT": np.ascontiguousarray(g["L1_gnn_bs"].T),
        "gamT": np.ascontiguousarray(g["L1_gnn_gammas"].T), "betT": np.ascontiguousarray(g["L1_gnn_betas"].T),
        "w_ss": w_ss, "w_vv": w_vv, "w_dot": w_dot, "w_outA": w_outA, "w_outB": w_outB,
        "mlp_w0": g["L2_gnn_mlp_w0"], "mlp_w1": g["L2_gnn_mlp_w1"],
        "mlp_w2A": np.ascontiguousarray(w2[:, colA]), "mlp_w2B": np.ascontiguousarray(w2[:, colB]),
        "mlp_b0": g["L2_gnn_mlp_b0"][:, None], "mlp_b1": g["L2_gnn_mlp_b1"][:, None],
        "mlp_b2A": b2[colA][:, None], "mlp_b2B": b2[colB][:, None],
        "W1": g["L3_gnn_W1"], "W2": g["L3_gnn_W2"], "b1": g["L3_gnn_b1"][:, None],
        "centre": np.repeat(np.arange(8, dtype=f32) / f32(7), 16)[:, None],
    }
    nc = bacc.Bacc("TRN2", target_bir_lowering=False, num_devices=1)
    feed, a = {}, {}
    for name, v in arrays.items():
        feed["in_" + name] = np.ascontiguousarray(v)
        a[name] = nc.dram_tensor("in_" + name, v.shape, mybir.dt.from_np(v.dtype), kind="ExternalInput").ap()
    out = nc.dram_tensor("out_x", (NP, D), F32, kind="ExternalOutput").ap()
    build(nc, a, out)
    r = run_bass_kernel_spmd(nc, [feed], core_ids=[0])
    return r.results[0]["out_x"][:N]
```

```python
from contextlib import ExitStack

import concourse.bass as bass
from concourse import mybir

P = 128
D = 128
N = 50000
TILES = 392
NP = TILES * P
TPC = 4
CW = TPC * P
C = TILES // TPC
ROWS = NP + 2 * P
EXT = D + 2
LANES = 2
HUGE = 3.0e38
EPS = 1e-5
LOG2 = 0.6931471805599453
L1 = 4

F32 = mybir.dt.float32
BF16 = mybir.dt.bfloat16
I32 = mybir.dt.int32
U8 = mybir.dt.uint8
ALU = mybir.AluOpType
ACT = mybir.ActivationFunctionType
AX = mybir.AxisListType.X


class Signal:

    def __init__(self, ctx, nc, name):
        self.sem = ctx.enter_context(nc.semaphore(name))
        self.base = 0

    def at(self, count):
        return count + self.base


RING = 4


class Chunk:

    def __init__(self, turn, lap):
        self.turn, self.lap = turn, lap
        self.k = RING * turn + lap
        self.slot = lap % 2
        self.round = RING // 2 * turn + lap // 2

    @property
    def before(self):
        return Chunk(self.turn, self.lap - 1) if self.lap else Chunk(self.turn - 1, RING - 1)

    @property
    def after(self):
        return Chunk(self.turn, self.lap + 1) if self.lap < RING - 1 else Chunk(self.turn + 1, 0)


TURNS = C // RING
TAIL = [Chunk(TURNS, lap) for lap in range(C % RING)]
LAST = TAIL[-1]


def paced(eng, step):
    for lap in range(RING):
        step(Chunk(0, lap))
    with eng.Fori(1, TURNS) as i:
        for lap in range(RING):
            step(Chunk(i, lap))
    for c in TAIL:
        step(c)


def skewed(eng, early, late):
    early(Chunk(0, 0))
    for lap in range(1, RING):
        early(Chunk(0, lap))
        late(Chunk(0, lap - 1))
    with eng.Fori(1, TURNS) as i:
        for lap in range(RING):
            early(Chunk(i, lap))
            late(Chunk(i, lap).before)
    for c in TAIL:
        early(c)
        late(c.before)
    late(LAST)


def early_chunk(k, ring=2):
    return isinstance(k, int) and k < ring


def rows_of(table, k, width=D):
    return table[bass.ds(k * CW, CW), 0:width].rearrange("(t p) d -> p t d", p=P)


def build(nc, a, out):
    with ExitStack() as ctx:
        def sb(name, shape, dt=F32):
            return ctx.enter_context(nc.sbuf_tensor(name, shape, dt))

        def dram(name, shape, dt=F32):
            return nc.dram_tensor(name, shape, dt).ap()

        def signal(name):
            return Signal(ctx, nc, name)

        t_agg = dram("t_agg", [ROWS, D])
        t_h = [dram(f"t_h{i}", [ROWS, D]) for i in range(L1)]
        t_x1e = dram("t_x1e", [ROWS, EXT])
        t_x2 = dram("t_x2", [ROWS, D])
        t_x3 = dram("t_x3", [ROWS, D])
        t_acc = [dram(f"t_acc{i}", [ROWS, D]) for i in range(LANES)]
        r_ns = dram("r_ns", [TILES, P])
        r_sq = dram("r_sq", [9, NP], BF16)
        r_mask = dram("r_mask", [NP], U8)
        r_lin = dram("r_lin", [2, NP])
        r_h2 = dram("r_h2", [64, NP])
        r_y = dram("r_y", [4, NP])
        r_emb = dram("r_emb", [8, NP])

        e_dst = dram("e_dst", [NP + 2, 1], I32)
        e_src = dram("e_src", [NP, 1], I32)
        e_w = dram("e_w", [NP, 1])
        e_v = [dram(f"e_v{c}", [NP, 1]) for c in range(3)]
        e_count = dram("e_count", [NP, 1])
        e_line = dram("e_line", [P, 1])

        mask = sb("mask", [P, NP], U8)
        src_i = sb("src_i", [P, TILES], I32)
        dst_i = sb("dst_i", [P, TILES], I32)
        pos_i = sb("pos_i", [P, TILES], I32)
        endp_i = sb("endp_i", [P, TILES], I32)
        endp_f = sb("endp_f", [P, TILES])
        nsrc = sb("nsrc", [P, TILES])
        ndst = sb("ndst", [P, TILES])
        ends = sb("ends", [P, TILES])
        ident = sb("ident", [P, P])
        below = sb("below", [P, P])
        above = sb("above", [P, P])
        ones = sb("ones", [P, P])
        epsc = sb("epsc", [P, 1])
        lane = sb("lane", [P, 1])
        half = sb("half", [P, 1])
        zer = sb("zer", [P, CW])
        one = sb("one", [1, CW])
        w = {}
        for name, shape in (("pool_wT", [D, D]), ("lin_wT", [D, D]), ("lin1_w", [D, D]), ("w_ss", [D, D]),
                            ("w_vv", [D, D]), ("w_outA", [D, D]), ("w_outB", [D, D]), ("w_dot", [D, D]),
                            ("mlp_w0", [8, 64]), ("mlp_w1", [64, 64]), ("mlp_w2A", [64, D]),
                            ("mlp_w2B", [64, D]), ("W1", [64, D]), ("W2", [D, D]),
                            ("pool_b", [D, 1]), ("bsT", [D, L1]), ("gamT", [D, L1]), ("betT", [D, L1]),
                            ("mlp_b0", [64, 1]), ("mlp_b1", [64, 1]), ("mlp_b2A", [D, 1]), ("mlp_b2B", [D, 1]),
                            ("b1", [D, 1]), ("centre", [P, 1]), ("third", [9, 3]), ("leads", [9, P])):
            w[name] = sb("w_" + name, shape)
        gcn_w = sb("gcn_w", [D, L1, D])
        bias9 = sb("bias9", [9, L1 + 3, D], BF16)
        ones9 = sb("ones9", [9, P], BF16)
        sq9 = sb("sq9", [9, 2, CW], BF16)
        esrc_i = sb("esrc_i", [P, TILES], I32)
        h2s = sb("h2s", [64, 2, CW])
        bcast = sb("bcast", [P, 2 + L1, D])
        czero = sb("czero", [P, L1, D])
        aff = sb("aff", [P, L1, 2])
        gat = sb("gat", [P, RING, TPC, EXT])
        idx = sb("idx", [P, RING, TPC], I32)
        xin = sb("xin", [P, 2, CW])
        brd = sb("brd", [P, 2, CW])
        sca = sb("sca", [P, 2, CW])
        tmp = sb("tmp", [P, 2, CW])
        res = sb("res", [P, 2, TPC, EXT])
        dev = sb("dev", [P, 2, 2, CW])
        sml = sb("sml", [P, 2, 64])
        scn = sb("scn", [P, 2, CW])
        row1 = sb("row1", [1, 2, CW])
        nst = sb("nst", [TPC, 2, P])
        embs = sb("embs", [8, 2, CW])
        att = sb("att", [64, 2, CW])
        sidx = sb("sidx", [P, RING, TPC], I32)
        lrg = sb("lrg", [P, 5 * 2048])

        ps = [ctx.enter_context(nc.psum_tensor(f"ps{i}", [P, CW], F32)) for i in range(8)]

        loaded = signal("loaded")
        got = [signal(f"got{i}") for i in range(RING)]
        idx_ready = signal("idx_ready")
        ld = [signal(f"ld{i}") for i in range(2)]
        rows_in = [signal(f"rows_in{i}") for i in range(RING)]
        norms_in = [signal(f"norms_in{i}") for i in range(2)]
        basis_in = [signal(f"basis_in{i}") for i in range(2)]
        norms_out = [signal(f"norms_out{i}") for i in range(2)]
        stored = [signal(f"stored{i}") for i in range(2)]
        pool_link = signal("pool_link")
        dve_link = signal("dve_link")
        act_link = signal("act_link")
        pe_t = signal("pe_t")
        pe_o = signal("pe_o")
        pe_s = signal("pe_s")
        act_x = signal("act_x")
        act_r = signal("act_r")
        dve_s = signal("dve_s")
        dve_d = signal("dve_d")
        act_q = signal("act_q")
        x_a = signal("x_a")
        x_b = signal("x_b")
        x_c = signal("x_c")
        x_d = signal("x_d")
        x_e = signal("x_e")
        x_f = signal("x_f")
        zeroed = signal("zeroed")
        act_e = signal("act_e")
        x_g = signal("x_g")
        x_h = signal("x_h")
        x_i = signal("x_i")
        x_j = signal("x_j")
        lanes = [signal(f"lane{i}") for i in range(LANES)]
        sort_load, sort_key, sort_got, sort_put, sort_tile, sort_step, sort_run, sort_sum, sort_move = (
            signal("sort_" + name) for name in ("load", "key", "got", "put", "tile", "step", "run", "sum", "move"))
        turn = {e: ctx.enter_context(nc.semaphore(f"turn_{e}")) for e in ("pool", "dve", "act", "pe", "sp")}

        def chunkwise(*signals, per=1):
            for s in signals:
                s.base += per * C

        def link(eng, sig, ins):
            ins.then_inc(sig.sem, 1)
            sig.base += 1
            eng.wait_ge(sig.sem, sig.base)


        def hold(eng, name):
            eng.sem_inc(turn[name], 1)

        def first(k):
            return isinstance(k, int) and k == 0

        def pool_ready(pool, c, index, freed, per=1):
            if not early_chunk(c.k, RING):
                pool.wait_ge(freed.sem, freed.at(per * (c.k - RING + 1)))
                hold(pool, "pool")
            pool.tensor_copy(idx[:, c.lap, :], index[:, bass.ds(c.k * TPC, TPC)]).then_inc(idx_ready.sem, 1)
            pool.wait_ge(idx_ready.sem, idx_ready.at(c.k + 1))
            hold(pool, "pool")

        def gather_tile(pool, c, t, table, width):
            pool.indirect_dma_start(gat[:, c.lap, t, 0:width], None, table,
                                    bass.IndirectOffsetOnAxis(ap=idx[:, c.lap, t:t + 1], axis=0))\
                .then_inc(got[c.lap].sem, 16)

        def pool_gather(pool, c, table, index, width, freed, per=1):
            pool_ready(pool, c, index, freed, per)
            for t in range(TPC):
                gather_tile(pool, c, t, table[0:NP + (index is src_i), :], width)

        def gathered():
            idx_ready.base += C
            for lap in range(RING):
                got[lap].base += 16 * TPC * (TURNS + (lap < C % RING))

        def wait_got(eng, c):
            eng.wait_ge(got[c.lap].sem, got[c.lap].at(16 * TPC * c.turn + 16 * TPC))

        def wait_loads(eng, slot, n, each):
            eng.wait_ge(ld[slot].sem, ld[slot].at(16 * each * n + 16 * each))

        def tiles(ap):
            return ap.rearrange("p (t d) -> p t d", t=TPC)

        with nc.Block() as block:
            @block.gpsimd
            def _(pool):
                for m, v in ((ones, 1.0), (ident, 0.0), (below, 0.0), (above, 0.0), (epsc, EPS), (zer, 0.0), (one, 1.0), (half, 0.5)):
                    pool.memset(m[:], v).then_inc(pool_link.sem, 1)
                pool.iota(idx[:, 0, 0:1], [[0, 1]], base=NP + 1, channel_multiplier=1).then_inc(pool_link.sem, 1)
                pool.wait_ge(pool_link.sem, 9)
                for m, op, step, mult in ((ident, ALU.not_equal, -1, 1), (below, ALU.is_ge, 1, -1),
                                          (above, ALU.is_ge, -1, 1)):
                    pool.affine_select(out=m[:], in_=m[:], compare_op=op, fill=1.0, base=0,
                                       pattern=[[step, P]], channel_multiplier=mult).then_inc(pool_link.sem, 1)
                pool.tensor_copy(lane[:], idx[:, 0, 0:1]).then_inc(pool_link.sem, 1)
                pool.wait_ge(pool_link.sem, 13)

            @block.sync
            def _(sp):
                n = 0
                for name, t in w.items():
                    sp.dma_start(t[:], a[name]).then_inc(loaded.sem, 16)
                    n += 1
                for t, s in ((gcn_w[:], a["gcn_w"].rearrange("l i o -> i l o")),
                             (bcast[:], a["bias_rows"].partition_broadcast(P)),
                             (dst_i[:], a["dst"]), (esrc_i[:], a["src"])):
                    sp.dma_start(t, s).then_inc(loaded.sem, 16)
                    n += 1
                sp.wait_ge(loaded.sem, 16 * n)
                sp.wait_ge(pool_link.sem, 8)
                for table, width in ((t_x1e, EXT), (t_x2, D)):
                    sp.dma_start(table[NP:NP + 1, :], zer[0:1, 0:width]).then_inc(loaded.sem, 16)
                    n += 1
                sp.wait_ge(loaded.sem, 16 * n)
        pool_link.base = 13
        loaded.base = 16 * (len(w) + 6)

        cur, prv = (lrg[:, i * TILES:(i + 1) * TILES].bitcast(I32) for i in range(2))
        fall = lrg[:, 2 * TILES:3 * TILES]
        rank = lrg[:, 3 * TILES:4 * TILES]
        count = lrg[:, 4 * TILES:5 * TILES]
        start = lrg[:, 5 * TILES:6 * TILES]
        one_f = lrg[:, 6 * TILES:7 * TILES]
        fields = lrg[:, 7 * TILES:11 * TILES].rearrange("p (q t) -> p q t", q=4)
        same = lrg[:, 11 * TILES:11 * TILES + P]
        same_b = lrg[:, 11 * TILES + P:11 * TILES + 2 * P]
        keys = lrg[:, 11 * TILES + 2 * P:11 * TILES + 3 * P].bitcast(I32)
        line = lrg[0:1, 11 * TILES + 3 * P:11 * TILES + 5 * P]
        falls, base_f, met, total, place_f, within = (sml[:, 0, i:i + 1] for i in range(6))
        unsorted = sml[0:1, 0, 8:9].bitcast(I32)
        place_i, place1_i, key_of = (sml[:, 0, i:i + 1].bitcast(I32) for i in (9, 10, 11))
        out_f = sml[:, 0, 16:20]
        out_i = sml[:, 0, 20:22].bitcast(I32)
        edge_tables = [(e_v[0], out_f[:, 0:1], 0), (e_v[1], out_f[:, 1:2], 0), (e_v[2], out_f[:, 2:3], 0),
                       (e_w, out_f[:, 3:4], 0), (e_src, out_i[:, 0:1], 0), (e_dst, out_i[:, 1:2], 1)]

        def flat(table):
            return table.rearrange("n o -> (n o)")

        def linear(row):
            return row.rearrange("(p t) -> p t", p=P)
        l_base, s_base = loaded.base, stored[0].base
        with nc.Block() as block:
            @block.sync
            def _(sp):
                sp.dma_start(cur, linear(a["dst_row"][1:NP + 1])).then_inc(loaded.sem, 16)
                sp.dma_start(prv, linear(a["dst_row"][0:NP])).then_inc(loaded.sem, 16)
                sp.dma_start(flat(e_dst), a["dst_row"]).then_inc(stored[0].sem, 16)
                sp.dma_start(flat(e_src), a["src_row"]).then_inc(stored[0].sem, 16)
                sp.dma_start(flat(e_w), a["weight"]).then_inc(stored[0].sem, 16)
                for c in range(3):
                    sp.dma_start(linear(flat(e_v[c])), a["edge_vec"][:, c, :]).then_inc(stored[0].sem, 16)
                sp.wait_ge(dve_link.sem, 2)
                sp.dma_start(flat(e_line), falls).then_inc(stored[0].sem, 16)
                sp.wait_ge(stored[0].sem, s_base + 16 * 7)
                sp.dma_start(line[:, 0:P], flat(e_line).unsqueeze(0)).then_inc(loaded.sem, 16)

            @block.vector
            def _(dve):
                dve.wait_ge(loaded.sem, l_base + 32)
                link(dve, dve_link, dve.tensor_tensor(fall, cur, prv, ALU.is_lt))
                link(dve, dve_link, dve.tensor_reduce(falls, fall, AX, ALU.max))
                dve.wait_ge(loaded.sem, l_base + 48)
                link(dve, dve_link, dve.tensor_reduce(base_f[0:1, :], line[:, 0:P], AX, ALU.max))
                link(dve, dve_link, dve.tensor_copy(unsorted, base_f[0:1, :]))
        loaded.base += 48
        stored[0].base += 16 * 7

        f_base = dve_link.base
        with nc.Block() as block:
            @block.gpsimd
            def _(pool):
                pool.wait_ge(dve_link.sem, f_base)
                flag = pool.value_load(unsorted, min_val=0, max_val=1)
                with pool.If(flag > 0):
                    pool.dma_start(linear(flat(e_count)), zer[:, 0:TILES]).then_inc(sort_load.sem, 16)
                    pool.dma_start(fields, a["edge_fields"]).then_inc(sort_load.sem, 16)
                    pool.wait_ge(sort_load.sem, 32)
                    with pool.Fori(0, TILES) as t:
                        pool.dma_start(keys, a["dst_row"][bass.ds(t * P + 1, P)].partition_broadcast(P))\
                            .then_inc(sort_load.sem, 16)
                        pool.tensor_copy(key_of, dst_i[:, bass.ds(t, 1)]).then_inc(sort_key.sem, 1)
                        pool.wait_ge(sort_key.sem, t + 1)
                        hold(pool, "pool")
                        pool.indirect_dma_start(met, None, e_count, bass.IndirectOffsetOnAxis(ap=key_of, axis=0))\
                            .then_inc(sort_got.sem, 16)
                        pool.wait_ge(sort_tile.sem, t + 1)
                        hold(pool, "pool")
                        pool.indirect_dma_start(e_count, bass.IndirectOffsetOnAxis(ap=key_of, axis=0), total, None)\
                            .then_inc(sort_put.sem, 16)
                        pool.wait_ge(sort_put.sem, 16 * t + 16)
                        hold(pool, "pool")
                    pool.dma_start(count, linear(flat(e_count))).then_inc(sort_load.sem, 16)
                    pool.wait_ge(sort_sum.sem, 1)
                    pool.dma_start(flat(e_line), total).then_inc(sort_move.sem, 16)
                    pool.wait_ge(sort_move.sem, 16)
                    pool.dma_start(line[:, 0:P], flat(e_line).unsqueeze(0)).then_inc(sort_move.sem, 16)
                    pool.wait_ge(sort_sum.sem, 2)
                    pool.dma_start(flat(e_line).unsqueeze(0), line[:, P:2 * P]).then_inc(sort_move.sem, 16)
                    pool.wait_ge(sort_move.sem, 48)
                    pool.dma_start(base_f, flat(e_line)).then_inc(sort_move.sem, 16)
                    pool.wait_ge(sort_sum.sem, 3)
                    pool.dma_start(linear(flat(e_count)), start).then_inc(sort_move.sem, 16)
                    pool.wait_ge(sort_move.sem, 80)
                    with pool.Fori(0, TILES) as t:
                        pool.tensor_copy(key_of, dst_i[:, bass.ds(t, 1)]).then_inc(sort_key.sem, 1)
                        pool.wait_ge(sort_key.sem, t + TILES + 1)
                        hold(pool, "pool")
                        pool.indirect_dma_start(met, None, e_count, bass.IndirectOffsetOnAxis(ap=key_of, axis=0))\
                            .then_inc(sort_got.sem, 16)
                        pool.wait_ge(sort_tile.sem, t + TILES + 1)
                        hold(pool, "pool")
                        for table, field, shift in edge_tables:
                            at = place1_i if shift else place_i
                            pool.indirect_dma_start(table, bass.IndirectOffsetOnAxis(ap=at, axis=0), field, None)\
                                .then_inc(sort_put.sem, 16)
                        pool.wait_ge(sort_put.sem, 16 * TILES + 96 * t + 96)
                        hold(pool, "pool")

            @block.vector
            def _(dve):
                flag = dve.value_load(unsorted, min_val=0, max_val=1)
                with dve.If(flag > 0):
                    with dve.Fori(0, TILES) as t:
                        dve.wait_ge(sort_load.sem, 16 * t + 48)
                        hold(dve, "dve")
                        dve.tensor_tensor(same, keys, dst_i[:, bass.ds(t, 1)].to_broadcast([P, P]), ALU.is_equal)\
                           .then_inc(sort_step.sem, 1)
                        dve.wait_ge(sort_step.sem, 5 * t + 1)
                        hold(dve, "dve")
                        dve.tensor_tensor(same_b, same, below[:], ALU.mult).then_inc(sort_step.sem, 1)
                        dve.tensor_reduce(total, same, AX, ALU.add).then_inc(sort_step.sem, 1)
                        dve.wait_ge(sort_step.sem, 5 * t + 3)
                        hold(dve, "dve")
                        dve.tensor_reduce(within, same_b, AX, ALU.add).then_inc(sort_step.sem, 1)
                        dve.wait_ge(sort_step.sem, 5 * t + 4)
                        hold(dve, "dve")
                        dve.wait_ge(sort_got.sem, 16 * t + 16)
                        hold(dve, "dve")
                        dve.tensor_tensor(rank[:, bass.ds(t, 1)], within, met, ALU.add).then_inc(sort_step.sem, 1)
                        dve.tensor_tensor(total, total, met, ALU.add).then_inc(sort_tile.sem, 1)
                    dve.wait_ge(sort_load.sem, 16 * TILES + 48)
                    dve.memset(one_f, 1.0).then_inc(sort_run.sem, 1)
                    dve.wait_ge(sort_run.sem, 1)
                    dve.tensor_tensor_scan(start, one_f, count, 0.0, ALU.mult, ALU.add).then_inc(sort_run.sem, 1)
                    dve.wait_ge(sort_run.sem, 2)
                    dve.wait_ge(sort_tile.sem, TILES)
                    dve.tensor_copy(total, start[:, TILES - 1:TILES]).then_inc(sort_sum.sem, 1)
                    dve.wait_ge(sort_move.sem, 32)
                    dve.memset(line[:, P:P + 1], 0.0).then_inc(sort_run.sem, 1)
                    dve.tensor_tensor_scan(line[:, P + 1:2 * P], one_f[0:1, 0:P - 1], line[:, 0:P - 1], 0.0, ALU.mult,
                                           ALU.add).then_inc(sort_run.sem, 1)
                    dve.wait_ge(sort_run.sem, 4)
                    dve.tensor_tensor(start, start, count, ALU.subtract).then_inc(sort_sum.sem, 1)
                    dve.wait_ge(sort_sum.sem, 2)
                    dve.wait_ge(sort_move.sem, 64)
                    dve.tensor_scalar(start, start, base_f, None, ALU.add).then_inc(sort_sum.sem, 1)
                    with dve.Fori(0, TILES) as t:
                        dve.tensor_copy(out_f, fields[:, :, bass.ds(t, 1)]).then_inc(sort_step.sem, 1)
                        dve.tensor_copy(out_i[:, 0:1], esrc_i[:, bass.ds(t, 1)]).then_inc(sort_step.sem, 1)
                        dve.tensor_copy(out_i[:, 1:2], dst_i[:, bass.ds(t, 1)]).then_inc(sort_step.sem, 1)
                        dve.wait_ge(sort_got.sem, 16 * TILES + 16 * t + 16)
                        hold(dve, "dve")
                        dve.tensor_tensor(place_f, rank[:, bass.ds(t, 1)], met, ALU.add).then_inc(sort_step.sem, 1)
                        dve.wait_ge(sort_step.sem, 5 * TILES + 5 * t + 4)
                        hold(dve, "dve")
                        dve.tensor_copy(place_i, place_f).then_inc(sort_step.sem, 1)
                        dve.tensor_scalar(place1_i, place_f, 1.0, None, ALU.add).then_inc(sort_tile.sem, 1)
                        dve.wait_ge(sort_step.sem, 5 * TILES + 5 * t + 5)
                        hold(dve, "dve")
                        dve.wait_ge(sort_put.sem, 16 * TILES + 96 * t + 96)
                        hold(dve, "dve")

        cur, prv, nxt = (lrg[:, i * TILES:(i + 1) * TILES].bitcast(I32) for i in range(3))
        m_f, c_f, q_f, s_f, e_f, o_f, z_f = (lrg[:, i * TILES:(i + 1) * TILES] for i in range(3, 10))
        m_u = lrg[:, 10 * TILES:10 * TILES + TILES // 4].bitcast(U8)
        part = [lrg[:, 11 * TILES + i * TILES // 2:11 * TILES + (i + 1) * TILES // 2].bitcast(BF16) for i in range(3)]
        crow = row1[0:1, 0, :]
        blocks = lrg[:, 13 * TILES:13 * TILES + 12 * P].rearrange("p (q b v) -> p q b v", q=3, b=4)
        b9, b9r = (lrg[0:9, 17 * TILES + i * 1024:17 * TILES + i * 1024 + 7 * D] for i in range(2))
        b9p = lrg[0:9, 17 * TILES + 2048:17 * TILES + 2048 + 7 * D // 2].bitcast(BF16)

        l_base, s_base = loaded.base, stored[0].base
        with nc.Block() as block:
            @block.sync
            def _(sp):
                sp.dma_start(cur, linear(flat(e_dst)[1:NP + 1])).then_inc(loaded.sem, 16)
                sp.dma_start(prv, linear(flat(e_dst)[0:NP])).then_inc(loaded.sem, 16)
                sp.dma_start(nxt, linear(flat(e_dst)[2:NP + 2])).then_inc(loaded.sem, 16)
                sp.dma_start(b9, a["rows"].rearrange("r d -> (r d)").partition_broadcast(9)).then_inc(loaded.sem, 16)
                sp.wait_ge(x_a.sem, 1)
                sp.dma_start(linear(r_mask), m_u).then_inc(stored[0].sem, 16)
                sp.wait_ge(stored[0].sem, s_base + 16)
                sp.dma_start(mask[:], r_mask.partition_broadcast(P)).then_inc(loaded.sem, 16)
                sp.wait_ge(x_a.sem, 3)
                sp.dma_start(linear(r_lin[0]), s_f).then_inc(stored[0].sem, 16)
                sp.dma_start(linear(r_lin[1]), e_f).then_inc(stored[0].sem, 16)
                sp.wait_ge(x_a.sem, 4)
                for r in range(9):
                    sp.dma_start(linear(r_sq[r]), part[r // 3]).then_inc(stored[0].sem, 16)
                sp.wait_ge(stored[0].sem, s_base + 16 * 12)
                sources = (r_lin[0], r_lin[1], flat(e_src))
                for q in range(3):
                    by_rows = sources[q].rearrange("(t p) -> t p", p=P)
                    target = blocks[:, q, :, :] if q < 2 else blocks[:, q, :, :].bitcast(I32)
                    sp.dma_start(target[:, 0:3, :], by_rows[0:384, :].rearrange("(b t) p -> t b p", b=3))\
                      .then_inc(loaded.sem, 16)
                    sp.dma_start(target[0:8, 3, :], by_rows[384:392, :]).then_inc(loaded.sem, 16)
                sp.wait_ge(loaded.sem, l_base + 16 * 11)

            @block.vector
            def _(dve):
                dve.wait_ge(loaded.sem, l_base + 64)
                link(dve, dve_link, dve.tensor_tensor(m_f, cur, prv, ALU.is_equal))
                link(dve, x_a, dve.tensor_copy(m_u, m_f))
                link(dve, dve_link, dve.memset(o_f, 1.0))
                link(dve, dve_link, dve.memset(z_f, 0.0))
                link(dve, dve_link, dve.tensor_tensor_scan(c_f, m_f, o_f, 0.0, ALU.mult, ALU.add))
                link(dve, dve_link, dve.tensor_tensor_scan(q_f, m_f, z_f, 1.0, ALU.mult, ALU.add))
                link(dve, dve_link, dve.tensor_copy(sml[:, 0, 0:1], c_f[:, TILES - 1:TILES]))
                link(dve, x_b, dve.tensor_copy(sml[:, 0, 1:2], q_f[:, TILES - 1:TILES]))
                dve.wait_ge(pe_t.sem, 1)
                link(dve, dve_link, dve.tensor_copy(crow[:, 0:256], ps[0][0:1, 0:256]))
                link(dve, dve_link, dve.memset(crow[:, 256:257], 0.0))
                link(dve, x_b, dve.tensor_tensor_scan(crow[:, 257:385], crow[:, 128:256], crow[:, 0:128], 0.0,
                                                      ALU.mult, ALU.add))
                dve.wait_ge(pe_t.sem, 2)
                link(dve, dve_link, dve.tensor_copy(sml[:, 0, 2:3], ps[1][:, 0:1]))
                link(dve, x_b, dve.scalar_tensor_tensor(out=c_f, in0=q_f, scalar=sml[:, 0, 2:3], in1=c_f,
                                                        op0=ALU.mult, op1=ALU.add))
                link(dve, dve_link, dve.tensor_tensor(e_f, cur, nxt, ALU.not_equal))
                link(dve, dve_link, dve.tensor_scalar(z_f, cur, float(N), None, ALU.is_lt))
                link(dve, x_a, dve.tensor_tensor(e_f, e_f, z_f, ALU.mult))
                dve.wait_ge(act_link.sem, 1)
                link(dve, x_a, dve.reciprocal(s_f, c_f))
                link(dve, dve_link, dve.tensor_copy(part[0], c_f))
                link(dve, dve_link, dve.tensor_tensor(c_f, c_f, part[0], ALU.subtract))
                link(dve, dve_link, dve.tensor_copy(part[1], c_f))
                link(dve, dve_link, dve.tensor_tensor(c_f, c_f, part[1], ALU.subtract))
                link(dve, x_a, dve.tensor_copy(part[2], c_f))
                link(dve, dve_link, dve.tensor_tensor(b9[:, 6 * D:7 * D], b9[:, 6 * D:7 * D], bcast[0:9, 1, :], ALU.add))
                for j in range(3):
                    link(dve, dve_link, dve.tensor_copy(b9p, b9))
                    link(dve, dve_link, dve.tensor_tensor(b9, b9, b9p, ALU.subtract))
                    sel = w["third"][:, j:j + 1]
                    if j == 0:
                        link(dve, dve_link, dve.tensor_scalar(b9r, b9p, sel, None, ALU.mult))
                    else:
                        link(dve, dve_link, dve.scalar_tensor_tensor(out=b9r, in0=b9p, scalar=sel, in1=b9r,
                                                                     op0=ALU.mult, op1=ALU.add))
                link(dve, dve_link, dve.tensor_copy(bias9[:], b9r.rearrange("p (r d) -> p r d", d=D)))
                link(dve, dve_link, dve.tensor_copy(ones9[:], w["leads"][:]))
                link(dve, dve_link, dve.tensor_scalar(czero[:], bcast[:, 2:2 + L1, :], 0.0, None, ALU.max))
                dve.wait_ge(loaded.sem, l_base + 16 * 11)
                link(dve, dve_link, dve.tensor_copy(blocks[:, 2, 0:3, :], blocks[:, 2, 0:3, :].bitcast(I32)))
                link(dve, x_b, dve.tensor_copy(blocks[0:8, 2, 3, :], blocks[0:8, 2, 3, :].bitcast(I32)))
                dve.wait_ge(pe_t.sem, 3)
                for q, t in enumerate((ndst, ends, src_i)):
                    link(dve, dve_link, dve.tensor_copy(t[:], ps[2 + q][:, 0:TILES]))

            @block.scalar
            def _(act):
                act.wait_ge(x_b.sem, 3)
                act.activation(c_f, c_f, ACT.Sqrt).then_inc(act_link.sem, 1)

            @block.tensor
            def _(pe):
                pe.wait_ge(x_b.sem, 1)
                for q in range(2):
                    mm = pe.matmul(ps[0][0:1, q * P:(q + 1) * P], sml[:, 0, q:q + 1], ident[:], start=True, stop=True)
                mm.then_inc(pe_t.sem, 1)
                pe.wait_ge(x_b.sem, 2)
                pe.matmul(ps[1][:, 0:1], crow[:, 256:384], one[0:1, 0:1], start=True, stop=True).then_inc(pe_t.sem, 1)
                pe.wait_ge(x_b.sem, 4)
                for q in range(3):
                    for b in range(4):
                        n = P if b < 3 else 8
                        mm = pe.transpose(ps[2 + q][:, b * P:b * P + n], blocks[0:n, q, b, :], ident[0:n, 0:n])
                mm.then_inc(pe_t.sem, 1)
        loaded.base += 16 * 11
        stored[0].base += 16 * 12
        act_link.base = 1
        pe_t.base = 3

        ea = lrg[:, 0:3 * TILES].rearrange("p (c t) -> p c t", c=3)
        sq = lrg[:, 3 * TILES:6 * TILES].rearrange("p (c t) -> p c t", c=3)
        yy = lrg[:, 6 * TILES:10 * TILES].rearrange("p (c t) -> p c t", c=4)
        nrm = lrg[:, 10 * TILES:11 * TILES]
        RB = NP // 16
        rad = lrg[:, 0:RB]
        wid = lrg[:, RB:2 * RB]
        inr = lrg[:, 2 * RB:3 * RB]
        y_base, l_base, q_base, s_base = x_b.base, loaded.base, act_link.base, stored[0].base
        with nc.Block() as block:
            @block.sync
            def _(sp):
                for c in range(3):
                    sp.dma_start(ea[:, c, :], linear(flat(e_v[c]))).then_inc(loaded.sem, 16)
                sp.wait_ge(x_b.sem, y_base + 2)
                sp.dma_start(r_y.rearrange("c (p t) -> p c t", p=P), yy).then_inc(stored[0].sem, 16)
                sp.wait_ge(stored[0].sem, s_base + 16)
                for c in range(8):
                    sp.dma_start(rad[16 * c:16 * c + 16, :], flat(e_w).rearrange("(s j) -> s j", s=16)).then_inc(loaded.sem, 16)
                sp.wait_ge(x_b.sem, y_base + 4)
                sp.dma_start(r_emb.rearrange("c (s j) -> (c s) j", s=16), wid).then_inc(stored[0].sem, 16)
                sp.wait_ge(stored[0].sem, s_base + 32)

            @block.vector
            def _(dve):
                dve.wait_ge(loaded.sem, l_base + 3 * 16)
                link(dve, dve_link, dve.tensor_tensor(sq, ea, ea, ALU.mult))
                link(dve, dve_link, dve.tensor_tensor(nrm, sq[:, 0, :], sq[:, 1, :], ALU.add))
                link(dve, x_b, dve.tensor_tensor(nrm, nrm, sq[:, 2, :], ALU.add))
                dve.wait_ge(act_link.sem, q_base + 1)
                link(dve, dve_link, dve.tensor_scalar(nrm, nrm, 1e-12, None, ALU.add))
                link(dve, dve_link, dve.reciprocal(nrm, nrm))
                link(dve, dve_link, dve.memset(yy[:, 0, :], 1.0))
                for c in range(3):
                    link(dve, dve_link, dve.tensor_tensor(sq[:, c, :], ea[:, c, :], nrm, ALU.mult))
                link(dve, x_b, dve.tensor_scalar(yy[:, 1:4, :], sq, 3.0 ** 0.5, None, ALU.mult))
                dve.wait_ge(loaded.sem, l_base + 11 * 16)
                link(dve, dve_link, dve.tensor_scalar(inr, rad, 1.0, 8.0 ** 0.5, ALU.is_le, ALU.mult))
                link(dve, dve_link, dve.tensor_scalar(wid, rad, 0.0, 1.0, ALU.max, ALU.min))
                link(dve, x_b, dve.tensor_scalar(wid, wid, w["centre"][:, 0:1], 7.0, ALU.subtract, ALU.mult))
                dve.wait_ge(act_link.sem, q_base + 3)
                link(dve, x_b, dve.tensor_tensor(wid, wid, inr, ALU.mult))

            @block.scalar
            def _(act):
                act.wait_ge(x_b.sem, y_base + 1)
                act.activation(nrm, nrm, ACT.Sqrt).then_inc(act_link.sem, 1)
                act.wait_ge(x_b.sem, y_base + 3)
                act.activation(wid, wid, ACT.Square).then_inc(act_link.sem, 1)
                act.wait_ge(act_link.sem, q_base + 2)
                act.activation(wid, wid, ACT.Exp, scale=-0.5).then_inc(act_link.sem, 1)
        act_link.base += 3
        stored[0].base += 32
        loaded.base += 11 * 16

        hot = lrg[:, 0:4096].bitcast(BF16).rearrange("p (s t q v) -> p s t q v", s=2, t=TPC, q=4)
        iota_i = lrg[:, 4096:4352].bitcast(I32)
        iota_b = lrg[:, 4352:4480].bitcast(BF16)
        key_i = lrg[:, 4480:4480 + 4 * TILES].bitcast(I32).rearrange("p (q t) -> p q t", q=4)
        key_f = lrg[:, 6048:6048 + 4 * TILES].rearrange("p (q t) -> p q t", q=4)
        work = lrg[:, 0:5 * 512].rearrange("p (q v) -> p q v", q=5)
        x_base, l_base, h_base, i_base, k_base = x_h.base, act_link.base, pe_s.base, pool_link.base, loaded.base
        neg = [lrg[:, 9216 + CW * s:9216 + CW * (s + 1)] for s in range(2)]
        with nc.Block() as block:
            @block.gpsimd
            def _(pool):
                pool.iota(iota_i, [[1, 256]], base=0, channel_multiplier=0).then_inc(pool_link.sem, 1)
                paced(pool, lambda c: pool_gather(pool, c, a["x"], src_i, D, pe_t))

            @block.sync
            def _(sp):
                def load(c):
                    k, slot, n = c.k, c.slot, c.round
                    if not early_chunk(k):
                        sp.wait_ge(x_b.sem, x_b.at(k - 1))
                        hold(sp, "sp")
                    sp.dma_start(brd[:, slot, :], flat(e_w)[bass.ds(k * CW, CW)].partition_broadcast(P))\
                      .then_inc(ld[slot].sem, 16)

                sp.dma_start(key_i[:, 0, :], linear(a["src_row"])).then_inc(loaded.sem, 16)
                sp.dma_start(key_i[:, 2, :], linear(a["dst_row"][1:NP + 1])).then_inc(loaded.sem, 16)
                paced(sp, load)

            @block.tensor
            def _(pe):
                for b in (6, 7):
                    pe.matmul(ps[b][:], zer[0:1, 0:P], zer[0:1, :], start=True, stop=False, skip_group_check=True)

                def turn_rows(c):
                    k, slot, n = c.k, c.slot, c.round
                    wait_got(pe, c)
                    if not early_chunk(k):
                        pe.wait_ge(act_x.sem, act_x.at(k - 1))
                    hold(pe, "pe")
                    for t in range(TPC):
                        mm = pe.transpose(ps[slot][:, t * P:(t + 1) * P], gat[:, c.lap, t, 0:D], ident[:])
                    mm.then_inc(pe_t.sem, 1)

                def out_rows(c):
                    k, slot, n = c.k, c.slot, c.round
                    pe.wait_ge(dve_s.sem, dve_s.at(k + 1))
                    if not early_chunk(k):
                        pe.wait_ge(act_r.sem, act_r.at(k - 1))
                    hold(pe, "pe")
                    for t in range(TPC):
                        pe.matmul(ps[4 + slot][:, t * P:(t + 1) * P], scn[:, slot, t * P:(t + 1) * P],
                                  w["lin_wT"][:], start=True, stop=False)
                        mm = pe.matmul(ps[4 + slot][:, t * P:(t + 1) * P], ones9[:], bias9[:, L1 + 2, :],
                                       start=False, stop=True)
                    mm.then_inc(pe_o.sem, 1)

                def late(c):
                    k, slot, n = c.k, c.slot, c.round
                    pe.wait_ge(act_x.sem, act_x.at(k + 1))
                    if not early_chunk(k):
                        pe.wait_ge(act_q.sem, act_q.at(k - 1))
                    hold(pe, "pe")
                    pe.matmul(ps[2 + slot][:], w["pool_wT"][:], xin[:, slot, :], start=True, stop=True)\
                      .then_inc(x_a.sem, 1)
                    if not first(k):
                        out_rows(c.before)
                    pe.wait_ge(x_i.sem, x_i.at(16 * k + 16))
                    hold(pe, "pe")
                    for t in range(TPC):
                        for q in range(2):
                            for h in range(2):
                                mm = pe.matmul(ps[6 + q][:, h * 256:(h + 1) * 256],
                                               hot[:, slot, t, 2 * q, h * P:(h + 1) * P],
                                               hot[:, slot, t, 2 * q + 1, :], start=False, stop=False,
                                               skip_group_check=True)
                    mm.then_inc(x_g.sem, 1)
                skewed(pe, turn_rows, late)
                out_rows(LAST)
                pe.wait_ge(x_h.sem, x_base + 1)
                pe.matmul(ps[3][:, 0:2], above[:], sml[:, 0, 0:2], start=True, stop=False, skip_group_check=True)
                pe.matmul(ps[3][:, 1:2], ones[:], sml[:, 0, 0:1], start=False, stop=True,
                          skip_group_check=True).then_inc(pe_s.sem, 1)
                pe.wait_ge(x_h.sem, x_base + 2)
                pe.wait_ge(act_r.sem, act_r.at(C))
                for q, r in ((0, 0), (1, 2)):
                    for b in range(4):
                        mm = pe.transpose(ps[4 + q][:, b * P:(b + 1) * P], work[:, r, b * P:(b + 1) * P], ident[:])
                mm.then_inc(pe_s.sem, 1)

            @block.scalar
            def _(act):
                def evacuate(c):
                    k, slot, n = c.k, c.slot, c.round
                    act.wait_ge(pe_t.sem, pe_t.at(k + 1))
                    if not early_chunk(k):
                        act.wait_ge(x_a.sem, x_a.at(k - 1))
                    hold(act, "act")
                    act.activation(xin[:, slot, :], ps[slot][:], ACT.Copy).then_inc(act_x.sem, 1)

                def pooled(c):
                    k, slot, n = c.k, c.slot, c.round
                    act.wait_ge(x_a.sem, x_a.at(k + 1))
                    if not early_chunk(k):
                        act.wait_ge(x_b.sem, x_b.at(k - 1))
                    hold(act, "act")
                    act.activation(sca[:, slot, :], ps[2 + slot][:], ACT.Relu, bias=w["pool_b"][:, 0:1])\
                       .then_inc(act_q.sem, 1)

                def finish(c):
                    k, slot, n = c.k, c.slot, c.round
                    act.wait_ge(pe_o.sem, pe_o.at(k + 1))
                    if not early_chunk(k):
                        act.wait_ge(stored[slot].sem, stored[slot].at(16 * n))
                    hold(act, "act")
                    act.activation(res[:, slot, :, 0:D], tiles(ps[4 + slot][:]), ACT.Copy).then_inc(act_r.sem, 1)
                    act.wait_ge(act_r.sem, act_r.at(k + 1))
                    hold(act, "act")
                    act.dma_start(rows_of(t_agg, k), res[:, slot, :, 0:D]).then_inc(stored[slot].sem, 16)

                def late(c):
                    k, slot, n = c.k, c.slot, c.round
                    if not early_chunk(k):
                        act.wait_ge(dve_s.sem, dve_s.at(k - 1))
                        hold(act, "act")
                    act.activation(neg[slot], mask[:, bass.ds(k * CW, CW)], ACT.Copy, bias=-HUGE, scale=HUGE)\
                       .then_inc(x_c.sem, 1)
                    pooled(c)
                    if not first(k):
                        finish(c.before)
                skewed(act, evacuate, late)
                finish(LAST)
                act.wait_ge(x_h.sem, x_base + 1)
                act.activation(work[:, 0, :], work[:, 0, :], ACT.Sqrt).then_inc(act_link.sem, 1)
                for s in range(2):
                    act.wait_ge(stored[s].sem, stored[s].at(8 * C))

            @block.vector
            def _(dve):
                dve.wait_ge(loaded.sem, k_base + 32)
                for q in (0, 2):
                    link(dve, dve_link, dve.tensor_scalar(key_i[:, q + 1, :], key_i[:, q, :], 255, None,
                                                          ALU.bitwise_and))
                    link(dve, dve_link, dve.tensor_scalar(key_i[:, q, :], key_i[:, q, :], 8, None,
                                                          ALU.arith_shift_right))
                link(dve, dve_link, dve.tensor_copy(key_f[:], key_i[:]))
                dve.wait_ge(pool_link.sem, i_base + 1)
                link(dve, dve_link, dve.tensor_copy(iota_b, iota_i))

                def scan(c):
                    k, slot, n = c.k, c.slot, c.round
                    if not early_chunk(k):
                        dve.wait_ge(x_g.sem, x_g.at(k - 1))
                        hold(dve, "dve")
                    for t in range(TPC):
                        for q in range(4):
                            dve.tensor_scalar(hot[:, slot, t, q, :], iota_b, key_f[:, q, bass.ds(k * TPC + t, 1)],
                                              None, ALU.is_equal).then_inc(x_i.sem, 1)
                    wait_loads(dve, slot, n, 1)
                    dve.wait_ge(act_q.sem, act_q.at(k + 1))
                    if not first(k):
                        dve.wait_ge(dve_s.sem, dve_s.at(k))
                    hold(dve, "dve")
                    dve.tensor_tensor(tmp[:, 0, :], sca[:, slot, :], brd[:, slot, :], ALU.mult).then_inc(x_b.sem, 1)
                    dve.wait_ge(x_b.sem, x_b.at(k + 1))
                    dve.wait_ge(x_c.sem, x_c.at(k + 1))
                    if not early_chunk(k):
                        dve.wait_ge(pe_o.sem, pe_o.at(k - 1))
                    hold(dve, "dve")
                    dve.tensor_tensor_scan(scn[:, slot, :], neg[slot], tmp[:, 0, :],
                                           0.0 if first(k) else scn[:, 1 - slot, CW - 1:CW],
                                           ALU.add, ALU.max).then_inc(dve_s.sem, 1)
                paced(dve, scan)
                dve.wait_ge(x_g.sem, x_g.at(C))
                cs, cd, ep, z, t5 = (work[:, i, :] for i in range(5))
                link(dve, dve_link, dve.tensor_scalar(cs, ps[6][:], 1.0, None, ALU.max))
                link(dve, dve_link, dve.tensor_copy(cd, ps[7][:]))
                link(dve, dve_link, dve.memset(t5, 1.0))
                for h in range(2):
                    link(dve, dve_link, dve.tensor_tensor_scan(
                        ep[:, h * 256:(h + 1) * 256], t5[:, 0:256], cd[:, h * 256:(h + 1) * 256], 0.0,
                        ALU.mult, ALU.add))
                link(dve, x_h, dve.tensor_copy(sml[:, 0, 0:2], ep[:, 255:512:256]))
                dve.wait_ge(pe_s.sem, h_base + 1)
                link(dve, dve_link, dve.tensor_copy(sml[:, 0, 2:4], ps[3][:, 0:2]))
                for h in range(2):
                    link(dve, dve_link, dve.tensor_scalar(ep[:, h * 256:(h + 1) * 256], ep[:, h * 256:(h + 1) * 256],
                                                          sml[:, 0, 2 + h:3 + h], -float(NP), ALU.add, ALU.add))
                link(dve, dve_link, dve.tensor_scalar(z, cd, 0.0, None, ALU.is_gt))
                link(dve, dve_link, dve.tensor_tensor(ep, ep, z, ALU.mult))
                link(dve, dve_link, dve.tensor_scalar(ep, ep, float(NP - 1), None, ALU.add))
                dve.wait_ge(act_link.sem, l_base + 1)
                link(dve, x_h, dve.reciprocal(cs, cs))
                dve.wait_ge(pe_s.sem, h_base + 2)
                for q, dest in ((0, nsrc), (1, endp_f)):
                    for h in range(2):
                        for o in range(2):
                            m = 128 if h == 0 else TILES // 2 - 128
                            link(dve, dve_link, dve.tensor_copy(
                                dest[:, h * 256 + o:h * 256 + o + 2 * m - 1:2],
                                ps[4 + q][:, (2 * h + o) * P:(2 * h + o) * P + m]))
                link(dve, dve_link, dve.tensor_copy(endp_i[:], endp_f[:]))
        gathered()
        loaded.base += 32
        pool_link.base += 1
        act_link.base += 1
        pe_s.base += 2
        chunkwise(x_g)
        chunkwise(x_i, per=16)
        chunkwise(pe_t, pe_o, x_a, x_b, x_c, act_x, act_q, act_r, dve_s)
        chunkwise(*ld, *stored, per=8)

        def node_pass(base_rows, agg, stores, extend=False, lanes_in=None):
            width = EXT if extend else D
            loads = LANES if lanes_in else 1
            wide = lrg[:, 0:RING * LANES * CW].rearrange("p (s l v) -> p s l v", s=RING, l=LANES)
            at = RING * LANES * CW
            sums = lrg[:, at:at + RING * CW].rearrange("p (s v) -> p s v", s=RING)
            stat = lrg[:, at + RING * CW:at + RING * (CW + 64)].rearrange("p (s v) -> p s v", s=RING)

            def wait_rows(eng, c):
                if lanes_in:
                    eng.wait_ge(rows_in[c.lap].sem, rows_in[c.lap].at(16 * loads * c.turn + 16 * loads))
                else:
                    wait_loads(eng, c.slot, c.round, loads)
            with nc.Block() as block:
                if not lanes_in:
                    @block.gpsimd
                    def _(pool):
                        paced(pool, lambda c: pool_gather(pool, c, agg, endp_i, D, x_a))

                @block.sync
                def _(sp):
                    def load(c):
                        k, slot, n = c.k, c.slot, c.round
                        ring = RING if lanes_in else 2
                        if not early_chunk(k, ring):
                            sp.wait_ge(x_a.sem, x_a.at(k - ring + 1))
                            hold(sp, "sp")
                        if lanes_in:
                            for l, table in enumerate(lanes_in):
                                sp.dma_start(tiles(wide[:, c.lap, l, :]), rows_of(table, k))\
                                  .then_inc(rows_in[c.lap].sem, 16)
                        else:
                            sp.dma_start(tiles(brd[:, slot, :]), rows_of(base_rows, k)).then_inc(ld[slot].sem, 16)

                    paced(sp, load)

                @block.vector
                def _(dve):
                    def stats(c):
                        k, slot, n = c.k, c.slot, c.round
                        wait_rows(dve, c)
                        if not lanes_in:
                            wait_got(dve, c)
                        if not early_chunk(k, RING):
                            dve.wait_ge(act_r.sem, act_r.at(k - RING + 1))
                        hold(dve, "dve")
                        if lanes_in:
                            dve.tensor_tensor(sums[:, c.lap, :], wide[:, c.lap, 0, :], wide[:, c.lap, 1, :], ALU.add)\
                               .then_inc(x_a.sem, 1)
                        else:
                            dve.tensor_tensor(tiles(sums[:, c.lap, :]), gat[:, c.lap, :, 0:D], tiles(brd[:, slot, :]),
                                              ALU.add).then_inc(x_a.sem, 1)
                        dve.wait_ge(x_a.sem, x_a.at(k + 1))
                        hold(dve, "dve")
                        for t in range(TPC):
                            dve.bn_stats(stat[:, c.lap, 6 * t:6 * t + 6], sums[:, c.lap, t * P:(t + 1) * P])\
                               .then_inc(x_e.sem, 1)
                        dve.wait_ge(x_e.sem, x_e.at(4 * k + 4))
                        hold(dve, "dve")
                        for t in range(TPC):
                            dve.bn_aggr(stat[:, c.lap, 24 + 2 * t:26 + 2 * t], stat[:, c.lap, 6 * t:6 * t + 6])\
                               .then_inc(x_b.sem, 1)

                    def scales(c):
                        k, slot, n = c.k, c.slot, c.round
                        dve.wait_ge(act_q.sem, act_q.at(k + 1))
                        hold(dve, "dve")
                        dve.reciprocal(stat[:, c.lap, 36:40], stat[:, c.lap, 32:36]).then_inc(x_f.sem, 1)
                        dve.wait_ge(x_f.sem, x_f.at(k + 1))
                        hold(dve, "dve")
                        dve.scalar_tensor_tensor(out=stat[:, c.lap, 40:44], in0=stat[:, c.lap, 24:32:2], scalar=-1.0,
                                                 in1=stat[:, c.lap, 36:40], op0=ALU.mult, op1=ALU.mult)\
                           .then_inc(x_c.sem, 1)
                    skewed(dve, stats, scales)

                @block.scalar
                def _(act):
                    def root(c):
                        k, slot, n = c.k, c.slot, c.round
                        act.wait_ge(x_b.sem, x_b.at(4 * k + 4))
                        hold(act, "act")
                        act.activation(stat[:, c.lap, 32:36], stat[:, c.lap, 25:32:2], ACT.Sqrt, bias=epsc[:, 0:1])\
                           .then_inc(act_q.sem, 1)

                    def normalise(c):
                        k, slot, n = c.k, c.slot, c.round
                        act.wait_ge(x_c.sem, x_c.at(k + 1))
                        if not early_chunk(k):
                            act.wait_ge(stored[slot].sem, stored[slot].at(16 * len(stores) * n))
                        hold(act, "act")
                        if extend:
                            act.activation(res[:, slot, :, D], nsrc[:, bass.ds(k * TPC, TPC)], ACT.Copy)
                            act.activation(res[:, slot, :, D + 1], endp_f[:, bass.ds(k * TPC, TPC)], ACT.Copy)
                        for t in range(TPC):
                            op = act.activation(res[:, slot, t, 0:D], sums[:, c.lap, t * P:(t + 1) * P], ACT.Identity,
                                                bias=stat[:, c.lap, 40 + t:41 + t], scale=stat[:, c.lap, 36 + t:37 + t])
                        op.then_inc(act_r.sem, 1)
                        act.wait_ge(act_r.sem, act_r.at(k + 1))
                        hold(act, "act")
                        for table in stores:
                            act.dma_start(rows_of(table, k, width), res[:, slot, :, 0:width])\
                               .then_inc(stored[slot].sem, 16)
                    skewed(act, root, normalise)
                    for s in range(2):
                        act.wait_ge(stored[s].sem, stored[s].at(8 * C * len(stores)))
            if not lanes_in:
                gathered()
            chunkwise(x_a, x_c, x_f, act_q, act_r)
            chunkwise(x_b, x_e, per=4)
            if not lanes_in:
                chunkwise(*ld, per=8)
            chunkwise(*stored, per=8 * len(stores))

        node_pass(a["x"], t_agg, [t_x1e], extend=True)

        def gcn_pass(l):
            table = t_x1e if l == 0 else t_h[l - 1]
            radial = l == 1
            acc = lrg[:, 0:2 * CW]
            saves = 2 if radial else 1
            freed = x_a if l == 0 else pe_t
            p_base = pe_o.base
            with nc.Block() as block:
                @block.gpsimd
                def _(pool):
                    if l == 0:
                        paced(pool, lambda c: pool_gather(pool, c, table, src_i, EXT, x_a, per=3))
                    else:
                        paced(pool, lambda c: pool_gather(pool, c, table, pos_i, D, pe_t))

                @block.sync
                def _(sp):
                    def load(c):
                        k, slot, n = c.k, c.slot, c.round
                        if radial:
                            if not early_chunk(k):
                                sp.wait_ge(x_d.sem, x_d.at(k - 1))
                                hold(sp, "sp")
                            sp.dma_start(embs[:, slot, :], r_emb[:, bass.ds(k * CW, CW)])\
                              .then_inc(basis_in[slot].sem, 16)
                        if l:
                            if not early_chunk(k):
                                sp.wait_ge(x_b.sem, x_b.at(k - 1))
                                hold(sp, "sp")
                            sp.dma_start(brd[:, slot, :], r_ns.rearrange("t p -> (t p)")[bass.ds(k * CW, CW)]
                                         .partition_broadcast(P)).then_inc(norms_in[slot].sem, 16)
                        if not early_chunk(k):
                            sp.wait_ge(pe_o.sem, pe_o.at(k - 1))
                            hold(sp, "sp")
                        sp.dma_start(sq9[:, slot, :], r_sq[:, bass.ds(k * CW, CW)]).then_inc(ld[slot].sem, 16)

                    paced(sp, load)

                @block.tensor
                def _(pe):
                    def turn_rows(c):
                        k, slot, n = c.k, c.slot, c.round
                        if radial:
                            pe.wait_ge(basis_in[slot].sem, basis_in[slot].at(16 * n + 16))
                            if not early_chunk(k):
                                pe.wait_ge(x_i.sem, x_i.at(k - 1))
                            hold(pe, "pe")
                            pe.matmul(ps[2 + slot][0:64, :], w["mlp_w0"][:], embs[:, slot, :], start=True, stop=True)\
                              .then_inc(x_d.sem, 1)
                        if l == 0:
                            pe.wait_ge(x_a.sem, x_a.at(3 * k + 3))
                        else:
                            wait_got(pe, c)
                        if not early_chunk(k):
                            pe.wait_ge(act_x.sem, act_x.at(k - 1))
                            if l == 0:
                                pe.wait_ge(x_d.sem, x_d.at(k - 1))
                        hold(pe, "pe")
                        if l == 0:
                            pe.matmul(ps[2 + slot][0:TPC, 0:P], sml[:, slot, 0:TPC], ident[:],
                                      start=True, stop=True)
                        for t in range(TPC):
                            rows_in = sca[:, slot, t * P:(t + 1) * P] if l == 0 else gat[:, c.lap, t, 0:D]
                            mm = pe.transpose(ps[slot][:, t * P:(t + 1) * P], rows_in, ident[:])
                        mm.then_inc(pe_t.sem, 1)

                    def late(c):
                        k, slot, n = c.k, c.slot, c.round
                        if radial:
                            pe.wait_ge(x_i.sem, x_i.at(k + 1))
                            if not early_chunk(k):
                                pe.wait_ge(x_j.sem, x_j.at(k - 1))
                            hold(pe, "pe")
                            pe.matmul(ps[6 + slot][0:64, :], w["mlp_w1"][:], sca[0:64, slot, :], start=True, stop=True)\
                              .then_inc(zeroed.sem, 1)
                        pe.wait_ge(dve_s.sem, dve_s.at(k + 1))
                        wait_loads(pe, slot, n, 1)
                        if not early_chunk(k):
                            pe.wait_ge(act_r.sem, act_r.at(k - 1))
                        hold(pe, "pe")
                        for t in range(TPC):
                            pe.matmul(ps[4 + slot][:, t * P:(t + 1) * P], scn[:, slot, t * P:(t + 1) * P],
                                      gcn_w[:, l, :], start=True, stop=False)
                            mm = pe.matmul(ps[4 + slot][:, t * P:(t + 1) * P], sq9[:, slot, t * P:(t + 1) * P],
                                           bias9[:, l, :], start=False, stop=True)
                        mm.then_inc(pe_o.sem, 1)
                    skewed(pe, turn_rows, late)
                    pe.wait_ge(pe_s.sem, pe_s.at(C))
                    if radial:
                        pe.wait_ge(x_j.sem, x_j.at(C))
                    for q in range(2):
                        for t in range(TPC):
                            mm = pe.matmul(ps[6][:, q:q + 1], acc[:, q * CW + t * P:q * CW + (t + 1) * P],
                                           ones[:, 0:1], start=(t == 0), stop=(t == TPC - 1))
                    mm.then_inc(x_f.sem, 1)

                @block.scalar
                def _(act):
                    def evacuate(c):
                        k, slot, n = c.k, c.slot, c.round
                        if radial:
                            act.wait_ge(x_d.sem, x_d.at(k + 1))
                            if not early_chunk(k):
                                act.wait_ge(zeroed.sem, zeroed.at(k - 1))
                            hold(act, "act")
                            act.activation(sca[0:64, slot, :], ps[2 + slot][0:64, :], ACT.Silu, bias=w["mlp_b0"][:, 0:1])\
                               .then_inc(x_i.sem, 1)
                        act.wait_ge(pe_t.sem, pe_t.at(k + 1))
                        if not early_chunk(k):
                            act.wait_ge((dve_s if l == 0 else x_b).sem, (dve_s if l == 0 else x_b).at(k - 1))
                            if l == 0:
                                act.wait_ge(norms_out[slot].sem, norms_out[slot].at(16 * n))
                        hold(act, "act")
                        if l == 0:
                            act.activation(nst[:, slot, :], ps[2 + slot][0:TPC, 0:P], ACT.Copy)\
                               .then_inc(x_d.sem, 1)
                            act.wait_ge(x_d.sem, x_d.at(k + 1))
                            hold(act, "act")
                            act.dma_start(r_ns[bass.ds(k * TPC, TPC), :], nst[:, slot, :])\
                               .then_inc(norms_out[slot].sem, 16)
                            act.activation(xin[:, slot, :], ps[slot][:], ACT.Copy).then_inc(act_x.sem, 1)
                        else:
                            act.activation(xin[:, slot, :], ps[slot][:], ACT.Relu, bias=aff[:, l - 1, 1:2],
                                           scale=aff[:, l - 1, 0:1]).then_inc(act_x.sem, 1)

                    def square(c):
                        k, slot, n = c.k, c.slot, c.round
                        act.wait_ge(x_g.sem, x_g.at(k + 1))
                        if not early_chunk(k):
                            act.wait_ge(pe_s.sem, pe_s.at(k - 1))
                        hold(act, "act")
                        act.activation(dev[:, slot, 1, :], dev[:, slot, 0, :], ACT.Square).then_inc(act_q.sem, 1)

                    def late(c):
                        k, slot, n = c.k, c.slot, c.round
                        if radial:
                            act.wait_ge(zeroed.sem, zeroed.at(k + 1))
                            if not early_chunk(k):
                                act.wait_ge(stored[slot].sem, stored[slot].at(16 * saves * n))
                            hold(act, "act")
                            act.activation(h2s[:, slot, :], ps[6 + slot][0:64, :], ACT.Silu, bias=w["mlp_b1"][:, 0:1])\
                               .then_inc(x_j.sem, 1)
                        if not first(k):
                            square(c.before)
                        act.wait_ge(pe_o.sem, pe_o.at(k + 1))
                        if not early_chunk(k):
                            act.wait_ge(stored[slot].sem, stored[slot].at(16 * saves * n))
                            act.wait_ge(dve_d.sem, dve_d.at(k - 1))
                        hold(act, "act")
                        for t in range(TPC):
                            op = act.activation(res[:, slot, t, 0:D], ps[4 + slot][:, t * P:(t + 1) * P], ACT.Relu,
                                                scale=ndst[:, bass.ds(k * TPC + t, 1)])
                        op.then_inc(act_r.sem, 1)
                        act.wait_ge(act_r.sem, act_r.at(k + 1))
                        hold(act, "act")
                        act.dma_start(rows_of(t_h[l], k), res[:, slot, :, 0:D]).then_inc(stored[slot].sem, 16)
                        if radial:
                            act.wait_ge(x_j.sem, x_j.at(k + 1))
                            hold(act, "act")
                            act.dma_start(r_h2[:, bass.ds(k * CW, CW)], h2s[:, slot, :]).then_inc(stored[slot].sem, 16)
                    if l < LANES:
                        act.dma_start(t_acc[l][NP:ROWS, :].rearrange("(p r) d -> p (r d)", p=P), zer[:, 0:2 * D])\
                           .then_inc(loaded.sem, 16)
                    skewed(act, evacuate, late)
                    square(LAST)
                    if l < LANES:
                        act.wait_ge(loaded.sem, loaded.at(16))
                    for s in range(2):
                        act.wait_ge(stored[s].sem, stored[s].at(8 * saves * C))
                        if l == 0:
                            act.wait_ge(norms_out[s].sem, norms_out[s].at(8 * C))
                    act.wait_ge(x_e.sem, x_e.at(1))
                    act.activation(sml[:, 1, 4:5], sml[:, 1, 3:4], ACT.Sqrt, bias=epsc[:, 0:1])\
                       .then_inc(act_link.sem, 1)

                @block.vector
                def _(dve):
                    def normed(c):
                        k, slot, n = c.k, c.slot, c.round
                        wait_got(dve, c)
                        if not early_chunk(k):
                            dve.wait_ge(pe_t.sem, pe_t.at(k - 1))
                        hold(dve, "dve")
                        dve.tensor_copy(sml[:, slot, 0:TPC], gat[:, c.lap, :, D]).then_inc(x_a.sem, 1)
                        dve.tensor_tensor(tiles(sca[:, slot, :]), gat[:, c.lap, :, 0:D],
                                          gat[:, c.lap, :, D:D + 1].to_broadcast([P, TPC, D]), ALU.mult)\
                           .then_inc(x_a.sem, 1)
                        dve.tensor_copy(pos_i[:, bass.ds(k * TPC, TPC)], gat[:, c.lap, :, D + 1])\
                           .then_inc(x_a.sem, 1)

                    def scan(c):
                        k, slot, n = c.k, c.slot, c.round
                        if l == 0 and c is not LAST:
                            normed(c.after)
                        dve.wait_ge(act_x.sem, act_x.at(k + 1))
                        if l:
                            dve.wait_ge(norms_in[slot].sem, norms_in[slot].at(16 * n + 16))
                        if not early_chunk(k):
                            dve.wait_ge(pe_o.sem, pe_o.at(k - 1))
                        if not first(k):
                            dve.wait_ge(dve_s.sem, dve_s.at(k))
                        hold(dve, "dve")
                        if l:
                            dve.tensor_tensor(tmp[:, slot, :], xin[:, slot, :], brd[:, slot, :], ALU.mult)\
                               .then_inc(x_b.sem, 1)
                            dve.wait_ge(x_b.sem, x_b.at(k + 1))
                            hold(dve, "dve")
                        dve.tensor_tensor_scan(scn[:, slot, :], mask[:, bass.ds(k * CW, CW)],
                                               (tmp if l else xin)[:, slot, :],
                                               0.0 if first(k) else scn[:, 1 - slot, CW - 1:CW],
                                               ALU.mult, ALU.add).then_inc(dve_s.sem, 1)

                    def deviate(c):
                        k, slot, n = c.k, c.slot, c.round
                        dve.wait_ge(act_r.sem, act_r.at(k + 1))
                        if not early_chunk(k):
                            dve.wait_ge(pe_s.sem, pe_s.at(k - 1))
                        hold(dve, "dve")
                        dve.tensor_tensor(tiles(dev[:, slot, 0, :]), res[:, slot, :, 0:D],
                                          czero[:, l:l + 1, :].to_broadcast([P, TPC, D]), ALU.subtract)\
                           .then_inc(dve_d.sem, 1)
                        dve.wait_ge(dve_d.sem, dve_d.at(k + 1))
                        hold(dve, "dve")
                        dve.tensor_tensor(tiles(dev[:, slot, 0, :]), tiles(dev[:, slot, 0, :]),
                                          ends[:, bass.ds(k * TPC, TPC)].unsqueeze(2).to_broadcast([P, TPC, D]),
                                          ALU.mult).then_inc(x_g.sem, 1)
                        if not first(k):
                            gather_sums(c.before)

                    def gather_sums(c):
                        k, slot = c.k, c.slot
                        dve.wait_ge(act_q.sem, act_q.at(k + 1))
                        if first(k):
                            dve.wait_ge(x_h.sem, x_h.at(1))
                        else:
                            dve.wait_ge(pe_s.sem, pe_s.at(k))
                        hold(dve, "dve")
                        dve.tensor_tensor(acc, acc, dev[:, slot, :, :].rearrange("p q v -> p (q v)"), ALU.add)\
                           .then_inc(pe_s.sem, 1)
                    dve.memset(acc, 0.0).then_inc(x_h.sem, 1)
                    if l == 0:
                        normed(Chunk(0, 0))
                    skewed(dve, scan, deviate)
                    gather_sums(LAST)
                    dve.wait_ge(x_f.sem, x_f.at(1))
                    m = sml[:, 1, :]
                    link(dve, dve_link, dve.tensor_scalar(m[:, 0:2], ps[6][:, 0:2], 1.0 / N, None, ALU.mult))
                    link(dve, dve_link, dve.tensor_tensor(m[:, 2:3], m[:, 0:1], m[:, 0:1], ALU.mult))
                    link(dve, x_e, dve.tensor_tensor(m[:, 3:4], m[:, 1:2], m[:, 2:3], ALU.subtract))
                    dve.wait_ge(act_link.sem, act_link.at(1))
                    link(dve, dve_link, dve.reciprocal(m[:, 5:6], m[:, 4:5]))
                    link(dve, dve_link, dve.tensor_tensor(aff[:, l, 0:1], m[:, 5:6], w["gamT"][:, l:l + 1], ALU.mult))
                    link(dve, dve_link, dve.tensor_scalar(m[:, 6:7], w["bsT"][:, l:l + 1], 0.0, m[:, 0:1],
                                                          ALU.max, ALU.add))
                    link(dve, dve_link, dve.tensor_tensor(m[:, 7:8], m[:, 6:7], aff[:, l, 0:1], ALU.mult))
                    link(dve, dve_link, dve.tensor_tensor(aff[:, l, 1:2], w["betT"][:, l:l + 1], m[:, 7:8],
                                                          ALU.subtract))
            act_link.base += 1
            gathered()
            loaded.base += 16 * (l < LANES)
            chunkwise(pe_t, pe_o, pe_s, act_x, act_q, act_r, dve_s, dve_d)
            chunkwise(x_g)
            x_h.base += 1
            x_f.base += 1
            if l == 0:
                chunkwise(x_a, per=3)
                chunkwise(x_d)
            else:
                chunkwise(x_b)
            if radial:
                chunkwise(x_d, x_i, x_j, zeroed)
                chunkwise(*basis_in, per=8)
            chunkwise(*(norms_in if l else norms_out), per=8)
            chunkwise(*ld, per=8)
            chunkwise(*stored, per=8 * saves)

        for l in range(L1):
            gcn_pass(l)

        hin = lrg[:, 0:4096].rearrange("p (s l t d) -> p s l t d", s=2, l=L1, t=TPC)
        hfm = lrg[:, 4096:8192].rearrange("p (s l v) -> p s l v", s=2, l=L1)
        with nc.Block() as block:
            @block.sync
            def _(sp):
                def load(c):
                    k, slot, n = c.k, c.slot, c.round
                    if not early_chunk(k):
                        sp.wait_ge(pe_t.sem, pe_t.at(L1 * (k - 1)))
                        hold(sp, "sp")
                    for l in range(L1):
                        sp.dma_start(hin[:, slot, l, :, :], rows_of(t_h[l], k)).then_inc(ld[slot].sem, 16)

                paced(sp, load)

            @block.tensor
            def _(pe):
                def turn_rows(c):
                    k, slot, n = c.k, c.slot, c.round
                    wait_loads(pe, slot, n, L1)
                    for l in range(L1):
                        if not first(k):
                            pe.wait_ge(act_x.sem, act_x.at(L1 * (k - 1) + l + 1))
                        hold(pe, "pe")
                        for t in range(TPC):
                            mm = pe.transpose(ps[l][:, t * P:(t + 1) * P], hin[:, slot, l, t, :], ident[:])
                        mm.then_inc(pe_t.sem, 1)

                def late(c):
                    k, slot, n = c.k, c.slot, c.round
                    pe.wait_ge(dve_s.sem, dve_s.at(k + 1))
                    if not early_chunk(k):
                        pe.wait_ge(act_r.sem, act_r.at(k - 1))
                    hold(pe, "pe")
                    for t in range(TPC):
                        pe.matmul(ps[4 + slot][:, t * P:(t + 1) * P], scn[:, slot, t * P:(t + 1) * P],
                                  w["lin1_w"][:], start=True, stop=False)
                        mm = pe.matmul(ps[4 + slot][:, t * P:(t + 1) * P], ones9[:], bias9[:, L1, :],
                                       start=False, stop=True)
                    mm.then_inc(pe_o.sem, 1)
                skewed(pe, turn_rows, late)

            @block.scalar
            def _(act):
                def normed(c):
                    k, slot, n = c.k, c.slot, c.round
                    for l in range(L1):
                        act.wait_ge(pe_t.sem, pe_t.at(L1 * k + l + 1))
                        if l == 0 and not early_chunk(k):
                            act.wait_ge(x_a.sem, x_a.at(2 * (k - 1)))
                        hold(act, "act")
                        act.activation(hfm[:, slot, l, :], ps[l][:], ACT.Relu, bias=aff[:, l, 1:2],
                                       scale=aff[:, l, 0:1]).then_inc(act_x.sem, 1)

                def finish(c):
                    k, slot, n = c.k, c.slot, c.round
                    act.wait_ge(pe_o.sem, pe_o.at(k + 1))
                    if not early_chunk(k):
                        act.wait_ge(stored[slot].sem, stored[slot].at(16 * n))
                    hold(act, "act")
                    act.activation(res[:, slot, :, 0:D], tiles(ps[4 + slot][:]), ACT.Relu).then_inc(act_r.sem, 1)
                    act.wait_ge(act_r.sem, act_r.at(k + 1))
                    hold(act, "act")
                    act.dma_start(rows_of(t_agg, k), res[:, slot, :, 0:D]).then_inc(stored[slot].sem, 16)
                skewed(act, normed, finish)
                for s in range(2):
                    act.wait_ge(stored[s].sem, stored[s].at(8 * C))

            @block.vector
            def _(dve):
                def step(c):
                    k, slot, n = c.k, c.slot, c.round
                    dve.wait_ge(act_x.sem, act_x.at(L1 * k + L1))
                    if not first(k):
                        dve.wait_ge(dve_s.sem, dve_s.at(k))
                    hold(dve, "dve")
                    dve.tensor_tensor(tmp[:, slot, :], hfm[:, slot, 0, :], hfm[:, slot, 1, :], ALU.max)\
                       .then_inc(x_a.sem, 1)
                    dve.tensor_tensor(sca[:, slot, :], hfm[:, slot, 2, :], hfm[:, slot, 3, :], ALU.max)\
                       .then_inc(x_a.sem, 1)
                    dve.wait_ge(x_a.sem, x_a.at(2 * k + 2))
                    if not early_chunk(k):
                        dve.wait_ge(pe_o.sem, pe_o.at(k - 1))
                    hold(dve, "dve")
                    dve.tensor_tensor(scn[:, slot, :], tmp[:, slot, :], sca[:, slot, :], ALU.max)\
                       .then_inc(dve_s.sem, 1)
                paced(dve, step)
        chunkwise(pe_o, act_r, dve_s)
        chunkwise(pe_t, act_x, per=L1)
        chunkwise(x_a, per=2)
        chunkwise(*ld, per=8 * L1)
        chunkwise(*stored, per=8)

        node_pass(t_x1e, t_agg, [t_x2])

        def big(i):
            return lrg[:, i * CW:(i + 1) * CW]
        wA, wB, vy, mA, mB = (big(i) for i in range(5))
        sA = [big(5), big(6)]
        sB = [big(7), big(8)]
        with nc.Block() as block:
            @block.gpsimd
            def _(pool):
                paced(pool, lambda c: pool_gather(pool, c, t_x2, src_i, D, pe_t))

            @block.sync
            def _(sp):
                def load(c):
                    k, slot, n = c.k, c.slot, c.round
                    if not early_chunk(k):
                        sp.wait_ge(x_c.sem, x_c.at(k - 1))
                        hold(sp, "sp")
                        sp.wait_ge(pe_s.sem, pe_s.at(2 * (k - 1)))
                        hold(sp, "sp")
                    sp.dma_start(h2s[:, slot, :], r_h2[:, bass.ds(k * CW, CW)]).then_inc(ld[slot].sem, 16)
                    for c in range(4):
                        sp.dma_start(brd[32 * c:32 * c + 32, slot, :],
                                     r_y[c, bass.ds(k * CW, CW)].partition_broadcast(32)).then_inc(ld[slot].sem, 16)

                paced(sp, load)

            @block.tensor
            def _(pe):
                def early(c):
                    k, slot, n = c.k, c.slot, c.round
                    wait_got(pe, c)
                    if not early_chunk(k):
                        pe.wait_ge(act_x.sem, act_x.at(k - 1))
                    hold(pe, "pe")
                    for t in range(TPC):
                        mm = pe.transpose(ps[slot][:, t * P:(t + 1) * P], gat[:, c.lap, t, 0:D], ident[:])
                    mm.then_inc(pe_t.sem, 1)

                def out_rows(c):
                    k, slot, n = c.k, c.slot, c.round
                    pe.wait_ge(dve_s.sem, dve_s.at(2 * k + 2))
                    if not first(k):
                        pe.wait_ge(act_r.sem, act_r.at(k))
                    hold(pe, "pe")
                    for t in range(TPC):
                        pe.matmul(ps[3][:, t * P:(t + 1) * P], sA[slot][:, t * P:(t + 1) * P], w["w_outA"][:],
                                  start=True, stop=False)
                        mm = pe.matmul(ps[3][:, t * P:(t + 1) * P], sB[slot][:, t * P:(t + 1) * P], w["w_outB"][:],
                                       start=False, stop=True)
                    mm.then_inc(pe_o.sem, 1)

                def late(c):
                    k, slot, n = c.k, c.slot, c.round
                    pe.wait_ge(act_x.sem, act_x.at(k + 1))
                    if not first(k):
                        pe.wait_ge(x_d.sem, x_d.at(k))
                    hold(pe, "pe")
                    pe.matmul(ps[7][:], w["w_vv"][:], xin[:, slot, :], start=True, stop=True,
                              skip_group_check=True).then_inc(x_a.sem, 1)
                    wait_loads(pe, slot, n, 5)
                    if not first(k):
                        pe.wait_ge(dve_d.sem, dve_d.at(2 * k))
                        pe.wait_ge(x_c.sem, x_c.at(k))
                    hold(pe, "pe")
                    pe.matmul(ps[4][:], w["mlp_w2A"][:], h2s[:, slot, :], start=True, stop=True).then_inc(pe_s.sem, 1)
                    pe.matmul(ps[6][:], w["w_ss"][:], xin[:, slot, :], start=True, stop=True).then_inc(x_a.sem, 1)
                    pe.matmul(ps[5][:], w["mlp_w2B"][:], h2s[:, slot, :], start=True, stop=True).then_inc(pe_s.sem, 1)
                    pe.wait_ge(x_b.sem, x_b.at(k + 1))
                    hold(pe, "pe")
                    pe.matmul(ps[7][:], w["w_dot"][:], vy, start=False, stop=True,
                              skip_group_check=True).then_inc(zeroed.sem, 1)
                    if not first(k):
                        out_rows(c.before)
                skewed(pe, early, late)
                out_rows(LAST)

            @block.scalar
            def _(act):
                def early(c):
                    k, slot, n = c.k, c.slot, c.round
                    act.wait_ge(pe_t.sem, pe_t.at(k + 1))
                    if not early_chunk(k):
                        act.wait_ge(x_a.sem, x_a.at(2 * (k - 1)))
                    hold(act, "act")
                    act.activation(xin[:, slot, :], ps[slot][:], ACT.Copy).then_inc(act_x.sem, 1)

                def finish(c):
                    k, slot, n = c.k, c.slot, c.round
                    act.wait_ge(pe_o.sem, pe_o.at(k + 1))
                    if not early_chunk(k):
                        act.wait_ge(stored[slot].sem, stored[slot].at(16 * n))
                    hold(act, "act")
                    act.activation(res[:, slot, :, 0:D], tiles(ps[3][:]), ACT.Copy,
                                   scale=1.0 / (32.0 ** 0.5 * 8.0 * 16.0)).then_inc(act_r.sem, 1)
                    act.wait_ge(act_r.sem, act_r.at(k + 1))
                    hold(act, "act")
                    act.dma_start(rows_of(t_agg, k), res[:, slot, :, 0:D]).then_inc(stored[slot].sem, 16)

                def late(c):
                    k, slot, n = c.k, c.slot, c.round
                    act.wait_ge(pe_s.sem, pe_s.at(2 * k + 1))
                    if not first(k):
                        act.wait_ge(x_c.sem, x_c.at(k))
                    hold(act, "act")
                    act.activation(wA, ps[4][:], ACT.Identity, bias=w["mlp_b2A"][:, 0:1]).then_inc(dve_d.sem, 1)
                    act.wait_ge(pe_s.sem, pe_s.at(2 * k + 2))
                    if not first(k):
                        act.wait_ge(x_d.sem, x_d.at(k))
                    hold(act, "act")
                    act.activation(wB, ps[5][:], ACT.Identity, bias=w["mlp_b2B"][:, 0:1]).then_inc(dve_d.sem, 1)
                    if not first(k):
                        finish(c.before)
                skewed(act, early, late)
                finish(LAST)
                for s in range(2):
                    act.wait_ge(stored[s].sem, stored[s].at(8 * C))

            @block.vector
            def _(dve):
                def step(c):
                    k, slot, n = c.k, c.slot, c.round
                    wait_loads(dve, slot, n, 5)
                    dve.wait_ge(x_a.sem, x_a.at(2 * k + 1))
                    if not first(k):
                        dve.wait_ge(zeroed.sem, zeroed.at(k))
                    hold(dve, "dve")
                    dve.tensor_tensor(vy, ps[7][:], brd[:, slot, :], ALU.mult).then_inc(x_b.sem, 1)
                    dve.wait_ge(x_a.sem, x_a.at(2 * k + 2))
                    dve.wait_ge(dve_d.sem, dve_d.at(2 * k + 1))
                    if not first(k):
                        dve.wait_ge(dve_s.sem, dve_s.at(2 * k))
                    hold(dve, "dve")
                    dve.tensor_tensor(mA, ps[6][:], wA, ALU.mult).then_inc(act_e.sem, 1)
                    dve.wait_ge(act_e.sem, act_e.at(k + 1))
                    hold(dve, "dve")
                    dve.tensor_tensor(mA, mA, brd[:, slot, :], ALU.mult).then_inc(x_c.sem, 1)
                    dve.wait_ge(x_c.sem, x_c.at(k + 1))
                    if not early_chunk(k):
                        dve.wait_ge(pe_o.sem, pe_o.at(k - 1))
                    hold(dve, "dve")
                    here = mask[:, bass.ds(k * CW, CW)]
                    dve.tensor_tensor_scan(sA[slot], here, mA, 0.0 if first(k) else sA[1 - slot][:, CW - 1:CW],
                                           ALU.mult, ALU.add).then_inc(dve_s.sem, 1)
                    dve.wait_ge(zeroed.sem, zeroed.at(k + 1))
                    dve.wait_ge(dve_d.sem, dve_d.at(2 * k + 2))
                    hold(dve, "dve")
                    dve.tensor_tensor(mB, ps[7][:], wB, ALU.mult).then_inc(x_d.sem, 1)
                    dve.wait_ge(x_d.sem, x_d.at(k + 1))
                    hold(dve, "dve")
                    dve.tensor_tensor_scan(sB[slot], here, mB, 0.0 if first(k) else sB[1 - slot][:, CW - 1:CW],
                                           ALU.mult, ALU.add).then_inc(dve_s.sem, 1)
                paced(dve, step)
        gathered()
        chunkwise(pe_t, pe_o, x_b, x_c, x_d, act_x, act_r, act_e, zeroed)
        chunkwise(x_a, pe_s, dve_d, dve_s, per=2)
        chunkwise(*ld, per=8 * 5)
        chunkwise(*stored, per=8)

        node_pass(t_x2, t_agg, [t_x3, t_acc[0], t_acc[1]])

        eqs = [lrg[:, at:at + CW] for at in (0, 1024, 6144, 6656)]
        eqb = lrg[:, 512:1024]
        f1 = [lrg[:, 2048 + CW * s:2048 + CW * (s + 1)] for s in range(2)]
        f2 = [lrg[:, 3072 + CW * s:3072 + CW * (s + 1)] for s in range(2)]
        msg = [lrg[:, 4096 + CW * s:4096 + CW * (s + 1)] for s in range(2)]
        srow = [lrg[:, 5120 + CW * s:5120 + CW * (s + 1)].bitcast(I32) for s in range(2)]
        summed_rows = dev[:].rearrange("p a b (t d) -> p (a b) t d", d=D)
        src_f = lrg[:, 8192:8192 + TILES]
        away = lrg[:, 8704:8704 + TILES]
        with nc.Block() as block:
            @block.gpsimd
            def _(pool):
                def scatter(c):
                    k, slot = c.k, c.slot
                    pool.wait_ge(act_r.sem, act_r.at(k + 1))
                    pool.wait_ge(x_d.sem, x_d.at(k + 1))
                    hold(pool, "pool")
                    for t in range(TPC):
                        scatter_tile(c, t)

                def scatter_tile(c, t):
                    lane, lap = t % LANES, t // LANES
                    if not (first(c.k) and lap == 0):
                        pool.wait_ge(lanes[lane].sem, lanes[lane].at(16 * (TPC // LANES * c.k + lap)))
                        hold(pool, "pool")
                    pool.indirect_dma_start(t_acc[lane],
                                            bass.IndirectOffsetOnAxis(ap=sidx[:, c.lap, t:t + 1], axis=0),
                                            summed_rows[:, c.lap, t, :], None, compute_op=ALU.add)\
                        .then_inc(lanes[lane].sem, 16)

                def ahead(c):
                    b = c.before.before.before
                    pool_ready(pool, c, dst_i, x_b)
                    pool.wait_ge(act_r.sem, act_r.at(b.k + 1))
                    pool.wait_ge(x_d.sem, x_d.at(b.k + 1))
                    hold(pool, "pool")
                    for t in range(TPC):
                        gather_tile(pool, c, t, t_x3[0:NP, :], D)
                        scatter_tile(b, t)
                for lap in range(3):
                    pool_gather(pool, Chunk(0, lap), t_x3, dst_i, D, x_b)
                for lap in range(3, RING):
                    ahead(Chunk(0, lap))
                with pool.Fori(1, TURNS) as i:
                    for lap in range(RING):
                        ahead(Chunk(i, lap))
                for c in TAIL:
                    ahead(c)
                scatter(LAST.before.before)
                scatter(LAST.before)
                scatter(LAST)
                for lane in range(LANES):
                    pool.wait_ge(lanes[lane].sem, lanes[lane].at(16 * TPC // LANES * C))

            @block.sync
            def _(sp):
                def load(c):
                    k, slot, n = c.k, c.slot, c.round
                    if not early_chunk(k):
                        sp.wait_ge(pe_t.sem, pe_t.at(k - 1))
                        hold(sp, "sp")
                        sp.wait_ge(x_a.sem, x_a.at(k - 1))
                        hold(sp, "sp")
                    sp.dma_start(att[:, slot, :], a["edge_attr"][:, bass.ds(k * CW, CW)]).then_inc(ld[slot].sem, 16)
                    sp.dma_start(srow[slot], a["src_row"][bass.ds(k * CW, CW)].partition_broadcast(P))\
                      .then_inc(ld[slot].sem, 16)
                paced(sp, load)

            @block.tensor
            def _(pe):
                def filt1(c):
                    k, slot, n = c.k, c.slot, c.round
                    wait_loads(pe, slot, n, 2)
                    if not early_chunk(k):
                        pe.wait_ge(x_e.sem, x_e.at(k - 1))
                    hold(pe, "pe")
                    pe.matmul(ps[slot][:], w["W1"][:], att[:, slot, :], start=True, stop=True).then_inc(pe_t.sem, 1)

                def dedupe(c):
                    k, slot, n = c.k, c.slot, c.round
                    pe.wait_ge(x_b.sem, x_b.at(k + 1))
                    pe.wait_ge(x_a.sem, x_a.at(k + 1))
                    if not early_chunk(k):
                        pe.wait_ge(act_r.sem, act_r.at(k - 1))
                    hold(pe, "pe")
                    for t in range(TPC):
                        mm = pe.matmul(ps[4 + slot][:, t * P:(t + 1) * P], eqs[c.lap][:, t * P:(t + 1) * P],
                                       msg[slot][:, t * P:(t + 1) * P], start=True, stop=True)
                    mm.then_inc(pe_o.sem, 1)

                def late(c):
                    k, slot, n = c.k, c.slot, c.round
                    pe.wait_ge(x_e.sem, x_e.at(k + 1))
                    if not early_chunk(k):
                        pe.wait_ge(x_i.sem, x_i.at(k - 1))
                    hold(pe, "pe")
                    for t in range(TPC):
                        pe.matmul(ps[2 + slot][:, t * P:(t + 1) * P], f1[slot][:, t * P:(t + 1) * P], w["W2"][:],
                                  start=True, stop=False)
                        mm = pe.matmul(ps[2 + slot][:, t * P:(t + 1) * P], ones9[:], bias9[:, L1 + 1, :],
                                       start=False, stop=True)
                    mm.then_inc(pe_s.sem, 1)
                    if not first(k):
                        dedupe(c.before)
                skewed(pe, filt1, late)
                dedupe(LAST)

            @block.scalar
            def _(act):
                def soft1(c):
                    k, slot, n = c.k, c.slot, c.round
                    act.wait_ge(x_g.sem, x_g.at(k + 1))
                    hold(act, "act")
                    act.activation(f1[slot], f1[slot], ACT.Exp).then_inc(act_q.sem, 1)
                    act.wait_ge(act_q.sem, act_q.at(k + 1))
                    hold(act, "act")
                    act.activation(f1[slot], f1[slot], ACT.Ln, bias=half[:, 0:1], scale=0.5).then_inc(act_x.sem, 1)

                def summed(c):
                    k, slot, n = c.k, c.slot, c.round
                    act.wait_ge(pe_o.sem, pe_o.at(k + 1))
                    if not early_chunk(k, RING):
                        for lane in range(LANES):
                            act.wait_ge(lanes[lane].sem, lanes[lane].at(16 * TPC // LANES * (k - RING + 2)))
                    hold(act, "act")
                    act.activation(summed_rows[:, c.lap, :, :], tiles(ps[4 + slot][:]), ACT.Copy).then_inc(act_r.sem, 1)

                def late(c):
                    k, slot, n = c.k, c.slot, c.round
                    if not first(k):
                        summed(c.before)
                    act.wait_ge(x_h.sem, x_h.at(k + 1))
                    hold(act, "act")
                    act.activation(f2[slot], f2[slot], ACT.Exp).then_inc(act_e.sem, 1)
                    act.wait_ge(act_e.sem, act_e.at(k + 1))
                    hold(act, "act")
                    act.activation(f2[slot], f2[slot], ACT.Ln, bias=half[:, 0:1], scale=0.5).then_inc(x_f.sem, 1)
                act.preload_act_table_set("natural_log_exp_and_others")
                skewed(act, soft1, late)
                summed(LAST)

            @block.vector
            def _(dve):
                link(dve, dve_link, dve.tensor_copy(src_f, esrc_i[:]))
                link(dve, dve_link, dve.tensor_scalar(away, src_f, -1.0, lane[:, 0:1], ALU.mult, ALU.add))

                link(dve, dve_link, dve.tensor_scalar(sml[:, 0, 63:64], w["b1"][:], -LOG2, None, ALU.add))

                def rows_to(c):
                    k, slot, n = c.k, c.slot, c.round
                    dve.wait_ge(x_c.sem, x_c.at(4 * k + 1))
                    hold(dve, "dve")
                    dve.tensor_reduce(sml[:, slot, 0:TPC], tiles(eqb), AX, ALU.max).then_inc(x_c.sem, 1)
                    dve.wait_ge(x_c.sem, x_c.at(4 * k + 2))
                    hold(dve, "dve")
                    dve.tensor_tensor(sml[:, slot, 8:8 + TPC], sml[:, slot, 0:TPC], away[:, bass.ds(k * TPC, TPC)],
                                      ALU.mult).then_inc(x_c.sem, 1)
                    dve.wait_ge(x_c.sem, x_c.at(4 * k + 3))
                    hold(dve, "dve")
                    dve.tensor_tensor(sml[:, slot, 16:16 + TPC], sml[:, slot, 8:8 + TPC],
                                      src_f[:, bass.ds(k * TPC, TPC)], ALU.add).then_inc(x_c.sem, 1)
                    dve.wait_ge(x_c.sem, x_c.at(4 * k + 4))
                    if not early_chunk(k, RING):
                        for lane in range(LANES):
                            dve.wait_ge(lanes[lane].sem, lanes[lane].at(16 * TPC // LANES * (k - RING + 1)))
                    hold(dve, "dve")
                    dve.tensor_copy(sidx[:, c.lap, :], sml[:, slot, 16:16 + TPC]).then_inc(x_d.sem, 1)

                def early(c):
                    k, slot, n = c.k, c.slot, c.round
                    dve.wait_ge(pe_t.sem, pe_t.at(k + 1))
                    if not early_chunk(k):
                        dve.wait_ge(pe_s.sem, pe_s.at(k - 1))
                    hold(dve, "dve")
                    dve.tensor_scalar(f1[slot], ps[slot][:], w["b1"][:, 0:1], 40.0, ALU.add, ALU.min)\
                       .then_inc(x_g.sem, 1)
                    wait_loads(dve, slot, n, 2)
                    if not early_chunk(k, RING):
                        dve.wait_ge(pe_o.sem, pe_o.at(k - RING + 1))
                    if not first(k):
                        dve.wait_ge(x_d.sem, x_d.at(k))
                    hold(dve, "dve")
                    dve.tensor_tensor(tiles(eqs[c.lap]), tiles(srow[slot]),
                                      esrc_i[:, bass.ds(k * TPC, TPC)].unsqueeze(2).to_broadcast([P, TPC, P]),
                                      ALU.is_equal).then_inc(x_a.sem, 1)
                    dve.wait_ge(x_a.sem, x_a.at(k + 1))
                    hold(dve, "dve")
                    dve.tensor_tensor(tiles(eqb), tiles(eqs[c.lap]), below[:].unsqueeze(1).to_broadcast([P, TPC, P]),
                                      ALU.mult).then_inc(x_c.sem, 1)
                    dve.wait_ge(act_x.sem, act_x.at(k + 1))
                    hold(dve, "dve")
                    dve.scalar_tensor_tensor(out=f1[slot], in0=ps[slot][:], scalar=sml[:, 0, 63:64], in1=f1[slot],
                                             op0=ALU.add, op1=ALU.max).then_inc(x_e.sem, 1)
                    if first(k):
                        rows_to(c)

                def late(c):
                    k, slot, n = c.k, c.slot, c.round
                    dve.wait_ge(pe_s.sem, pe_s.at(k + 1))
                    hold(dve, "dve")
                    dve.tensor_scalar(f2[slot], ps[2 + slot][:], 40.0, None, ALU.min).then_inc(x_h.sem, 1)
                    if c is not LAST:
                        rows_to(c.after)
                    message(c)

                def message(c):
                    k, slot, n = c.k, c.slot, c.round
                    dve.wait_ge(x_f.sem, x_f.at(k + 1))
                    if not early_chunk(k):
                        dve.wait_ge(pe_o.sem, pe_o.at(k - 1))
                    hold(dve, "dve")
                    dve.scalar_tensor_tensor(out=msg[slot], in0=ps[2 + slot][:], scalar=-LOG2, in1=f2[slot],
                                             op0=ALU.add, op1=ALU.max).then_inc(x_i.sem, 1)
                    dve.wait_ge(x_i.sem, x_i.at(k + 1))
                    wait_got(dve, c)
                    hold(dve, "dve")
                    dve.tensor_tensor(tiles(msg[slot]), tiles(msg[slot]), gat[:, c.lap, :, 0:D], ALU.mult)\
                       .then_inc(x_b.sem, 1)
                skewed(dve, early, late)
        gathered()
        chunkwise(pe_t, pe_s, pe_o, x_a, x_b, x_d, x_e, x_f, x_g, x_h, x_i, act_x, act_q, act_e, act_r)
        chunkwise(x_c, per=4)
        chunkwise(*ld, per=16)
        chunkwise(*lanes, per=16 * TPC // LANES)

        node_pass(None, None, [out], lanes_in=t_acc)


def kernel(**inputs):
    import numpy as np
    import concourse.bacc as bacc
    from concourse.bass_utils import run_bass_kernel_spmd

    f32 = np.float32
    g = {k: np.asarray(v) for k, v in inputs.items()}
    pad = NP - N

    def edges(v, fill):
        return np.concatenate([v, np.full((pad,) + v.shape[1:], fill, v.dtype)])

    def by_tile(v):
        return np.ascontiguousarray(v.reshape(TILES, P).T)

    src = edges(g["src"], NP)
    dst = edges(g["dst"], NP - 1)
    x = np.zeros((ROWS, D), f32)
    x[:N] = g["x"]
    up0, up1 = g["L2_gnn_W_up0"], g["L2_gnn_W_up1"]
    o0, o1 = g["L2_gnn_W_out0"], g["L2_gnn_W_out1"]
    w_ss, w_vv, w_dot = (np.zeros((D, D), f32) for _ in range(3))
    w_outA, w_outB = np.zeros((D, D), f32), np.zeros((D, D), f32)
    w_outA[0:32, 0:32], w_outB[0:32, 0:32] = o0[0:32], o0[32:64]
    for c in range(4):
        w_ss[0:32, 32 * c:32 * c + 32] = up0
    for c in range(3):
        b = 32 * (c + 1)
        w_vv[32 + c:D:3, b:b + 32] = up1
        w_outA[b:b + 32, 32 + c:D:3] = o1[0:32]
        w_outB[b:b + 32, 32 + c:D:3] = o1[32:64]
        w_dot[np.arange(b, b + 32), np.arange(32)] = 3.0 ** -0.5
    w2, b2 = g["L2_gnn_mlp_w2"], g["L2_gnn_mlp_b2"]
    colA = np.concatenate([np.arange(0, 32)] + 3 * [np.arange(32, 64)])
    colB = np.concatenate([np.arange(96, 128)] + 3 * [np.arange(64, 96)])
    arrays = {
        "x": x, "src": by_tile(src), "dst": by_tile(dst),
        "dst_row": np.concatenate([np.full(1, -1, dst.dtype), dst, np.full(1, -1, dst.dtype)]), "src_row": src,
        "weight": edges(g["edge_weight"], 0), 
        "edge_vec": np.ascontiguousarray(edges(g["edge_attr_3"], 0).reshape(P, TILES, 3).transpose(0, 2, 1)),
        "edge_fields": np.ascontiguousarray(edges(np.concatenate([g["edge_attr_3"], g["edge_weight"][:, None]], axis=1), 0)
                                            .reshape(TILES, P, 4).transpose(1, 2, 0)),
        "edge_attr": np.ascontiguousarray(edges(g["edge_attr_64"], 0).T),
        "pool_wT": np.ascontiguousarray(g["L0_gnn_pool_w"].T), "lin_wT": np.ascontiguousarray(g["L0_gnn_lin_w"].T),
        "pool_b": g["L0_gnn_pool_b"][:, None], "lin1_w": g["L1_gnn_lin1_w"],
        "bias_rows": np.concatenate([g["L0_gnn_lin_b"][None], g["L0_gnn_bias"][None], g["L1_gnn_bs"]]),
        "rows": np.concatenate([g["L1_gnn_bs"], g["L1_gnn_lin1_b"][None], g["L3_gnn_b2"][None],
                                g["L0_gnn_lin_b"][None]]),
        "third": np.tile(np.eye(3, dtype=f32), (3, 1)),
        "leads": np.repeat((np.arange(9) < 3).astype(f32)[:, None], P, axis=1),
        "gcn_w": g["L1_gnn_Ws"], "bsT": np.ascontiguousarray(g["L1_gnn_bs"].T),
        "gamT": np.ascontiguousarray(g["L1_gnn_gammas"].T), "betT": np.ascontiguousarray(g["L1_gnn_betas"].T),
        "w_ss": w_ss, "w_vv": w_vv, "w_dot": w_dot, "w_outA": w_outA, "w_outB": w_outB,
        "mlp_w0": g["L2_gnn_mlp_w0"], "mlp_w1": g["L2_gnn_mlp_w1"],
        "mlp_w2A": np.ascontiguousarray(w2[:, colA]), "mlp_w2B": np.ascontiguousarray(w2[:, colB]),
        "mlp_b0": g["L2_gnn_mlp_b0"][:, None], "mlp_b1": g["L2_gnn_mlp_b1"][:, None],
        "mlp_b2A": b2[colA][:, None], "mlp_b2B": b2[colB][:, None],
        "W1": g["L3_gnn_W1"], "W2": g["L3_gnn_W2"], "b1": g["L3_gnn_b1"][:, None],
        "centre": np.repeat(np.arange(8, dtype=f32) / f32(7), 16)[:, None],
    }
    nc = bacc.Bacc("TRN2", target_bir_lowering=False, num_devices=1)
    feed, a = {}, {}
    for name, v in arrays.items():
        feed["in_" + name] = np.ascontiguousarray(v)
        a[name] = nc.dram_tensor("in_" + name, v.shape, mybir.dt.from_np(v.dtype), kind="ExternalInput").ap()
    out = nc.dram_tensor("out_x", (NP, D), F32, kind="ExternalOutput").ap()
    build(nc, a, out)
    r = run_bass_kernel_spmd(nc, [feed], core_ids=[0])
    return r.results[0]["out_x"][:N]
```
